# Optimizing a Trainium2 kernel written in Bass

```python
import numpy as np
import jax
import jax.numpy as jnp

def _softmax(x, axis=-1):
    return jax.nn.softmax(x, axis=axis)

def _gelu(x):
    return jax.nn.gelu(x, approximate=True)

def _silu(x):
    return jax.nn.silu(x)

def _sigmoid(x):
    return jax.nn.sigmoid(x)

def _layernorm(x, axis=-1, eps=1e-05):
    m = jnp.mean(x, axis=axis, keepdims=True)
    v = jnp.var(x, axis=axis, keepdims=True)
    return (x - m) / jnp.sqrt(v + eps)

def _scatter_add(tgt, idx, src, axis=0):
    return tgt.at[idx].add(src)

def _segment_sum(src, seg, n):
    return jax.ops.segment_sum(src, seg, n)
kernel_name = 'mk_adaln_attn_ffn_d2_seqx_r8_3a0e22'

def setup_inputs(seed: int=0):
    np.random.seed(seed)
    _w = jnp.asarray

    def _rec_inputs():
        import jax
        import jax.numpy as jnp
        _rk = jax.random.key(seed)
        x = 7.22e-05 + 1 * jax.random.normal(jax.random.fold_in(_rk, 1), (32, 128, 128), jnp.float32)
        _lenS = 128 - jax.random.randint(jax.random.fold_in(_rk, 7), (32,), 0, max(1, 128 // 4) + 1, jnp.int32)
        _lenS2 = 128 - jax.random.randint(jax.random.fold_in(_rk, 8), (32,), 0, max(1, 128 // 4) + 1, jnp.int32)
        itok_B_4_6 = jax.random.randint(jax.random.fold_in(_rk, 11), (32,), 4, 7, jnp.int32)
        condB_tauraws = -5.74692 + 0.777674 * jax.random.normal(jax.random.fold_in(_rk, 12), (32,), jnp.float32)
        cond_256 = -0.000235209 + 0.019331 * jax.random.normal(jax.random.fold_in(_rk, 13), (32, 32), jnp.float32)
        condB_bn2 = jnp.zeros((32,), jnp.float32)
        cond_1024 = -4.10585e-05 + 0.0199478 * jax.random.normal(jax.random.fold_in(_rk, 15), (32, 128), jnp.float32)
        condB_zX = jax.random.uniform(jax.random.fold_in(_rk, 16), (32,), jnp.float32, 0.0, 0.983423)
        condB_zY = jax.random.uniform(jax.random.fold_in(_rk, 17), (32,), jnp.float32, 0.0, 0.979075)
        condB_zR = jax.random.uniform(jax.random.fold_in(_rk, 18), (32,), jnp.float32, 0.0, 0.9968)
        itok_B_0_8 = jax.random.randint(jax.random.fold_in(_rk, 19), (32,), 0, 9, jnp.int32)
        return (x, itok_B_4_6, condB_tauraws, cond_256, condB_bn2, cond_1024, condB_zX, condB_zY, condB_zR, itok_B_0_8)
    x, itok_B_4_6, condB_tauraws, cond_256, condB_bn2, cond_1024, condB_zX, condB_zY, condB_zR, itok_B_0_8 = _rec_inputs()

    def _L0_cond_setup():
        import jax, jax.numpy as jnp
        import numpy as np
        B, S, H, E, R = (4, 256, 128, 8, 16)
        ALPHA = 32
        SCALING = ALPHA / R
        key = jax.random.key(seed)
        ks = jax.random.split(key, 8)
        x = jax.random.normal(ks[0], (B, S, H), dtype=jnp.float32)
        formalism_ids = jax.random.randint(ks[1], (B,), 0, E - 1)
        lora_A = jax.random.normal(ks[2], (E, R, H), dtype=jnp.float32) * (1.0 / np.sqrt(H))
        lora_B = jax.random.normal(ks[3], (E, H, R), dtype=jnp.float32) * 0.02
        Hq = H // 4
        gate_W1 = jax.random.normal(ks[4], (H, Hq), dtype=jnp.float32) * (1.0 / np.sqrt(H))
        gate_b1 = jnp.zeros((Hq,), dtype=jnp.float32)
        gate_W2 = jax.random.normal(ks[5], (Hq, E), dtype=jnp.float32) * (1.0 / np.sqrt(Hq))
        gate_b2 = jnp.zeros((E,), dtype=jnp.float32)
        return {'x': x, 'lora_A': lora_A, 'lora_B': lora_B, 'gate_W1': gate_W1, 'gate_b1': gate_b1, 'gate_W2': gate_W2, 'gate_b2': gate_b2, 'formalism_ids': formalism_ids}
    _L0_cond_all = _L0_cond_setup()
    _L0_cond_in = {k: v for k, v in _L0_cond_all.items() if k in ('lora_A', 'lora_B', 'gate_W1', 'gate_b1', 'gate_W2', 'gate_b2')}
    del _L0_cond_all

    def _L0_attn_setup():
        import jax, jax.numpy as jnp
        import numpy as np
        D_MODEL = 128
        D_STATE = 16
        D_CONV = 4
        EXPAND = 2
        D_INNER = D_MODEL * EXPAND
        B_SZ, L_SEQ = (4, 128)

        def _selective_scan(x, delta, Bp, Cp, A_log, D_param):
            A = -jnp.exp(A_log)
            deltaA = jnp.exp(delta[..., None] * A)
            deltaB_x = delta[..., None] * Bp[:, :, None, :] * x[..., None]

            def step(h, inp):
                dA, dBx, Ct = inp
                h = dA * h + dBx
                y = jnp.einsum('bn,bdn->bd', Ct, h)
                return (h, y)
            h0 = jnp.zeros((x.shape[0], x.shape[2], A.shape[1]), x.dtype)
            xs = (jnp.swapaxes(deltaA, 0, 1), jnp.swapaxes(deltaB_x, 0, 1), jnp.swapaxes(Cp, 0, 1))
            _, ys = jax.lax.scan(step, h0, xs)
            return jnp.swapaxes(ys, 0, 1) + x * D_param
        key = jax.random.key(seed)
        ks = jax.random.split(key, 8)
        s = lambda fan_in: 1.0 / np.sqrt(fan_in)
        x = jax.random.normal(ks[0], (B_SZ, L_SEQ, D_MODEL), dtype=jnp.float32)
        in_proj_w = jax.random.uniform(ks[1], (2 * D_INNER, D_MODEL), jnp.float32, -s(D_MODEL), s(D_MODEL))
        conv_w = jax.random.uniform(ks[2], (D_INNER, 1, D_CONV), jnp.float32, -s(D_CONV), s(D_CONV))
        conv_b = jax.random.uniform(ks[3], (D_INNER,), jnp.float32, -s(D_CONV), s(D_CONV))
        x_proj_w = jax.random.uniform(ks[4], (2 * D_STATE + D_INNER, D_INNER), jnp.float32, -s(D_INNER), s(D_INNER))
        dt_proj_w = jax.random.uniform(ks[5], (D_INNER, D_INNER), jnp.float32, -s(D_INNER), s(D_INNER))
        dt_proj_b = jax.random.uniform(ks[6], (D_INNER,), jnp.float32, -0.001, 0.001)
        A = jnp.tile(jnp.arange(1, D_STATE + 1, dtype=jnp.float32), (D_INNER, 1))
        A_log = jnp.log(A)
        D_param = jnp.ones((D_INNER,), jnp.float32)
        out_proj_w = jax.random.uniform(ks[7], (D_MODEL, D_INNER), jnp.float32, -s(D_INNER), s(D_INNER))
        return {'x': x, 'in_proj_w': in_proj_w, 'conv_w': conv_w, 'conv_b': conv_b, 'x_proj_w': x_proj_w, 'dt_proj_w': dt_proj_w, 'dt_proj_b': dt_proj_b, 'A_log': A_log, 'D_param': D_param, 'out_proj_w': out_proj_w}
    _L0_attn_all = _L0_attn_setup()
    _L0_attn_in = {k: v for k, v in _L0_attn_all.items() if k in ('in_proj_w', 'conv_w', 'conv_b', 'x_proj_w', 'dt_proj_w', 'dt_proj_b', 'A_log', 'D_param', 'out_proj_w')}
    del _L0_attn_all

    def _L0_cond2_setup():
        import jax, jax.numpy as jnp
        import numpy as np
        import math
        B, T, E, D = (4, 256, 128, 4)

        def _tau_init(t):
            a = 0.1 ** (1.0 / max(t - 1, 1))
            tt = -math.log(max(a, 1e-10))
            return math.log(math.exp(tt) - 1 + 1e-10)

        def causal_ema(b, tau_raw):
            alpha = jnp.exp(-jax.nn.softplus(tau_raw)).astype(b.dtype)

            def step(h, bt):
                h = alpha * h + bt
                return (h, h)
            h0 = jnp.zeros((b.shape[0], b.shape[2]), b.dtype)
            _, hs = jax.lax.scan(step, h0, jnp.swapaxes(b, 0, 1))
            return jnp.swapaxes(hs, 0, 1)
        key = jax.random.key(seed)
        ks = jax.random.split(key, 10)
        s = 0.02
        return {'x': jax.random.normal(ks[0], (B, T, E), jnp.float32), 'tau_ctx': jnp.float32(_tau_init(max(T // 2, 4))), 'tau_raws': jnp.array([_tau_init(max(T // 2 ** i, 2)) for i in range(D)], jnp.float32), 'Wg': jax.random.normal(ks[1], (E, 2 * E), jnp.float32) * s, 'bg': jnp.full((E,), -0.5, jnp.float32), 'Wn1': jax.random.normal(ks[2], (E // 4, E), jnp.float32) * s, 'bn1': jnp.zeros((E // 4,), jnp.float32), 'Wn2': jax.random.normal(ks[3], (D, E // 4), jnp.float32) * s, 'bn2': jnp.zeros((D,), jnp.float32), 'blend': jax.random.normal(ks[4], (D, E), jnp.float32) * s, 'Wsoma': jax.random.normal(ks[5], (E, E), jnp.float32) * s, 'bsoma': jnp.zeros((E,), jnp.float32), 'Wtemp': jax.random.normal(ks[6], (E, E), jnp.float32) * s, 'btemp': jnp.zeros((E,), jnp.float32), 'Wout': jax.random.normal(ks[7], (E, E), jnp.float32) * s, 'gamma': jnp.ones((E,), jnp.float32), 'beta': jnp.zeros((E,), jnp.float32)}
    _L0_cond2_all = _L0_cond2_setup()
    _L0_cond2_in = {k: v for k, v in _L0_cond2_all.items() if k in ('tau_ctx', 'Wg', 'bg', 'Wn1', 'bn1', 'Wsoma', 'bsoma', 'Wtemp', 'btemp', 'Wout', 'gamma', 'beta')}
    del _L0_cond2_all

    def _L0_ffn_setup():
        import jax, jax.numpy as jnp
        import numpy as np
        B, S, D, E = (2, 256, 128, 8)
        key = jax.random.key(seed)
        ks = jax.random.split(key, 5)
        x = jax.random.normal(ks[0], (B, S, D), dtype=jnp.float32)
        router_w = jax.random.normal(ks[1], (E, D), dtype=jnp.float32) * 0.02
        router_b = jnp.zeros((E,), dtype=jnp.float32)
        expert_w = jax.random.normal(ks[2], (E, D, D), dtype=jnp.float32) * 0.02
        expert_b = jnp.zeros((E, D), dtype=jnp.float32)
        return {'x': x, 'router_w': router_w, 'router_b': router_b, 'expert_w': expert_w, 'expert_b': expert_b}
    _L0_ffn_all = _L0_ffn_setup()
    _L0_ffn_in = {k: v for k, v in _L0_ffn_all.items() if k in ('router_w', 'router_b', 'expert_w', 'expert_b')}
    del _L0_ffn_all

    def _L1_cond_setup():
        import jax, jax.numpy as jnp
        import numpy as np
        key = jax.random.key(seed)
        k1, k2, k3, k4 = jax.random.split(key, 4)
        B, H, W = (64, 128, 128)
        return {'y': jax.random.uniform(k1, (B, H, W), dtype=jnp.float32), 'zX': jax.random.uniform(k2, (B, 1), dtype=jnp.float32), 'zY': jax.random.uniform(k3, (B, 1), dtype=jnp.float32), 'zR': jax.random.uniform(k4, (B, 1), dtype=jnp.float32), 'dx': 1, 'dy': 1}
    _L1_cond_all = _L1_cond_setup()
    _L1_cond_in = {k: v for k, v in _L1_cond_all.items() if k in ()}
    del _L1_cond_all

    def _L1_attn_setup():
        import jax, jax.numpy as jnp
        import numpy as np
        import math
        DIM = 128
        NUM_HEADS = 16
        HEAD_DIM = DIM // NUM_HEADS
        LOGIT_SCALE_MAX = math.log(1.0 / 0.01)
        EPS = 1e-12

        def _l2_normalize(t):
            n = jnp.sqrt(jnp.sum(t * t, axis=-1, keepdims=True))
            return t / jnp.maximum(n, EPS)
        key = jax.random.key(seed)
        ks = jax.random.split(key, 4)
        L, N, C = (128, 8, DIM)
        scale = HEAD_DIM ** (-0.5)
        x = jax.random.normal(ks[0], (L, N, C), dtype=jnp.float32)
        in_proj_weight = jax.random.normal(ks[1], (3 * C, C), dtype=jnp.float32) * scale
        in_proj_bias = jnp.zeros((3 * C,), dtype=jnp.float32)
        logit_scale = jnp.full((NUM_HEADS, 1, 1), math.log(10.0), dtype=jnp.float32)
        head_scale = jnp.ones((NUM_HEADS, 1, 1), dtype=jnp.float32)
        out_w = jax.random.normal(ks[2], (C, C), dtype=jnp.float32) * C ** (-0.5)
        out_b = jax.random.normal(ks[3], (C,), dtype=jnp.float32) * 0.01
        return {'x': x, 'in_proj_weight': in_proj_weight, 'in_proj_bias': in_proj_bias, 'logit_scale': logit_scale, 'head_scale': head_scale, 'out_w': out_w, 'out_b': out_b}
    _L1_attn_all = _L1_attn_setup()
    _L1_attn_in = {k: v for k, v in _L1_attn_all.items() if k in ('in_proj_weight', 'in_proj_bias', 'logit_scale', 'head_scale', 'out_w', 'out_b')}
    del _L1_attn_all

    def _L1_cond2_setup():
        import jax, jax.numpy as jnp
        import numpy as np
        LN_EPS = 1e-05
        key = jax.random.key(seed)
        ks = jax.random.split(key, 8)
        B, S, H, A, L = (32, 256, 128, 32, 10)
        return {'hidden_states': jax.random.normal(ks[0], (B, S, H), dtype=jnp.float32), 'language_ids': jax.random.randint(ks[1], (B,), 0, L, dtype=jnp.int64), 'W1': jax.random.normal(ks[2], (L, H, A), dtype=jnp.float32) * (1.0 / np.sqrt(H)), 'b1': jnp.zeros((L, A), dtype=jnp.float32), 'W2': jax.random.normal(ks[3], (L, A, H), dtype=jnp.float32) * (1.0 / np.sqrt(A)), 'b2': jnp.zeros((L, H), dtype=jnp.float32), 'gamma': jnp.ones((L, H), dtype=jnp.float32), 'beta': jnp.zeros((L, H), dtype=jnp.float32)}
    _L1_cond2_all = _L1_cond2_setup()
    _L1_cond2_in = {k: v for k, v in _L1_cond2_all.items() if k in ('W1', 'b1', 'W2', 'b2', 'gamma', 'beta')}
    del _L1_cond2_all

    def _L1_ffn_setup():
        import jax, jax.numpy as jnp
        import numpy as np
        D = 128
        H = 256
        E = 8
        TOP_K = 2
        N_SHARED = 1
        B, S = (2, 128)
        key = jax.random.key(seed)
        ks = jax.random.split(key, 12)
        sc = 0.02
        return {'hidden': jax.random.normal(ks[0], (B, S, D), jnp.float32), 'router_w': jax.random.normal(ks[1], (D, E), jnp.float32) * sc, 'router_b': jnp.zeros((E,), jnp.float32), 'sw1': jax.random.normal(ks[2], (D, H), jnp.float32) * sc, 'sb1': jnp.zeros((H,), jnp.float32), 'sw2': jax.random.normal(ks[3], (H, D), jnp.float32) * sc, 'sb2': jnp.zeros((D,), jnp.float32), 'rw1': jax.random.normal(ks[4], (E, D, H), jnp.float32) * sc, 'rb1': jnp.zeros((E, H), jnp.float32), 'rw2': jax.random.normal(ks[5], (E, H, D), jnp.float32) * sc, 'rb2': jnp.zeros((E, D), jnp.float32)}
    _L1_ffn_all = _L1_ffn_setup()
    _L1_ffn_in = {k: v for k, v in _L1_ffn_all.items() if k in ('router_w', 'router_b', 'sw1', 'sb1', 'sw2', 'sb2', 'rw1', 'rb1', 'rw2', 'rb2')}
    del _L1_ffn_all
    return {'x': x, 'itok_B_4_6': itok_B_4_6, 'condB_tauraws': condB_tauraws, 'cond_256': cond_256, 'condB_bn2': condB_bn2, 'cond_1024': cond_1024, 'condB_zX': condB_zX, 'condB_zY': condB_zY, 'condB_zR': condB_zR, 'itok_B_0_8': itok_B_0_8, 'L0_cond_lora_A': _L0_cond_in['lora_A'], 'L0_cond_lora_B': _L0_cond_in['lora_B'], 'L0_cond_gate_W1': _L0_cond_in['gate_W1'], 'L0_cond_gate_b1': _L0_cond_in['gate_b1'], 'L0_cond_gate_W2': _L0_cond_in['gate_W2'], 'L0_cond_gate_b2': _L0_cond_in['gate_b2'], 'L0_attn_in_proj_w': _L0_attn_in['in_proj_w'], 'L0_attn_conv_w': _L0_attn_in['conv_w'], 'L0_attn_conv_b': _L0_attn_in['conv_b'], 'L0_attn_x_proj_w': _L0_attn_in['x_proj_w'], 'L0_attn_dt_proj_w': _L0_attn_in['dt_proj_w'], 'L0_attn_dt_proj_b': _L0_attn_in['dt_proj_b'], 'L0_attn_A_log': _L0_attn_in['A_log'], 'L0_attn_D_param': _L0_attn_in['D_param'], 'L0_attn_out_proj_w': _L0_attn_in['out_proj_w'], 'L0_cond2_tau_ctx': _L0_cond2_in['tau_ctx'], 'L0_cond2_Wg': _L0_cond2_in['Wg'], 'L0_cond2_bg': _L0_cond2_in['bg'], 'L0_cond2_Wn1': _L0_cond2_in['Wn1'], 'L0_cond2_bn1': _L0_cond2_in['bn1'], 'L0_cond2_Wsoma': _L0_cond2_in['Wsoma'], 'L0_cond2_bsoma': _L0_cond2_in['bsoma'], 'L0_cond2_Wtemp': _L0_cond2_in['Wtemp'], 'L0_cond2_btemp': _L0_cond2_in['btemp'], 'L0_cond2_Wout': _L0_cond2_in['Wout'], 'L0_cond2_gamma': _L0_cond2_in['gamma'], 'L0_cond2_beta': _L0_cond2_in['beta'], 'L0_ffn_router_w': _L0_ffn_in['router_w'], 'L0_ffn_router_b': _L0_ffn_in['router_b'], 'L0_ffn_expert_w': _L0_ffn_in['expert_w'], 'L0_ffn_expert_b': _L0_ffn_in['expert_b'], 'L1_attn_in_proj_weight': _L1_attn_in['in_proj_weight'], 'L1_attn_in_proj_bias': _L1_attn_in['in_proj_bias'], 'L1_attn_logit_scale': _L1_attn_in['logit_scale'], 'L1_attn_head_scale': _L1_attn_in['head_scale'], 'L1_attn_out_w': _L1_attn_in['out_w'], 'L1_attn_out_b': _L1_attn_in['out_b'], 'L1_cond2_W1': _L1_cond2_in['W1'], 'L1_cond2_b1': _L1_cond2_in['b1'], 'L1_cond2_W2': _L1_cond2_in['W2'], 'L1_cond2_b2': _L1_cond2_in['b2'], 'L1_cond2_gamma': _L1_cond2_in['gamma'], 'L1_cond2_beta': _L1_cond2_in['beta'], 'L1_ffn_router_w': _L1_ffn_in['router_w'], 'L1_ffn_router_b': _L1_ffn_in['router_b'], 'L1_ffn_sw1': _L1_ffn_in['sw1'], 'L1_ffn_sb1': _L1_ffn_in['sb1'], 'L1_ffn_sw2': _L1_ffn_in['sw2'], 'L1_ffn_sb2': _L1_ffn_in['sb2'], 'L1_ffn_rw1': _L1_ffn_in['rw1'], 'L1_ffn_rb1': _L1_ffn_in['rb1'], 'L1_ffn_rw2': _L1_ffn_in['rw2'], 'L1_ffn_rb2': _L1_ffn_in['rb2']}

def reference(x, itok_B_4_6, condB_tauraws, cond_256, condB_bn2, cond_1024, condB_zX, condB_zY, condB_zR, itok_B_0_8, L0_cond_lora_A, L0_cond_lora_B, L0_cond_gate_W1, L0_cond_gate_b1, L0_cond_gate_W2, L0_cond_gate_b2, L0_attn_in_proj_w, L0_attn_conv_w, L0_attn_conv_b, L0_attn_x_proj_w, L0_attn_dt_proj_w, L0_attn_dt_proj_b, L0_attn_A_log, L0_attn_D_param, L0_attn_out_proj_w, L0_cond2_tau_ctx, L0_cond2_Wg, L0_cond2_bg, L0_cond2_Wn1, L0_cond2_bn1, L0_cond2_Wsoma, L0_cond2_bsoma, L0_cond2_Wtemp, L0_cond2_btemp, L0_cond2_Wout, L0_cond2_gamma, L0_cond2_beta, L0_ffn_router_w, L0_ffn_router_b, L0_ffn_expert_w, L0_ffn_expert_b, L1_attn_in_proj_weight, L1_attn_in_proj_bias, L1_attn_logit_scale, L1_attn_head_scale, L1_attn_out_w, L1_attn_out_b, L1_cond2_W1, L1_cond2_b1, L1_cond2_W2, L1_cond2_b2, L1_cond2_gamma, L1_cond2_beta, L1_ffn_router_w, L1_ffn_router_b, L1_ffn_sw1, L1_ffn_sb1, L1_ffn_sw2, L1_ffn_sb2, L1_ffn_rw1, L1_ffn_rb1, L1_ffn_rw2, L1_ffn_rb2):
    import jax
    import jax.numpy as jnp

    def _L0_cond_ref(x, lora_A, lora_B, gate_W1, gate_b1, gate_W2, gate_b2, formalism_ids):
        import jax, jax.numpy as jnp
        import numpy as np
        B, S, H, E, R = (4, 256, 128, 8, 16)
        ALPHA = 32
        SCALING = ALPHA / R
        h = jax.nn.relu(jnp.einsum('bsh,hq->bsq', x, gate_W1) + gate_b1)
        gate_logits = jnp.einsum('bsq,qe->bse', h, gate_W2) + gate_b2
        eidx = jnp.arange(E)
        allowed = (eidx == 0)[None, None, :] | (eidx[None, None, :] == formalism_ids[:, None, None] + 1)
        masked_logits = jnp.where(allowed, gate_logits, gate_logits - 1000000000.0)
        gate_weights = jax.nn.softmax(masked_logits, axis=-1)
        a = jnp.einsum('bsh,erh->bser', x, lora_A)
        expert_out = jnp.einsum('bser,ehr->bseh', a, lora_B) * SCALING
        mixed = jnp.einsum('bseh,bse->bsh', expert_out, gate_weights)
        return mixed

    def _L0_attn_ref(x, in_proj_w, conv_w, conv_b, x_proj_w, dt_proj_w, dt_proj_b, A_log, D_param, out_proj_w):
        import jax, jax.numpy as jnp
        import numpy as np
        D_MODEL = 128
        D_STATE = 16
        D_CONV = 4
        EXPAND = 2
        D_INNER = D_MODEL * EXPAND
        B_SZ, L_SEQ = (4, 128)

        def _selective_scan(x, delta, Bp, Cp, A_log, D_param):
            A = -jnp.exp(A_log)
            deltaA = jnp.exp(delta[..., None] * A)
            deltaB_x = delta[..., None] * Bp[:, :, None, :] * x[..., None]

            def step(h, inp):
                dA, dBx, Ct = inp
                h = dA * h + dBx
                y = jnp.einsum('bn,bdn->bd', Ct, h)
                return (h, y)
            h0 = jnp.zeros((x.shape[0], x.shape[2], A.shape[1]), x.dtype)
            xs = (jnp.swapaxes(deltaA, 0, 1), jnp.swapaxes(deltaB_x, 0, 1), jnp.swapaxes(Cp, 0, 1))
            _, ys = jax.lax.scan(step, h0, xs)
            return jnp.swapaxes(ys, 0, 1) + x * D_param
        B, L, _ = x.shape
        xz = x @ in_proj_w.T
        xi, z = jnp.split(xz, 2, axis=-1)
        xc = jnp.swapaxes(xi, 1, 2)
        xc = jax.lax.conv_general_dilated(xc, conv_w, window_strides=(1,), padding=[(D_CONV - 1, 0)], feature_group_count=D_INNER, dimension_numbers=('NCH', 'OIH', 'NCH'))
        xc = xc + conv_b[None, :, None]
        xi = jax.nn.silu(jnp.swapaxes(xc, 1, 2))
        deltaBC = xi @ x_proj_w.T
        delta, Bp, Cp = jnp.split(deltaBC, [D_INNER, D_INNER + D_STATE], axis=-1)
        delta = jax.nn.softplus(delta @ dt_proj_w.T + dt_proj_b)
        y = _selective_scan(xi, delta, Bp, Cp, A_log, D_param)
        return y * jax.nn.silu(z) @ out_proj_w.T

    def _L0_cond2_ref(x, tau_ctx, tau_raws, Wg, bg, Wn1, bn1, Wn2, bn2, blend, Wsoma, bsoma, Wtemp, btemp, Wout, gamma, beta):
        import jax, jax.numpy as jnp
        import numpy as np
        import math
        B, T, E, D = (4, 256, 128, 4)

        def _tau_init(t):
            a = 0.1 ** (1.0 / max(t - 1, 1))
            tt = -math.log(max(a, 1e-10))
            return math.log(math.exp(tt) - 1 + 1e-10)

        def causal_ema(b, tau_raw):
            alpha = jnp.exp(-jax.nn.softplus(tau_raw)).astype(b.dtype)

            def step(h, bt):
                h = alpha * h + bt
                return (h, h)
            h0 = jnp.zeros((b.shape[0], b.shape[2]), b.dtype)
            _, hs = jax.lax.scan(step, h0, jnp.swapaxes(b, 0, 1))
            return jnp.swapaxes(hs, 0, 1)
        ctx = causal_ema(x, tau_ctx)
        gate_in = jnp.concatenate([x, ctx], axis=-1)
        wg = jax.nn.sigmoid(jnp.einsum('btc,ec->bte', gate_in, Wg) + bg)
        gated = x * wg
        h1 = jax.nn.gelu(jnp.einsum('btc,hc->bth', x, Wn1) + bn1, approximate=False)
        mod = 0.5 + jax.nn.sigmoid(jnp.einsum('bth,dh->btd', h1, Wn2) + bn2)
        traces = jax.vmap(lambda tau, m: causal_ema(gated * m[..., None], tau))(tau_raws, jnp.moveaxis(mod, -1, 0))
        blend_w = jax.nn.softmax(blend, axis=0)
        temporal = jnp.einsum('dbtc,dc->btc', traces, blend_w)
        gate = jax.nn.sigmoid(jnp.einsum('btc,ec->bte', temporal, Wtemp) + btemp)
        soma = jax.nn.gelu(jnp.einsum('btc,ec->bte', x, Wsoma) + bsoma, approximate=False)
        out = jnp.einsum('btc,ec->bte', soma * gate, Wout)
        mu = out.mean(-1, keepdims=True)
        var = out.var(-1, keepdims=True)
        return (out - mu) / jnp.sqrt(var + 1e-05) * gamma + beta

    def _L0_ffn_ref(x, router_w, router_b, expert_w, expert_b):
        import jax, jax.numpy as jnp
        import numpy as np
        B, S, D, E = (2, 256, 128, 8)
        logits = jnp.einsum('bsd,ed->bse', x, router_w) + router_b
        probs = jax.nn.softmax(logits, axis=-1)
        weights = jnp.max(probs, axis=-1)
        top1 = jnp.argmax(probs, axis=-1)
        y_all = jnp.einsum('bsd,eod->bseo', x, expert_w) + expert_b
        y = jnp.take_along_axis(y_all, top1[:, :, None, None], axis=2)[:, :, 0, :]
        out = y * weights[:, :, None]
        return out

    def _L1_cond_ref(y, zX, zY, zR, dx, dy):
        import jax, jax.numpy as jnp
        import numpy as np
        yp_x = jnp.pad(y, ((0, 0), (0, 0), (1, 1)), mode='reflect')
        lap_x = (yp_x[:, :, :-2] - 2.0 * y + yp_x[:, :, 2:]) / (dx * dx)
        yp_y = jnp.pad(y, ((0, 0), (1, 1), (0, 0)), mode='reflect')
        lap_y = (yp_y[:, :-2, :] - 2.0 * y + yp_y[:, 2:, :]) / (dy * dy)
        du_dt = zX[:, :, None] * lap_x + zY[:, :, None] * lap_y + zR[:, :, None] * y * (1.0 - y)
        return du_dt

    def _L1_attn_ref(x, in_proj_weight, in_proj_bias, logit_scale, head_scale, out_w, out_b):
        import jax, jax.numpy as jnp
        import numpy as np
        import math
        DIM = 128
        NUM_HEADS = 16
        HEAD_DIM = DIM // NUM_HEADS
        LOGIT_SCALE_MAX = math.log(1.0 / 0.01)
        EPS = 1e-12

        def _l2_normalize(t):
            n = jnp.sqrt(jnp.sum(t * t, axis=-1, keepdims=True))
            return t / jnp.maximum(n, EPS)
        L, N, C = x.shape
        H, hd = (NUM_HEADS, HEAD_DIM)
        qkv = x @ in_proj_weight.T + in_proj_bias
        q, k, v = jnp.split(qkv, 3, axis=-1)

        def to_heads(t):
            return t.reshape(L, N, H, hd).transpose(1, 2, 0, 3)
        q, k, v = (to_heads(q), to_heads(k), to_heads(v))
        ls = jnp.exp(jnp.minimum(logit_scale, LOGIT_SCALE_MAX))
        attn = jnp.einsum('nhld,nhmd->nhlm', _l2_normalize(q), _l2_normalize(k)) * ls
        attn = jax.nn.softmax(attn, axis=-1)
        o = jnp.einsum('nhlm,nhmd->nhld', attn, v)
        o = o * head_scale
        o = o.transpose(2, 0, 1, 3).reshape(L, N, C)
        return o @ out_w.T + out_b

    def _L1_cond2_ref(hidden_states, language_ids, W1, b1, W2, b2, gamma, beta):
        import jax, jax.numpy as jnp
        import numpy as np
        LN_EPS = 1e-05
        w1 = W1[language_ids]
        w2 = W2[language_ids]
        h = jnp.einsum('bsh,bha->bsa', hidden_states, w1) + b1[language_ids][:, None, :]
        h = jax.nn.relu(h)
        adapted = jnp.einsum('bsa,bah->bsh', h, w2) + b2[language_ids][:, None, :]
        x = hidden_states + adapted
        mean = jnp.mean(x, axis=-1, keepdims=True)
        var = jnp.mean(jnp.square(x - mean), axis=-1, keepdims=True)
        normed = (x - mean) * jax.lax.rsqrt(var + LN_EPS)
        return normed * gamma[language_ids][:, None, :] + beta[language_ids][:, None, :]

    def _L1_ffn_ref(hidden, router_w, router_b, sw1, sb1, sw2, sb2, rw1, rb1, rw2, rb2):
        import jax, jax.numpy as jnp
        import numpy as np
        D = 128
        H = 256
        E = 8
        TOP_K = 2
        N_SHARED = 1
        B, S = (2, 128)
        b, s, d = hidden.shape
        T = b * s
        flat = hidden.reshape(T, d)
        router_logits = flat @ router_w + router_b
        router_probs = jax.nn.softmax(router_logits, axis=-1)
        topk_probs, topk_idx = jax.lax.top_k(router_probs, TOP_K)
        weights = jnp.zeros_like(router_probs).at[jnp.arange(T)[:, None], topk_idx].add(topk_probs)
        sh = jax.nn.gelu(flat @ sw1 + sb1, approximate=False)
        shared_out = (sh @ sw2 + sb2) / N_SHARED
        h1 = jax.nn.gelu(jnp.einsum('td,edh->teh', flat, rw1) + rb1[None], approximate=False)
        expert_out = jnp.einsum('teh,ehd->ted', h1, rw2) + rb2[None]
        mixed = jnp.einsum('ted,te->td', expert_out, weights)
        return (shared_out + mixed).reshape(b, s, d)
    x = x + _L0_attn_ref(_L0_cond_ref(x, L0_cond_lora_A, L0_cond_lora_B, L0_cond_gate_W1, L0_cond_gate_b1, L0_cond_gate_W2, L0_cond_gate_b2, itok_B_4_6), L0_attn_in_proj_w, L0_attn_conv_w, L0_attn_conv_b, L0_attn_x_proj_w, L0_attn_dt_proj_w, L0_attn_dt_proj_b, L0_attn_A_log, L0_attn_D_param, L0_attn_out_proj_w)
    x = x + _L0_ffn_ref(_L0_cond2_ref(x, L0_cond2_tau_ctx, condB_tauraws, L0_cond2_Wg, L0_cond2_bg, L0_cond2_Wn1, L0_cond2_bn1, cond_256, condB_bn2, cond_1024, L0_cond2_Wsoma, L0_cond2_bsoma, L0_cond2_Wtemp, L0_cond2_btemp, L0_cond2_Wout, L0_cond2_gamma, L0_cond2_beta), L0_ffn_router_w, L0_ffn_router_b, L0_ffn_expert_w, L0_ffn_expert_b)
    x = x + _L1_attn_ref(_L1_cond_ref(x, condB_zX[:, None], condB_zY[:, None], condB_zR[:, None], 1, 1), L1_attn_in_proj_weight, L1_attn_in_proj_bias, L1_attn_logit_scale, L1_attn_head_scale, L1_attn_out_w, L1_attn_out_b)
    x = x + _L1_ffn_ref(_L1_cond2_ref(x, itok_B_0_8, L1_cond2_W1, L1_cond2_b1, L1_cond2_W2, L1_cond2_b2, L1_cond2_gamma, L1_cond2_beta), L1_ffn_router_w, L1_ffn_router_b, L1_ffn_sw1, L1_ffn_sb1, L1_ffn_sw2, L1_ffn_sb2, L1_ffn_rw1, L1_ffn_rb1, L1_ffn_rw2, L1_ffn_rb2)
    return x

_drawn_inputs = setup_inputs


def setup_inputs(seed=0):
    import zlib

    import numpy as np

    out = dict(_drawn_inputs(seed))
    spreads = {'condB_bn2': (0.0, 0.1),
     'L0_cond_gate_b1': (0.0, 0.1),
     'L0_cond_gate_b2': (0.0, 0.1),
     'L0_attn_D_param': (1.0, 0.2),
     'L0_cond2_bg': (-0.5, 0.2),
     'L0_cond2_bn1': (0.0, 0.1),
     'L0_cond2_bsoma': (0.0, 0.1),
     'L0_cond2_btemp': (0.0, 0.1),
     'L0_cond2_gamma': (1.0, 0.2),
     'L0_cond2_beta': (0.0, 0.1),
     'L0_ffn_router_b': (0.0, 0.1),
     'L0_ffn_expert_b': (0.0, 0.1),
     'L1_attn_in_proj_bias': (0.0, 0.1),
     'L1_attn_logit_scale': (2.3025851249694824, 0.2),
     'L1_attn_head_scale': (1.0, 0.2),
     'L1_cond2_b1': (0.0, 0.1),
     'L1_cond2_b2': (0.0, 0.1),
     'L1_cond2_gamma': (1.0, 0.2),
     'L1_cond2_beta': (0.0, 0.1),
     'L1_ffn_router_b': (0.0, 0.1),
     'L1_ffn_sb1': (0.0, 0.1),
     'L1_ffn_sb2': (0.0, 0.1),
     'L1_ffn_rb1': (0.0, 0.1),
     'L1_ffn_rb2': (0.0, 0.1)}
    factors = {}
    for name, (base, spread) in spreads.items():
        noise = np.random.default_rng([zlib.crc32(name.encode()), seed]).standard_normal(out[name].shape)
        drawn = base * np.exp(spread * noise) if base else spread * noise
        out[name] = jnp.asarray(drawn.astype(out[name].dtype))
    for name, factor in factors.items():
        out[name] = (out[name] * factor).astype(out[name].dtype)
    return out
```

```python
from contextlib import ExitStack, contextmanager

import numpy as np

import concourse.bass as bass
from concourse import mybir

F32 = mybir.dt.float32
BF16 = mybir.dt.bfloat16
I32 = mybir.dt.int32
ALU = mybir.AluOpType
ACT = mybir.ActivationFunctionType
X = mybir.AxisListType.X

P = 128
NB = 32
S = 128
C = 128
GB = 4
NG = NB // GB
N = GB * S
NE = 8
R = 16
DI = 256
NT = DI // P
NS = 16
LORA_SCALE = 32 / R
ND = 32
LAGS = 8
CHUNKS = S // LAGS
LN_EPS = 1e-5
LOGIT_SCALE_MAX = float(np.log(1.0 / 0.01))
L2_EPS = 1e-12
HQ = 4
TB = 8
NL = 10


class Chain:

    def __init__(self, eng, sem, turn, per_turn):
        self.eng, self.sem, self.base, self.per_turn, self.at = eng, sem, turn * per_turn, per_turn, 0

    def link(self, ins):
        ins.then_inc(self.sem, 1)
        self.at += 1
        self.eng.wait_ge(self.sem, self.base + self.at)

    def end(self):
        assert self.at == self.per_turn, (self.at, self.per_turn)


@contextmanager
def phase_semaphores(nc):
    taken = []

    def sem(name):
        taken.append(nc.alloc_semaphore(name))
        return taken[-1]

    yield sem
    nc.clear_and_free_semaphores(taken)
    nc.all_engine_barrier()


def by_group(ap):
    return ap.rearrange("p (b t) -> p b t", b=GB)


def setup_scan(nc, ctx, D, W, xt):
    def sb(name, shape, dt=F32):
        return ctx.enter_context(nc.sbuf_tensor(name, shape, dt))

    with ExitStack() as own:
        def tmp(name, shape, dt=F32):
            return own.enter_context(nc.sbuf_tensor(name, shape, dt))

        def psum(name, shape):
            return own.enter_context(nc.psum_tensor(name, shape, F32))

        sem = own.enter_context(phase_semaphores(nc))

        lora_b = tmp("lora_b", [P, P])
        in_proj = tmp("in_proj", [P, 2 * DI])
        xp_rows = tmp("xp_rows", [P, NT, DI])
        dt_w = tmp("dt_w", [P, NT, DI])
        gate_w1 = tmp("gate_w1", [P, 32])
        gate_b1 = tmp("gate_b1", [32, 1])
        gate_w2 = tmp("gate_w2", [32, NE])
        gate_b2 = tmp("gate_b2", [P, NE])
        ids = tmp("ids", [P, NB], I32)
        idf = tmp("idf", [P, NB])
        expert = tmp("expert", [P, NE])
        allowed = tmp("allowed", [P, NB, NE])
        hid = tmp("hid", [32, NG, N])
        top = tmp("top", [P, NB])
        ps_h = psum("ps_h", [32, 2, N])
        ps_l = psum("ps_l", [P, NB, NE])
        ps_ab = psum("ps_ab", [P, 2 * DI])
        ps_d = psum("ps_d", [P, NT, DI])

        loaded = sem("setup_loaded")
        x_loaded = sem("x_loaded")
        hid_done = sem("hid_done")
        h_mm = sem("h_mm")
        logits_done = sem("logits_done")
        ab_mm = sem("ab_mm")
        delta_mm = sem("delta_mm")
        chain_v = sem("setup_chain_v")
        act_ready = sem("setup_act_ready")
        shifted = sem("logits_shifted")
        exped = sem("gates_exped")

        loads = [
            (lora_b[:, :], D["L0_cond_lora_B"]), (in_proj[:, :], D["L0_attn_in_proj_w"]),
            (xp_rows[:, :, :], D["x_proj_delta"]), (dt_w[:, :, :], D["L0_attn_dt_proj_w"]),
            (gate_w1[:, :], D["L0_cond_gate_W1"]), (gate_b1[:, :], D["L0_cond_gate_b1"]),
            (gate_w2[:, :], D["L0_cond_gate_W2"]),
            (gate_b2[:, :], D["L0_cond_gate_b2"].to_broadcast([P, NE])),
            (ids[:, :], D["itok_B_4_6"].to_broadcast([P, NB])),
            (expert[:, :], D["c_expert"].to_broadcast([P, NE])),
            (W["ident"][:, :], D["c_ident"]), (W["lora_a"][:, :], D["L0_cond_lora_A"]),
            (W["w_bc"][:, :, :], D["x_proj_bc"]), (W["conv_w"][:, :, :], D["L0_attn_conv_w"]),
            (W["conv_b"][:, :], D["L0_attn_conv_b"]), (W["dt_b"][:, :], D["L0_attn_dt_proj_b"]),
            (W["a"][:, :, :], D["L0_attn_A_log"]), (W["d_skip"][:, :], D["L0_attn_D_param"]),
            (W["out_w"][:, :, :], D["L0_attn_out_proj_w"]), (W["pick"][:, :], D["c_pick"]),
        ]
        block = own.enter_context(nc.Block())

        @block.sync
        def _(sp):
            sp.dma_start(xt[:, :], D["x"]).then_inc(x_loaded, 16)
            for dst, src in loads:
                sp.dma_start(dst, src).then_inc(loaded, 16)

        @block.tensor
        def _(pe):
            pe.wait_ge(loaded, 16 * len(loads))
            pe.wait_ge(x_loaded, 16)
            for g in range(NG):
                if g >= 2:
                    pe.wait_ge(hid_done, g - 1)
                nc.tensor.matmul(ps_h[:, g % 2, :], gate_w1[:, :], xt[:, g * N:(g + 1) * N],
                                 start=True, stop=True).then_inc(h_mm, 1)
            nc.tensor.matmul(ps_ab[:, :], lora_b[:, :], in_proj[:, :], start=True, stop=True).then_inc(ab_mm, 1)
            for kt in range(NT):
                for mt in range(NT):
                    last = nc.tensor.matmul(ps_d[:, kt, :], xp_rows[:, mt, kt * P:(kt + 1) * P], dt_w[:, mt, :],
                                            start=(mt == 0), stop=(mt == NT - 1))
            last.then_inc(delta_mm, 1)
            pe.wait_ge(hid_done, NG)
            for b in range(NB):
                last = nc.tensor.matmul(ps_l[:, b, :], hid[:, b // GB, (b % GB) * S:(b % GB + 1) * S],
                                        gate_w2[:, :], start=True, stop=True)
            last.then_inc(logits_done, 1)

        @block.scalar
        def _(act):
            act.wait_ge(loaded, 16 * len(loads))
            for g in range(NG):
                act.wait_ge(h_mm, g + 1)
                nc.scalar.activation(hid[:, g, :], ps_h[:, g % 2, :], ACT.Relu,
                                     bias=gate_b1[:, 0:1]).then_inc(hid_done, 1)
            act.wait_ge(ab_mm, 1)
            nc.scalar.mul(W["w_ab"][:, :], ps_ab[:, :], LORA_SCALE)
            act.wait_ge(delta_mm, 1)
            nc.scalar.copy(W["w_delta"][:, :, :], ps_d[:, :, :])
            nc.scalar.activation(W["a"][:, :, :], W["a"][:, :, :], ACT.Exp).then_inc(act_ready, 1)
            act.wait_ge(act_ready, 1)
            nc.scalar.mul(W["a"][:, :, :], W["a"][:, :, :], -1.0)
            act.wait_ge(shifted, 1)
            nc.scalar.activation(W["gates"][:, :, :], W["gates"][:, :, :], ACT.Exp).then_inc(exped, 1)

        @block.vector
        def _(dve):
            ch = Chain(dve, chain_v, 0, 12)
            dve.wait_ge(loaded, 16 * len(loads))
            ch.link(nc.vector.tensor_copy(idf[:, :], ids[:, :]))
            ch.link(nc.vector.tensor_scalar(idf[:, :], idf[:, :], 1.0, None, ALU.add))
            ch.link(nc.vector.tensor_tensor(allowed[:, :, :], idf[:, :].unsqueeze(2).to_broadcast([P, NB, NE]),
                                            expert[:, :].unsqueeze(1).to_broadcast([P, NB, NE]), ALU.is_equal))
            ch.link(nc.vector.memset(allowed[:, :, 0:1], 1.0))
            ch.link(nc.vector.tensor_scalar(allowed[:, :, :], allowed[:, :, :], 1e9, -1e9, ALU.mult, ALU.add))
            dve.wait_ge(logits_done, 1)
            gates = W["gates"][:, :, :]
            ch.link(nc.vector.tensor_tensor(gates, ps_l[:, :, :],
                                            gate_b2[:, :].unsqueeze(1).to_broadcast([P, NB, NE]), ALU.add))
            ch.link(nc.vector.tensor_tensor(gates, gates, allowed[:, :, :], ALU.add))
            ch.link(nc.vector.tensor_reduce(top[:, :], gates, X, ALU.max))
            nc.vector.tensor_tensor(gates, gates, top[:, :].unsqueeze(2).to_broadcast([P, NB, NE]),
                                    ALU.subtract).then_inc(shifted, 1)
            dve.wait_ge(exped, 1)
            ch.link(nc.vector.tensor_reduce(top[:, :], gates, X, ALU.add))
            ch.link(nc.vector.reciprocal(top[:, :], top[:, :]))
            ch.link(nc.vector.tensor_tensor(gates, gates, top[:, :].unsqueeze(2).to_broadcast([P, NB, NE]), ALU.mult))
            ch.link(nc.vector.memset(W["decay"][:, :, :, :, :], 0.0))
            ch.end()


def selective_scan(nc, D, W, xt):
    with ExitStack() as own:
        def sb(name, shape, dt=F32):
            return own.enter_context(nc.sbuf_tensor(name, shape, dt))

        def psum(name, shape):
            return own.enter_context(nc.psum_tensor(name, shape, F32))

        sem = own.enter_context(phase_semaphores(nc))

        ps_y = psum("ps_y", [P, NT, N])
        ps_b = psum("ps_b", [P, 2, N])
        ps_c = psum("ps_c", [P, 2, N])
        ps_w = psum("ps_w", [P, 2, N])
        gates_g = sb("gates_g", [P, GB, NE, R])
        gexp = sb("gexp", [P, N])
        mixed = sb("mixed", [P, N])
        conv = sb("conv", [P, NT, N])
        xi = sb("xi", [P, NT, N])
        zs = sb("zs", [P, NT, N])
        spa = sb("spa", [P, NT, N])
        spr = sb("spr", [P, NT, N])
        delta = sb("delta", [P, NT, N])
        u = sb("u", [P, NT, N])
        bc_parts = sb("bc_parts", [96, N], BF16)
        bc_mid = sb("bc_mid", [96, N], BF16)
        bc_rest = sb("bc_rest", [96, N])
        b_sb = sb("b_sb", [P, 2, 2, N])
        decay = W["decay"]
        dbx = sb("dbx", [P, 2, 2, N])
        h = sb("h", [P, 2, 2, N])
        ch_sb = sb("ch_sb", [P, 2, 2, N])
        yd = sb("yd", [P, NT, N])

        copied = sem("gates_copied")
        a_mm = sem("lora_a_mm")
        gexp_mm = sem("gexp_mm")
        gexp_done = sem("gexp_done")
        mixed_done = sem("mixed_done")
        xz_mm = sem("xz_mm")
        conv0 = sem("conv_first_tap")
        zs_done = sem("z_silu")
        conv_done = sem("conv_done")
        xi_done = sem("xi_done")
        bc_mm = sem("bc_mm")
        delta_mm = sem("delta_mm2")
        parts_done = sem("bc_parts_done")
        sp_act = sem("softplus_act")
        sp_max = sem("softplus_max")
        u_done = sem("u_done")
        bcast = sem("bc_broadcast")
        b_copied = sem("b_copied")
        decays = sem("decays")
        dbx_done = sem("dbx_done")
        scans = sem("scans")
        weighted = sem("weighted")
        reduced = sem("reduced")
        gated = sem("y_gated")
        out_mm = sem("out_mm")
        x_done = sem("x_done")
        chain_v = sem("scan_chain_v")
        chain_v2 = sem("scan_chain_v2")

        NP2 = NS // 2
        UNITS = NP2 * NT

        block = own.enter_context(nc.Block())

        @block.tensor
        def _(pe):
            pe.sem_inc(x_done, 1)
            with pe.Fori(0, NG) as g:
                xg = xt[:, bass.ds(g * N, N)]
                pe.wait_ge(x_done, g + 1)
                nc.tensor.matmul(ps_w[:, 0, :], W["lora_a"][:, :], xg, start=True, stop=True).then_inc(a_mm, 1)
                pe.wait_ge(copied, g + 1)
                for b in range(GB):
                    last = nc.tensor.matmul(ps_w[:, 1, b * S:(b + 1) * S],
                                            gates_g[:, b, :, :].rearrange("p e r -> p (e r)"),
                                            W["ident"][:, :], start=True, stop=True)
                last.then_inc(gexp_mm, 1)
                pe.wait_ge(mixed_done, g + 1)
                for j in range(4):
                    dst = ps_b[:, j, :] if j < 2 else ps_c[:, j - 2, :]
                    last = nc.tensor.matmul(dst, W["w_ab"][:, j * P:(j + 1) * P], mixed[:, :], start=True, stop=True)
                last.then_inc(xz_mm, 1)
                pe.wait_ge(xi_done, g + 1)
                for kt in range(NT):
                    last = nc.tensor.matmul(ps_w[0:96, 0, :], W["w_bc"][:, kt, :], xi[:, kt, :],
                                            start=(kt == 0), stop=(kt == NT - 1))
                last.then_inc(bc_mm, 1)
                for jt in range(NT):
                    for kt in range(NT):
                        last = nc.tensor.matmul(ps_b[:, jt, :], W["w_delta"][:, kt, jt * P:(jt + 1) * P],
                                                xi[:, kt, :], start=(kt == 0), stop=(kt == NT - 1))
                last.then_inc(delta_mm, 1)
                pe.wait_ge(parts_done, g + 1)
                pe.wait_ge(sp_act, 3 * g + 3)

                def reduce(unit):
                    tile = unit % NT
                    pe.wait_ge(weighted, g * UNITS + unit + 1)
                    for n in range(2):
                        last = nc.tensor.matmul(ps_y[:, tile, :], W["ident"][:, :], ch_sb[:, unit % 2, n, :],
                                                start=(unit < NT and n == 0),
                                                stop=(unit >= UNITS - NT and n == 1))
                    last.then_inc(reduced, 1)

                for pair in range(NP2):
                    if pair >= 1:
                        pe.wait_ge(b_copied, g * NP2 + pair)
                    for n in range(2):
                        last = nc.tensor.matmul(
                            ps_b[:, n, :], W["pick"][:, 2 * pair + n:2 * pair + n + 1].to_broadcast([96, P]),
                            bc_parts[:, :], start=True, stop=True)
                    last.then_inc(bcast, 1)
                    if pair >= 1:
                        pe.wait_ge(weighted, g * UNITS + NT * pair)
                    for n in range(2):
                        last = nc.tensor.matmul(
                            ps_c[:, n, :], W["pick"][:, NS + 2 * pair + n:NS + 2 * pair + n + 1].to_broadcast([96, P]),
                            bc_parts[:, :], start=True, stop=True)
                    last.then_inc(bcast, 1)
                    if pair >= 1:
                        for tile in range(NT):
                            reduce((pair - 1) * NT + tile)
                for tile in range(NT):
                    reduce((NP2 - 1) * NT + tile)
                pe.wait_ge(gated, g + 1)
                for kt in range(NT):
                    last = nc.tensor.matmul(ps_w[:, 0, :], W["out_w"][:, kt, :], yd[:, kt, :],
                                            start=(kt == 0), stop=(kt == NT - 1))
                last.then_inc(out_mm, 1)

        @block.scalar
        def _(act):
            with act.Fori(0, NG) as g:
                act.wait_ge(gexp_mm, g + 1)
                nc.scalar.copy(gexp[:, :], ps_w[:, 1, :]).then_inc(gexp_done, 1)
                act.wait_ge(xz_mm, g + 1)
                for tile in range(NT):
                    last = nc.scalar.activation(conv[:, tile, :], ps_b[:, tile, :], ACT.Identity,
                                                bias=W["conv_b"][:, tile:tile + 1], scale=W["conv_w"][:, tile, 3:4])
                last.then_inc(conv0, 1)
                nc.scalar.activation(zs[:, :, :], ps_c[:, :, :], ACT.Silu).then_inc(zs_done, 1)
                act.wait_ge(conv_done, g + 1)
                nc.scalar.activation(xi[:, :, :], conv[:, :, :], ACT.Silu).then_inc(xi_done, 1)
                act.wait_ge(delta_mm, g + 1)
                for tile in range(NT):
                    last = nc.scalar.activation(spa[:, tile, :], ps_b[:, tile, :], ACT.Abs,
                                                bias=W["dt_b"][:, tile:tile + 1])
                last.then_inc(sp_act, 1)
                for tile in range(NT):
                    last = nc.scalar.activation(spr[:, tile, :], ps_b[:, tile, :], ACT.Relu,
                                                bias=W["dt_b"][:, tile:tile + 1])
                last.then_inc(sp_max, 1)
                act.wait_ge(sp_act, 3 * g + 1)
                nc.scalar.activation(spa[:, :, :], spa[:, :, :], ACT.Exp, scale=-1.0).then_inc(sp_act, 1)
                act.wait_ge(sp_act, 3 * g + 2)
                nc.scalar.activation(spa[:, :, :], spa[:, :, :], ACT.Ln, bias=1.0).then_inc(sp_act, 1)
                act.wait_ge(u_done, g + 1)
                for pair in range(NP2):
                    act.wait_ge(bcast, g * 2 * NP2 + 2 * pair + 1)
                    if pair >= 2:
                        act.wait_ge(dbx_done, g * UNITS + NT * (pair - 1))
                    nc.scalar.copy(b_sb[:, pair % 2, :, :], ps_b[:, :, :]).then_inc(b_copied, 1)
                    for tile in range(NT):
                        unit = pair * NT + tile
                        if unit >= 2:
                            act.wait_ge(scans, g * UNITS + unit - 1)
                        for n in range(2):
                            last = nc.scalar.activation(
                                decay[:, unit % 2, n, :, 1:S], by_group(delta[:, tile, :])[:, :, 1:S], ACT.Exp,
                                scale=W["a"][:, tile, 2 * pair + n:2 * pair + n + 1])
                        last.then_inc(decays, 1)

        @block.gpsimd
        def _(pool):
            with pool.Fori(0, NG) as g:
                pool.wait_ge(x_done, g + 1)
                nc.gpsimd.tensor_copy(
                    gates_g[:, :, :, :],
                    W["gates"][:, bass.ds(g * GB, GB), :].unsqueeze(3).to_broadcast([P, GB, NE, R])).then_inc(copied, 1)
                pool.wait_ge(u_done, g + 1)
                for unit in range(UNITS):
                    pair, tile = divmod(unit, NT)
                    if tile == 0:
                        pool.wait_ge(b_copied, g * NP2 + pair + 1)
                    if unit >= 2:
                        pool.wait_ge(scans, g * UNITS + unit - 1)
                    nc.gpsimd.tensor_tensor(dbx[:, unit % 2, :, :], b_sb[:, pair % 2, :, :],
                                            u[:, tile, :].unsqueeze(1).to_broadcast([P, 2, N]),
                                            ALU.mult).then_inc(dbx_done, 1)

        @block.vector
        def _(dve):
            with dve.Fori(0, NG) as g:
                ch = Chain(dve, chain_v, g, 9)
                dve.wait_ge(a_mm, g + 1)
                dve.wait_ge(gexp_done, g + 1)
                nc.vector.tensor_tensor(mixed[:, :], ps_w[:, 0, :], gexp[:, :], ALU.mult).then_inc(mixed_done, 1)
                dve.wait_ge(conv0, g + 1)
                for k in (2, 1, 0):
                    lag = 3 - k
                    for tile in range(NT):
                        to = by_group(conv[:, tile, :])[:, :, lag:S]
                        ins = nc.vector.scalar_tensor_tensor(
                            out=to, in0=by_group(ps_b[:, tile, :])[:, :, 0:S - lag],
                            scalar=W["conv_w"][:, tile, k:k + 1], in1=to, op0=ALU.mult, op1=ALU.add)
                        if tile < NT - 1:
                            continue
                        if k:
                            ch.link(ins)
                        else:
                            ins.then_inc(conv_done, 1)
                dve.wait_ge(bc_mm, g + 1)
                split3(nc, ch, bc_parts, bc_mid, bc_rest, ps_w[0:96, 0, :]).then_inc(parts_done, 1)
                dve.wait_ge(sp_max, g + 1)
                dve.wait_ge(sp_act, 3 * g + 3)
                ch.link(nc.vector.tensor_tensor(delta[:, :, :], spr[:, :, :], spa[:, :, :], ALU.add))
                dve.wait_ge(xi_done, g + 1)
                nc.vector.tensor_tensor(u[:, :, :], delta[:, :, :], xi[:, :, :], ALU.mult).then_inc(u_done, 1)
                for unit in range(UNITS):
                    pair, tile = divmod(unit, NT)
                    at = unit % 2
                    dve.wait_ge(decays, g * UNITS + unit + 1)
                    dve.wait_ge(dbx_done, g * UNITS + unit + 1)
                    nc.vector.tensor_tensor_scan(
                        h[:, at, :, :].rearrange("p n t -> p (n t)"),
                        decay[:, at, :, :, :].rearrange("p n b t -> p (n b t)"),
                        dbx[:, at, :, :].rearrange("p n t -> p (n t)"), 0.0, ALU.mult, ALU.add).then_inc(scans, 1)
                    dve.wait_ge(scans, g * UNITS + unit + 1)
                    if tile == 0:
                        dve.wait_ge(bcast, g * 2 * NP2 + 2 * pair + 2)
                    if unit >= 2:
                        dve.wait_ge(reduced, g * UNITS + unit - 1)
                    nc.vector.tensor_tensor(ch_sb[:, at, :, :], h[:, at, :, :], ps_c[:, :, :],
                                            ALU.mult).then_inc(weighted, 1)
                dve.wait_ge(reduced, g * UNITS + UNITS)
                for tile in range(NT):
                    last = nc.vector.scalar_tensor_tensor(out=yd[:, tile, :], in0=xi[:, tile, :],
                                                          scalar=W["d_skip"][:, tile:tile + 1], in1=ps_y[:, tile, :],
                                                          op0=ALU.mult, op1=ALU.add)
                ch.link(last)
                dve.wait_ge(zs_done, g + 1)
                nc.vector.tensor_tensor(yd[:, :, :], yd[:, :, :], zs[:, :, :], ALU.mult).then_inc(gated, 1)
                dve.wait_ge(out_mm, g + 1)
                xg = xt[:, bass.ds(g * N, N)]
                ch.link(nc.vector.tensor_copy(spr[:, 0, :], ps_w[:, 0, :]))
                nc.vector.tensor_tensor(xg, xg, spr[:, 0, :], ALU.add).then_inc(x_done, 1)
                ch.end()


def setup_ffn0(nc, D, W):
    with ExitStack() as own:
        def tmp(name, shape, dt=F32):
            return own.enter_context(nc.sbuf_tensor(name, shape, dt))

        def sem(name):
            return own.enter_context(nc.semaphore(name))

        taus = tmp("taus", [P, ND + 2])
        tau_abs = tmp("tau_abs", [P, ND + 2])
        tau_max = tmp("tau_max", [P, ND + 2])
        soft = tmp("soft", [P, ND + 2])
        rate = tmp("rate", [P, ND + 2])
        blend_t = tmp("blend_t", [P, ND])
        blend4 = tmp("blend4", [P, 4, ND])
        top = tmp("blend_top", [P, 1])
        pow_at = tmp("pow_at", [P, LAGS])
        lag_pow = tmp("lag_pow", [P, LAGS])
        upto_at = tmp("upto_at", [P, CHUNKS])
        upto_on = tmp("upto_on", [P, CHUNKS])
        from_at = tmp("from_at", [P, 4, S])
        from_on = tmp("from_on", [P, 4, S])
        ctx_at = tmp("ctx_at", [P, S])
        ctx_on = tmp("ctx_on", [P, S])
        ps_bw = own.enter_context(nc.psum_tensor("ps_bw", [P, C], F32))

        loaded = sem("s2_loaded")
        a_abs = sem("s2_abs")
        a_exp = sem("s2_exp")
        a_ln = sem("s2_ln")
        rate_done = sem("s2_rate")
        shifted = sem("s2_blend_shifted")
        b_exp = sem("s2_blend_exp")
        b_done = sem("s2_blend_done")
        bw_mm = sem("s2_bw_mm")
        bw_copied = sem("s2_bw_copied")
        upto_arg = sem("s2_upto_arg")
        exps = sem("s2_exps")
        chain_v = sem("s2_chain_v")

        loads = [
            (taus[:, 0:ND], D["condB_tauraws"].to_broadcast([P, ND])),
            (taus[:, ND:ND + 1], D["tau_column"]),
            (taus[:, ND + 1:ND + 2], D["L0_cond2_tau_ctx"].to_broadcast([P, 1])),
            (blend_t[:, :], D["cond_1024"]), (pow_at[:, :], D["c_lag"].to_broadcast([P, LAGS])),
            (upto_at[:, :], D["c_upto_at"]), (upto_on[:, :], D["c_upto_on"]),
            (from_at[:, :, :], D["c_from_at"]), (from_on[:, :, :], D["c_from_on"]),
            (ctx_at[:, :], D["c_ctx_at"]), (ctx_on[:, :], D["c_ctx_on"]),
            (W["shift"][:, :, :], D["c_shift"]),
            (W["wg_x"][:, :], D["wg_x"]), (W["wg_ctx"][:, :], D["wg_ctx"]), (W["bg"][:, :], D["L0_cond2_bg"]),
            (W["wn1"][:, :], D["L0_cond2_Wn1"]), (W["bn1"][:, :], D["L0_cond2_bn1"]),
            (W["wn2"][:, :], D["cond_256"]), (W["bn2"][:, :], D["condB_bn2"]),
            (W["w_soma"][:, :], D["L0_cond2_Wsoma"]), (W["b_soma"][:, :], D["L0_cond2_bsoma"]),
            (W["w_temp"][:, :], D["L0_cond2_Wtemp"]), (W["b_temp"][:, :], D["L0_cond2_btemp"]),
            (W["w_out"][:, :], D["L0_cond2_Wout"]),
            (W["gamma"][:, :], D["L0_cond2_gamma"]), (W["beta"][:, :], D["L0_cond2_beta"]),
            (W["router"][:, :], D["L0_ffn_router_w"]),
            (W["router_b"][:, :], D["L0_ffn_router_b"].to_broadcast([P, NE])),
            (W["expert_w"][:, :, :], D["L0_ffn_expert_w"]), (W["expert_b"][:, :], D["L0_ffn_expert_b"]),
            (W["rank"][:, :], D["c_rank"].to_broadcast([P, NE])), (W["pick8"][:, :], D["c_pick"]),
        ]
        block = own.enter_context(nc.Block())

        @block.sync
        def _(sp):
            for dst, src in loads:
                sp.dma_start(dst, src).then_inc(loaded, 16)

        @block.scalar
        def _(act):
            act.wait_ge(loaded, 16 * len(loads))
            nc.scalar.activation(tau_abs[:, :], taus[:, :], ACT.Abs).then_inc(a_abs, 1)
            nc.scalar.activation(tau_max[:, :], taus[:, :], ACT.Relu).then_inc(a_abs, 1)
            act.wait_ge(a_abs, 1)
            nc.scalar.activation(soft[:, :], tau_abs[:, :], ACT.Exp, scale=-1.0).then_inc(a_exp, 1)
            act.wait_ge(a_exp, 1)
            nc.scalar.activation(soft[:, :], soft[:, :], ACT.Ln, bias=1.0).then_inc(a_ln, 1)
            act.wait_ge(shifted, 1)
            nc.scalar.activation(blend_t[:, :], blend_t[:, :], ACT.Exp).then_inc(b_exp, 1)
            act.wait_ge(rate_done, 1)
            nc.scalar.activation(lag_pow[:, :], pow_at[:, :], ACT.Exp, scale=rate[:, ND:ND + 1]).then_inc(exps, 1)
            nc.scalar.activation(W["from_start"][:, :, :], from_at[:, :, :], ACT.Exp,
                                 scale=rate[:, ND:ND + 1]).then_inc(exps, 1)
            nc.scalar.activation(W["k_ctx"][:, :], ctx_at[:, :], ACT.Exp,
                                 scale=rate[:, ND + 1:ND + 2]).then_inc(exps, 1)
            act.wait_ge(upto_arg, 1)
            nc.scalar.activation(W["upto_end"][:, :, :], W["upto_end"][:, :, :], ACT.Exp).then_inc(exps, 1)

        @block.tensor
        def _(pe):
            pe.wait_ge(b_done, 1)
            nc.tensor.matmul(ps_bw[:, :], blend4[:, :, :].rearrange("p k d -> p (k d)"), W["ident"][:, :],
                             start=True, stop=True).then_inc(bw_mm, 1)

        @block.gpsimd
        def _(pool):
            nc.gpsimd.memset(W["ones"][:, :], 1.0)
            nc.gpsimd.memset(W["mw96"][:, :, :, :], 0.0)
            nc.gpsimd.memset(W["neg_half"][:, :], -0.5)

        @block.vector
        def _(dve):
            ch = Chain(dve, chain_v, 0, 5)
            dve.wait_ge(loaded, 16 * len(loads))
            ch.link(nc.vector.tensor_reduce(top[:, :], blend_t[:, :], X, ALU.max))
            nc.vector.tensor_scalar(blend_t[:, :], blend_t[:, :], top[:, 0:1], None, ALU.subtract).then_inc(shifted, 1)
            dve.wait_ge(a_abs, 2)
            dve.wait_ge(a_ln, 1)
            nc.vector.scalar_tensor_tensor(out=rate[:, :], in0=tau_max[:, :], scalar=-1.0, in1=soft[:, :],
                                           op0=ALU.mult, op1=ALU.subtract).then_inc(rate_done, 1)
            dve.wait_ge(rate_done, 1)
            nc.vector.tensor_tensor(W["upto_end"][:, :, :], upto_at[:, :].unsqueeze(2).to_broadcast([P, CHUNKS, ND]),
                                    rate[:, 0:ND].unsqueeze(1).to_broadcast([P, CHUNKS, ND]),
                                    ALU.mult).then_inc(upto_arg, 1)
            dve.wait_ge(b_exp, 1)
            ch.link(nc.vector.tensor_reduce(top[:, :], blend_t[:, :], X, ALU.add))
            ch.link(nc.vector.reciprocal(top[:, :], top[:, :]))
            ch.link(nc.vector.tensor_scalar(blend_t[:, :], blend_t[:, :], top[:, 0:1], None, ALU.mult))
            nc.vector.tensor_copy(blend4[:, :, :], blend_t[:, :].unsqueeze(1).to_broadcast([P, 4, ND])).then_inc(b_done, 1)
            dve.wait_ge(bw_mm, 1)
            nc.vector.tensor_copy(W["bw"][:, :], ps_bw[:, :]).then_inc(bw_copied, 1)
            dve.wait_ge(exps, 4)
            dve.wait_ge(bw_copied, 1)
            ch.link(nc.vector.tensor_tensor(
                W["bw_lag"][:, :, :], W["bw"][0:ND, :].unsqueeze(1).to_broadcast([ND, LAGS, C]),
                lag_pow[0:ND, :].unsqueeze(2).to_broadcast([ND, LAGS, C]), ALU.mult))
            nc.vector.tensor_tensor(W["from_start"][:, :, :], W["from_start"][:, :, :], from_on[:, :, :], ALU.mult)
            nc.vector.tensor_tensor(W["k_ctx"][:, :], W["k_ctx"][:, :], ctx_on[:, :], ALU.mult)
            nc.vector.tensor_tensor(W["upto_end"][:, :, :], W["upto_end"][:, :, :],
                                    upto_on[:, :].unsqueeze(2).to_broadcast([P, CHUNKS, ND]), ALU.mult)
            ch.end()


def split3(nc, ch, parts, mid, rest, src):
    ch.link(nc.vector.tensor_copy(parts[:, :], src))
    ch.link(nc.vector.tensor_tensor(rest[:, :], src, parts[:, :], ALU.subtract))
    ch.link(nc.vector.tensor_copy(mid[:, :], rest[:, :]))
    ch.link(nc.vector.tensor_copy(parts[32:64, :], mid[32:64, :]))
    return nc.vector.tensor_tensor(parts[64:96, :], rest[64:96, :], mid[64:96, :], ALU.subtract)


def traces_and_experts(nc, W, xt):
    with ExitStack() as own:
        def sb(name, shape, dt=F32):
            return own.enter_context(nc.sbuf_tensor(name, shape, dt))

        def sem(name):
            return own.enter_context(nc.semaphore(name))

        ps = own.enter_context(nc.psum_tensor("ps2", [P, 8, N], F32))
        x1 = sb("x1", [P, N])
        xs = sb("xs", [P, GB, C])
        h1 = sb("h1", [32, N])
        soma = sb("soma", [P, N])
        ctx_t = sb("ctx_t", [P, N])
        mod_t = sb("mod_t", [ND, N])
        mod_s = sb("mod_s", [P, GB, ND])
        wg = sb("wg", [P, N])
        gated = sb("gated", [P, GB, C])
        upto = sb("upto", [P, 2, CHUNKS, ND])
        states = sb("states", [P, 2, 4, C])
        lagged = sb("lagged", [P, 2, LAGS, C])
        temp_t = sb("temp_t", [P, N])
        gate = sb("gate", [P, N])
        prod = sb("prod", [P, N])
        mean = sb("mean", [P, GB])
        var = sb("var", [P, GB])
        rstd = sb("rstd", [P, GB])
        xc = sb("xc", [P, GB, C])
        sq = sb("sq", [P, GB, C])
        xn = sb("xn", [P, GB, C])
        yt = sb("yt", [P, N])
        lg = sb("lg", [P, GB, NE])
        ex = sb("ex", [P, GB, NE])
        hot = sb("hot", [P, GB, NE])
        top = sb("top2", [P, GB])
        den = sb("den", [P, GB])
        first = sb("first", [P, GB])
        m_parts = sb("m_parts", [96, N], BF16)
        m_mid = sb("m_mid", [96, N], BF16)
        m_rest = sb("m_rest", [96, N])
        mw_t = sb("mw_t", [NE, N])
        ym = sb("ym", [P, 2, N])

        names = ("x1_copied xs_mm xs_copied h1_mm h1_done soma_mm soma_done ctx_mm ctx_copied mod_mm sig_done "
                 "mod_done wg_mm wg_done gated_done mods_mm mods_done upto_done states_mm lags_mm states_done "
                 "lagged_done temp_mm temp_copied gate_mm gate_done prod_done out_mm centred squared var_done "
                 "rstd_done xn_done xn_mm yt_done router_mm shifted_r exped_r mw_done mw_copied mw_mm m_split "
                 "mask_mm masked experts_mm x2_done chain_v2").split()
        Z = {n: sem("p2_" + n) for n in names}
        block = own.enter_context(nc.Block())

        @block.tensor
        def _(pe):
            with pe.Fori(0, NG) as g:
                pe.wait_ge(Z["x1_copied"], g + 1)
                for b in range(GB):
                    last = nc.tensor.transpose(ps[:, 0, b * S:(b + 1) * S], x1[:, b * S:(b + 1) * S], W["ident"][:, :])
                last.then_inc(Z["xs_mm"], 1)
                nc.tensor.matmul(ps[0:32, 1, :], W["wn1"][:, :], x1[:, :], start=True, stop=True).then_inc(Z["h1_mm"], 1)
                nc.tensor.matmul(ps[:, 2, :], W["w_soma"][:, :], x1[:, :], start=True, stop=True).then_inc(Z["soma_mm"], 1)
                pe.wait_ge(Z["xs_copied"], g + 1)
                pe.wait_ge(Z["h1_done"], g + 1)
                for b in range(GB):
                    last = nc.tensor.matmul(ps[:, 3, b * S:(b + 1) * S], xs[:, b, :], W["k_ctx"][:, :],
                                            start=True, stop=True)
                last.then_inc(Z["ctx_mm"], 1)
                nc.tensor.matmul(ps[0:ND, 1, :], W["wn2"][:, :], h1[:, :], start=True, stop=True).then_inc(Z["mod_mm"], 1)
                pe.wait_ge(Z["ctx_copied"], g + 1)
                for b in range(GB):
                    to, part = ps[:, 0, b * S:(b + 1) * S], slice(b * S, (b + 1) * S)
                    nc.tensor.matmul(to, x1[:, part], W["wg_x"][:, :], start=True, stop=False)
                    nc.tensor.matmul(to, ctx_t[:, part], W["wg_ctx"][:, :], start=False, stop=False)
                    last = nc.tensor.matmul(to, W["ones"][0:1, :], W["bg"][:, :], start=False, stop=True)
                last.then_inc(Z["wg_mm"], 1)
                pe.wait_ge(Z["mod_done"], g + 1)
                for b in range(GB):
                    last = nc.tensor.matmul(ps[:, 1, b * ND:(b + 1) * ND], mod_t[:, b * S:(b + 1) * S],
                                            W["ident"][0:ND, 0:ND], start=True, stop=True)
                last.then_inc(Z["mods_mm"], 1)
                pe.wait_ge(Z["gated_done"], g + 1)
                pe.wait_ge(Z["soma_done"], g + 1)

                def spread(b):
                    if b >= 1:
                        pe.wait_ge(Z["lagged_done"], g * GB + b)
                    for half in range(2):
                        last = nc.tensor.matmul(
                            ps[:, 2 + half, :], mod_t[:, b * S:(b + 1) * S],
                            W["bw_lag"][:, 4 * half:4 * half + 4, :].rearrange("d l c -> d (l c)"),
                            start=True, stop=True)
                    last.then_inc(Z["lags_mm"], 1)
                    pe.wait_ge(Z["upto_done"], g * GB + b + 1)
                    if b >= 2:
                        pe.wait_ge(Z["states_done"], g * GB + b - 1)
                    for j in range(4):
                        last = nc.tensor.matmul(
                            ps[:, 4 + b % 2, j * C:(j + 1) * C],
                            upto[:, b % 2, 4 * j:4 * j + 4, :].rearrange("s k d -> s (k d)"), gated[:, b, :],
                            start=True, stop=True)
                    last.then_inc(Z["states_mm"], 1)

                def gather(b):
                    to = ps[:, 6, b * S:(b + 1) * S]
                    pe.wait_ge(Z["states_done"], g * GB + b + 1)
                    for j in range(4):
                        nc.tensor.matmul(to, states[:, b % 2, j, :], W["from_start"][:, j, :],
                                         start=(j == 0), stop=False)
                    pe.wait_ge(Z["lagged_done"], g * GB + b + 1)
                    for lag in range(LAGS):
                        last = nc.tensor.matmul(to, lagged[:, b % 2, lag, :], W["shift"][:, lag, :],
                                                start=False, stop=(lag == LAGS - 1))
                    last.then_inc(Z["temp_mm"], 1)

                spread(0)
                for b in range(1, GB):
                    spread(b)
                    gather(b - 1)
                gather(GB - 1)
                pe.wait_ge(Z["temp_copied"], g + 1)
                nc.tensor.matmul(ps[:, 7, :], W["w_temp"][:, :], temp_t[:, :], start=True, stop=True).then_inc(Z["gate_mm"], 1)
                pe.wait_ge(Z["prod_done"], g + 1)
                for b in range(GB):
                    last = nc.tensor.matmul(ps[:, 0, b * C:(b + 1) * C], prod[:, b * S:(b + 1) * S], W["w_out"][:, :],
                                            start=True, stop=True)
                last.then_inc(Z["out_mm"], 1)
                pe.wait_ge(Z["xn_done"], g + 1)
                for b in range(GB):
                    last = nc.tensor.transpose(ps[:, 1, b * S:(b + 1) * S], xn[:, b, :], W["ident"][:, :])
                last.then_inc(Z["xn_mm"], 1)
                pe.wait_ge(Z["yt_done"], g + 1)
                for b in range(GB):
                    last = nc.tensor.matmul(ps[:, 2, b * NE:(b + 1) * NE], yt[:, b * S:(b + 1) * S], W["router"][:, :],
                                            start=True, stop=True)
                last.then_inc(Z["router_mm"], 1)
                pe.wait_ge(Z["mw_copied"], g + 1)
                for b in range(GB):
                    last = nc.tensor.matmul(ps[0:96, 3, b * S:(b + 1) * S],
                                            W["mw96"][:, b, :, :].rearrange("p k e -> p (k e)"), W["ident"][:, :],
                                            start=True, stop=True)
                last.then_inc(Z["mw_mm"], 1)
                pe.wait_ge(Z["m_split"], g + 1)

                def mask(e):
                    if e >= 2:
                        pe.wait_ge(Z["masked"], g * NE + e - 1)
                    nc.tensor.matmul(ps[:, 4 + e % 2, :], W["pick8"][:, e:e + 1].to_broadcast([96, P]), m_parts[:, :],
                                     start=True, stop=True).then_inc(Z["mask_mm"], 1)

                mask(0)
                nc.tensor.matmul(ps[:, 6, :], W["expert_b"][:, :], mw_t[:, :], start=True, stop=False)
                for e in range(NE):
                    if e + 1 < NE:
                        mask(e + 1)
                    pe.wait_ge(Z["masked"], g * NE + e + 1)
                    last = nc.tensor.matmul(ps[:, 6, :], W["expert_w"][:, e, :], ym[:, e % 2, :],
                                            start=False, stop=(e == NE - 1))
                last.then_inc(Z["experts_mm"], 1)

        @block.scalar
        def _(act):
            with act.Fori(0, NG) as g:
                act.wait_ge(Z["xs_mm"], g + 1)
                nc.scalar.copy(xs[:, :, :].rearrange("p b c -> p (b c)"), ps[:, 0, :]).then_inc(Z["xs_copied"], 1)
                act.wait_ge(Z["h1_mm"], g + 1)
                nc.scalar.activation(h1[:, :], ps[0:32, 1, :], ACT.Gelu, bias=W["bn1"][:, 0:1]).then_inc(Z["h1_done"], 1)
                act.wait_ge(Z["soma_mm"], g + 1)
                nc.scalar.activation(soma[:, :], ps[:, 2, :], ACT.Gelu, bias=W["b_soma"][:, 0:1]).then_inc(Z["soma_done"], 1)
                act.wait_ge(Z["mod_mm"], g + 1)
                nc.scalar.activation(mod_t[:, :], ps[0:ND, 1, :], ACT.Sigmoid, bias=W["bn2"][:, 0:1]).then_inc(Z["sig_done"], 1)
                act.wait_ge(Z["wg_mm"], g + 1)
                nc.scalar.activation(wg[:, :], ps[:, 0, :], ACT.Sigmoid).then_inc(Z["wg_done"], 1)
                act.wait_ge(Z["temp_mm"], GB * g + GB)
                nc.scalar.copy(temp_t[:, :], ps[:, 6, :]).then_inc(Z["temp_copied"], 1)
                act.wait_ge(Z["gate_mm"], g + 1)
                nc.scalar.activation(gate[:, :], ps[:, 7, :], ACT.Sigmoid, bias=W["b_temp"][:, 0:1]).then_inc(Z["gate_done"], 1)
                act.wait_ge(Z["centred"], g + 1)
                nc.scalar.activation(sq[:, :, :], xc[:, :, :], ACT.Square).then_inc(Z["squared"], 1)
                act.wait_ge(Z["xn_mm"], g + 1)
                nc.scalar.activation(yt[:, :], ps[:, 1, :], ACT.Identity, bias=W["beta"][:, 0:1],
                                     scale=W["gamma"][:, 0:1]).then_inc(Z["yt_done"], 1)
                act.wait_ge(Z["shifted_r"], g + 1)
                nc.scalar.activation(ex[:, :, :], ex[:, :, :], ACT.Exp).then_inc(Z["exped_r"], 1)
                act.wait_ge(Z["mw_done"], g + 1)
                nc.scalar.copy(W["mw96"][:, :, :, 0:NE],
                               hot[:, :, :].unsqueeze(2).to_broadcast([P, GB, 3, NE])).then_inc(Z["mw_copied"], 1)

        @block.gpsimd
        def _(pool):
            pool.sem_inc(Z["x2_done"], 1)
            with pool.Fori(0, NG) as g:
                pool.wait_ge(Z["x2_done"], g + 1)
                nc.gpsimd.tensor_copy(x1[:, :], xt[:, bass.ds(g * N, N)]).then_inc(Z["x1_copied"], 1)
                pool.wait_ge(Z["mods_done"], g + 1)
                for b in range(GB):
                    if b >= 2:
                        pool.wait_ge(Z["states_mm"], g * GB + b - 1)
                    nc.gpsimd.tensor_tensor(upto[:, b % 2, :, :], W["upto_end"][:, :, :],
                                            mod_s[:, b, :].unsqueeze(1).to_broadcast([P, CHUNKS, ND]),
                                            ALU.mult).then_inc(Z["upto_done"], 1)
                pool.wait_ge(Z["var_done"], g + 1)
                nc.gpsimd.tensor_tensor(rstd[:, :], var[:, :], W["neg_half"][:, :], ALU.pow).then_inc(Z["rstd_done"], 1)

        @block.vector
        def _(dve):
            with dve.Fori(0, NG) as g:
                ch = Chain(dve, Z["chain_v2"], g, 15)
                dve.wait_ge(Z["ctx_mm"], g + 1)
                nc.vector.tensor_copy(ctx_t[:, :], ps[:, 3, :]).then_inc(Z["ctx_copied"], 1)
                dve.wait_ge(Z["sig_done"], g + 1)
                nc.vector.tensor_scalar(mod_t[:, :], mod_t[:, :], 0.5, None, ALU.add).then_inc(Z["mod_done"], 1)
                dve.wait_ge(Z["wg_done"], g + 1)
                nc.vector.tensor_tensor(gated[:, :, :], xs[:, :, :], wg[:, :].rearrange("p (b c) -> p b c", b=GB),
                                        ALU.mult).then_inc(Z["gated_done"], 1)
                dve.wait_ge(Z["mods_mm"], g + 1)
                nc.vector.tensor_copy(mod_s[:, :, :], ps[:, 1, 0:GB * ND].rearrange("p (b d) -> p b d", b=GB)
                                      ).then_inc(Z["mods_done"], 1)
                dve.wait_ge(Z["gated_done"], g + 1)
                for b in range(GB):
                    dve.wait_ge(Z["lags_mm"], g * GB + b + 1)
                    if b >= 2:
                        dve.wait_ge(Z["temp_mm"], g * GB + b - 1)
                    nc.vector.tensor_tensor(
                        lagged[:, b % 2, :, :], ps[:, 2:4, :].rearrange("p h (l c) -> p (h l) c", c=C),
                        gated[:, b, :].unsqueeze(1).to_broadcast([P, LAGS, C]), ALU.mult).then_inc(Z["lagged_done"], 1)
                    dve.wait_ge(Z["states_mm"], g * GB + b + 1)
                    nc.vector.tensor_tensor(
                        states[:, b % 2, :, :], ps[:, 4 + b % 2, :].rearrange("p (j c) -> p j c", c=C),
                        W["bw"][:, :].unsqueeze(1).to_broadcast([P, 4, C]), ALU.mult).then_inc(Z["states_done"], 1)
                dve.wait_ge(Z["gate_done"], g + 1)
                nc.vector.tensor_tensor(prod[:, :], soma[:, :], gate[:, :], ALU.mult).then_inc(Z["prod_done"], 1)
                dve.wait_ge(Z["out_mm"], g + 1)
                o = ps[:, 0, :].rearrange("p (b c) -> p b c", b=GB)
                ch.link(nc.vector.tensor_reduce(mean[:, :], o, X, ALU.add))
                ch.link(nc.vector.tensor_scalar(mean[:, :], mean[:, :], 1.0 / C, None, ALU.mult))
                nc.vector.tensor_tensor(xc[:, :, :], o, mean[:, :].unsqueeze(2).to_broadcast([P, GB, C]),
                                        ALU.subtract).then_inc(Z["centred"], 1)
                dve.wait_ge(Z["squared"], g + 1)
                ch.link(nc.vector.tensor_reduce(var[:, :], sq[:, :, :], X, ALU.add))
                nc.vector.tensor_scalar(var[:, :], var[:, :], 1.0 / C, LN_EPS, ALU.mult, ALU.add).then_inc(Z["var_done"], 1)
                dve.wait_ge(Z["rstd_done"], g + 1)
                nc.vector.tensor_tensor(xn[:, :, :], xc[:, :, :], rstd[:, :].unsqueeze(2).to_broadcast([P, GB, C]),
                                        ALU.mult).then_inc(Z["xn_done"], 1)
                dve.wait_ge(Z["router_mm"], g + 1)
                ch.link(nc.vector.tensor_tensor(lg[:, :, :], ps[:, 2, 0:GB * NE].rearrange("p (b e) -> p b e", b=GB),
                                                W["router_b"][:, :].unsqueeze(1).to_broadcast([P, GB, NE]), ALU.add))
                ch.link(nc.vector.tensor_reduce(top[:, :], lg[:, :, :], X, ALU.max))
                top_b = top[:, :].unsqueeze(2).to_broadcast([P, GB, NE])
                nc.vector.tensor_tensor(ex[:, :, :], lg[:, :, :], top_b, ALU.subtract).then_inc(Z["shifted_r"], 1)
                ch.link(nc.vector.tensor_tensor(hot[:, :, :], lg[:, :, :], top_b, ALU.is_equal))
                ch.link(nc.vector.tensor_tensor(hot[:, :, :], hot[:, :, :],
                                                W["rank"][:, :].unsqueeze(1).to_broadcast([P, GB, NE]), ALU.mult))
                ch.link(nc.vector.tensor_reduce(first[:, :], hot[:, :, :], X, ALU.max))
                ch.link(nc.vector.tensor_tensor(hot[:, :, :], hot[:, :, :],
                                                first[:, :].unsqueeze(2).to_broadcast([P, GB, NE]), ALU.is_equal))
                dve.wait_ge(Z["exped_r"], g + 1)
                ch.link(nc.vector.tensor_reduce(den[:, :], ex[:, :, :], X, ALU.add))
                ch.link(nc.vector.reciprocal(den[:, :], den[:, :]))
                nc.vector.tensor_tensor(hot[:, :, :], hot[:, :, :], den[:, :].unsqueeze(2).to_broadcast([P, GB, NE]),
                                        ALU.mult).then_inc(Z["mw_done"], 1)
                dve.wait_ge(Z["mw_mm"], g + 1)
                nc.vector.tensor_copy(mw_t[:, :], ps[0:NE, 3, :])
                split3(nc, ch, m_parts, m_mid, m_rest, ps[0:96, 3, :]).then_inc(Z["m_split"], 1)
                for e in range(NE):
                    dve.wait_ge(Z["mask_mm"], g * NE + e + 1)
                    nc.vector.tensor_tensor(ym[:, e % 2, :], yt[:, :], ps[:, 4 + e % 2, :],
                                            ALU.mult).then_inc(Z["masked"], 1)
                dve.wait_ge(Z["experts_mm"], g + 1)
                nc.vector.tensor_tensor(xt[:, bass.ds(g * N, N)], x1[:, :], ps[:, 6, :], ALU.add).then_inc(Z["x2_done"], 1)
                ch.end()


def setup_attention(nc, D, W):
    with ExitStack() as own:
        def sem(name):
            return own.enter_context(nc.semaphore(name))

        loaded = sem("s3_loaded")
        capped = sem("s3_capped")
        scaled = sem("s3_scaled")
        loads = [
            (W["lap"][:, :], D["c_lap"]), (W["z"][:, 0, :], D["condB_zX"].to_broadcast([P, NB])),
            (W["z"][:, 1, :], D["condB_zY"].to_broadcast([P, NB])), (W["z"][:, 2, :], D["condB_zR"].to_broadcast([P, NB])),
            (W["w_qkv"][:, :], D["L1_attn_in_proj_weight"]), (W["b_qkv"][:, :], D["L1_attn_in_proj_bias"]),
            (W["scale"][:, :], D["L1_attn_logit_scale"]), (W["head"][:, :], D["L1_attn_head_scale"]),
            (W["w_o"][:, :], D["L1_attn_out_w"]), (W["b_o"][:, :], D["L1_attn_out_b"]),
            (W["same_head"][:, :], D["c_same_head"]), (W["head_of"][:, :], D["c_head_of"]),
            (W["v_block"][:, :], D["c_v_block"]),
        ]
        block = own.enter_context(nc.Block())

        @block.sync
        def _(sp):
            for dst, src in loads:
                sp.dma_start(dst, src).then_inc(loaded, 16)

        @block.vector
        def _(dve):
            dve.wait_ge(loaded, 16 * len(loads))
            nc.vector.tensor_scalar(W["scale"][:, :], W["scale"][:, :], LOGIT_SCALE_MAX, None, ALU.min).then_inc(capped, 1)
            nc.vector.tensor_tensor(W["v_bias"][:, :], W["b_qkv"][:, 2:3], W["head"][:, :], ALU.mult)

        @block.scalar
        def _(act):
            act.wait_ge(capped, 1)
            nc.scalar.activation(W["scale"][:, :], W["scale"][:, :], ACT.Exp).then_inc(scaled, 1)


def diffusion_and_qk(nc, W, xt, du_p, q_p, k_p):
    with ExitStack() as own:
        def sb(name, shape, dt=F32):
            return own.enter_context(nc.sbuf_tensor(name, shape, dt))

        ps = own.enter_context(nc.psum_tensor("ps3", [P, 5, N], F32))
        w = sb("stencil", [P, GB, S])
        du = sb("du", [P, GB, S])
        react = sb("react", [P, GB, S])
        qk = sb("qk", [P, 2, N])
        qk_sq = sb("qk_sq", [P, 2, N])
        norm = sb("norm", [P, 2, N])
        names = ("lap_mm summed edged chain_a du_done qk_mm qk_copied qk_squared norm_mm rooted turn_done "
                 "du_kept").split()
        Z = {n: own.enter_context(nc.semaphore("p3_" + n)) for n in names}
        block = own.enter_context(nc.Block())

        @block.tensor
        def _(pe):
            pe.sem_inc(Z["turn_done"], 1)
            with pe.Fori(0, NG) as g:
                pe.wait_ge(Z["turn_done"], g + 1)
                nc.tensor.matmul(ps[:, 0, :], W["lap"][:, :], xt[:, bass.ds(g * N, N)],
                                 start=True, stop=True).then_inc(Z["lap_mm"], 1)
                pe.wait_ge(Z["du_done"], g + 1)
                for j in range(2):
                    nc.tensor.matmul(ps[:, 1 + j, :], W["w_qkv"][:, j * C:(j + 1) * C],
                                     du[:, :, :].rearrange("p b t -> p (b t)"),
                                     start=True, stop=True).then_inc(Z["qk_mm"], 1)
                pe.wait_ge(Z["qk_squared"], 2 * g + 2)
                for j in range(2):
                    last = nc.tensor.matmul(ps[:, 3 + j, :], W["same_head"][:, :], qk_sq[:, j, :],
                                            start=True, stop=True)
                last.then_inc(Z["norm_mm"], 1)

        @block.scalar
        def _(act):
            with act.Fori(0, NG) as g:
                for j in range(2):
                    act.wait_ge(Z["qk_mm"], 2 * g + j + 1)
                    nc.scalar.activation(qk_sq[:, j, :], ps[:, 1 + j, :], ACT.Square,
                                         bias=W["b_qkv"][:, j:j + 1]).then_inc(Z["qk_squared"], 1)
                    nc.scalar.activation(qk[:, j, :], ps[:, 1 + j, :], ACT.Identity,
                                         bias=W["b_qkv"][:, j:j + 1]).then_inc(Z["qk_copied"], 1)
                act.wait_ge(Z["norm_mm"], g + 1)
                nc.scalar.activation(norm[:, :, :], ps[:, 3:5, :], ACT.Sqrt).then_inc(Z["rooted"], 1)

        @block.gpsimd
        def _(pool):
            with pool.Fori(0, NG) as g:
                pool.wait_ge(Z["turn_done"], g + 1)
                x = by_group(xt[:, bass.ds(g * N, N)])
                nc.gpsimd.tensor_tensor(w[:, :, 1:S - 1], x[:, :, 0:S - 2], x[:, :, 2:S], ALU.add).then_inc(Z["summed"], 1)

        @block.vector
        def _(dve):
            with dve.Fori(0, NG) as g:
                ch = Chain(dve, Z["chain_a"], g, 9)
                x = by_group(xt[:, bass.ds(g * N, N)])

                def z(k):
                    return W["z"][:, k, bass.ds(g * GB, GB)].unsqueeze(2).to_broadcast([P, GB, S])

                dve.wait_ge(Z["summed"], g + 1)
                nc.vector.tensor_scalar(w[:, :, 0:1], x[:, :, 1:2], 2.0, None, ALU.mult)
                ch.link(nc.vector.tensor_scalar(w[:, :, S - 1:S], x[:, :, S - 2:S - 1], 2.0, None, ALU.mult))
                nc.vector.scalar_tensor_tensor(out=react[:, :, :], in0=x, scalar=1.0, in1=x,
                                               op0=ALU.subtract, op1=ALU.mult)
                ch.link(nc.vector.scalar_tensor_tensor(out=w[:, :, :], in0=x, scalar=-2.0, in1=w[:, :, :],
                                                       op0=ALU.mult, op1=ALU.add))
                ch.link(nc.vector.tensor_tensor(w[:, :, :], w[:, :, :], z(1), ALU.mult))
                ch.link(nc.vector.tensor_tensor(react[:, :, :], react[:, :, :], z(2), ALU.mult))
                dve.wait_ge(Z["lap_mm"], g + 1)
                ch.link(nc.vector.tensor_tensor(du[:, :, :], by_group(ps[:, 0, :]), z(0), ALU.mult))
                ch.link(nc.vector.tensor_tensor(du[:, :, :], du[:, :, :], w[:, :, :], ALU.add))
                nc.vector.tensor_tensor(du[:, :, :], du[:, :, :], react[:, :, :], ALU.subtract).then_inc(Z["du_done"], 1)
                dve.wait_ge(Z["du_done"], g + 1)

                def by_position(kept):
                    return kept[:, :, bass.ds(g * GB, GB)].rearrange("p t b -> p b t")

                nc.vector.tensor_copy(by_position(du_p), du[:, :, :]).then_inc(Z["du_kept"], 1)
                dve.wait_ge(Z["rooted"], g + 1)
                ch.link(nc.vector.tensor_scalar(norm[:, :, :], norm[:, :, :], L2_EPS, None, ALU.max))
                ch.link(nc.vector.reciprocal(norm[:, :, :], norm[:, :, :]))
                dve.wait_ge(Z["qk_copied"], 2 * g + 2)
                ch.link(nc.vector.scalar_tensor_tensor(out=by_position(q_p), in0=by_group(qk[:, 0, :]),
                                                       scalar=W["scale"][:, 0:1], in1=by_group(norm[:, 0, :]),
                                                       op0=ALU.mult, op1=ALU.mult))
                nc.vector.tensor_tensor(by_position(k_p), by_group(qk[:, 1, :]), by_group(norm[:, 1, :]),
                                        ALU.mult).then_inc(Z["turn_done"], 1)
                ch.end()


def attention(nc, W, xt, du_p, q_p, k_p):
    with ExitStack() as own:
        def sb(name, shape, dt=F32):
            return own.enter_context(nc.sbuf_tensor(name, shape, dt))

        def psum(name, shape):
            return own.enter_context(nc.psum_tensor(name, shape, F32))

        ps_v = psum("ps_v", [P, TB, C])
        ps_s = psum("ps_s", [P, HQ, N])
        ps_o = psum("ps_o", [P, TB, NB])
        ps_f = psum("ps_f", [P, TB, NB])
        du4 = sb("du4", [P, TB, HQ, NB])
        k_s = sb("k_s", [P, TB, NB])
        qx = sb("qx", [P, TB, HQ, NB])
        vb = sb("vb", [P, TB, C])
        sc = sb("sc", [P, HQ, TB, NB])
        pt = sb("pt", [P, HQ, TB, NB])
        top = sb("top4", [P, HQ, TB])
        den = sb("den4", [P, HQ, TB])
        o_t = sb("o_t", [P, TB, NB])
        names = ("du_copied k_copied q_spread v_mm v_done s_mm chain_b shifted exped p_turned o_mm o_done f_mm "
                 "turn_done").split()
        Z = {n: own.enter_context(nc.semaphore("p3b_" + n)) for n in names}
        block = own.enter_context(nc.Block())
        TURNS = S // TB

        @block.gpsimd
        def _(pool):
            pool.sem_inc(Z["turn_done"], 1)
            with pool.Fori(0, TURNS) as i:
                pool.wait_ge(Z["turn_done"], i + 1)
                nc.gpsimd.tensor_copy(du4[:, :, :, :], du_p[:, bass.ds(i * TB, TB), :].unsqueeze(2)
                                      .to_broadcast([P, TB, HQ, NB])).then_inc(Z["du_copied"], 1)
                nc.gpsimd.tensor_copy(k_s[:, :, :], k_p[:, bass.ds(i * TB, TB), :]).then_inc(Z["k_copied"], 1)

        @block.tensor
        def _(pe):
            with pe.Fori(0, TURNS) as i:
                pe.wait_ge(Z["du_copied"], i + 1)
                for t in range(TB):
                    last = nc.tensor.matmul(ps_v[:, t, :], du4[:, t, :, :].rearrange("p h b -> p (h b)"),
                                            W["w_qkv"][:, 2 * C:3 * C], start=True, stop=True)
                last.then_inc(Z["v_mm"], 1)
                pe.wait_ge(Z["k_copied"], i + 1)
                pe.wait_ge(Z["q_spread"], i + 1)
                for t in range(TB):
                    for q in range(HQ):
                        rows = slice(32 * q, 32 * q + 32)
                        last = nc.tensor.matmul(ps_s[:, q, t * NB:(t + 1) * NB],
                                                qx[rows, t, :, :].rearrange("p h b -> p (h b)"), k_s[rows, t, :],
                                                start=True, stop=True)
                last.then_inc(Z["s_mm"], 1)
                pe.wait_ge(Z["v_done"], i + 1)
                pe.wait_ge(Z["p_turned"], i + 1)
                for t in range(TB):
                    for q in range(HQ):
                        last = nc.tensor.matmul(ps_o[32 * q:32 * q + 32, t, :], vb[:, t, 32 * q:32 * q + 32],
                                                pt[:, q, t, :], start=True, stop=True)
                last.then_inc(Z["o_mm"], 1)
                pe.wait_ge(Z["o_done"], i + 1)
                nc.tensor.matmul(ps_f[:, :, :].rearrange("p t b -> p (t b)"), W["w_o"][:, :],
                                 o_t[:, :, :].rearrange("p t b -> p (t b)"), start=True, stop=True).then_inc(Z["f_mm"], 1)

        @block.scalar
        def _(act):
            with act.Fori(0, TURNS) as i:
                act.wait_ge(Z["shifted"], i + 1)
                nc.scalar.activation(sc[:, :, :, :], sc[:, :, :, :], ACT.Exp).then_inc(Z["exped"], 1)
                act.wait_ge(Z["o_mm"], i + 1)
                nc.scalar.activation(o_t[:, :, :], ps_o[:, :, :], ACT.Identity, bias=W["v_bias"][:, 0:1],
                                     scale=W["head"][:, 0:1]).then_inc(Z["o_done"], 1)

        @block.vector
        def _(dve):
            with dve.Fori(0, TURNS) as i:
                ch = Chain(dve, Z["chain_b"], i, 4)
                dve.wait_ge(Z["turn_done"], i + 1)
                nc.vector.tensor_tensor(qx[:, :, :, :],
                                        q_p[:, bass.ds(i * TB, TB), :].unsqueeze(2).to_broadcast([P, TB, HQ, NB]),
                                        W["head_of"][:, :].unsqueeze(1).unsqueeze(3).to_broadcast([P, TB, HQ, NB]),
                                        ALU.mult).then_inc(Z["q_spread"], 1)
                dve.wait_ge(Z["v_mm"], i + 1)
                nc.vector.tensor_tensor(vb[:, :, :], ps_v[:, :, :], W["v_block"][:, :].unsqueeze(1)
                                        .to_broadcast([P, TB, C]), ALU.mult).then_inc(Z["v_done"], 1)
                dve.wait_ge(Z["s_mm"], i + 1)
                s = ps_s[:, :, 0:TB * NB].rearrange("p q (t b) -> p q t b", t=TB)
                ch.link(nc.vector.tensor_reduce(top[:, :, :], s, X, ALU.max))
                for q in range(HQ):
                    last = nc.vector.tensor_tensor(sc[:, q, :, :], s[:, q, :, :],
                                                   top[:, q, :].unsqueeze(2).to_broadcast([P, TB, NB]), ALU.subtract)
                last.then_inc(Z["shifted"], 1)
                dve.wait_ge(Z["exped"], i + 1)
                flat = sc[:, :, :, :].rearrange("p q t b -> p (q t) b")
                ch.link(nc.vector.tensor_reduce(den[:, :, :].rearrange("p q t -> p (q t)"), flat, X, ALU.add))
                ch.link(nc.vector.reciprocal(den[:, :, :], den[:, :, :]))
                ch.link(nc.vector.tensor_tensor(flat, flat, den[:, :, :].rearrange("p q t -> p (q t)").unsqueeze(2)
                                                .to_broadcast([P, HQ * TB, NB]), ALU.mult))
                nc.vector.transpose(pt[:, :, :, :].rearrange("p q t b -> p (q t b)"),
                                    sc[:, :, :, :].rearrange("p q t b -> p (q t b)")).then_inc(Z["p_turned"], 1)
                dve.wait_ge(Z["f_mm"], i + 1)
                x = xt[:, :].rearrange("p (b t) -> p b t", b=NB)[:, :, bass.ds(i * TB, TB)]
                nc.vector.scalar_tensor_tensor(out=x, in0=ps_f[:, :, :].rearrange("p t b -> p b t"),
                                               scalar=W["b_o"][:, 0:1], in1=x, op0=ALU.add,
                                               op1=ALU.add).then_inc(Z["turn_done"], 1)
                ch.end()


def setup_ffn1(nc, D, W):
    with ExitStack() as own:
        def tmp(name, shape, dt=F32):
            return own.enter_context(nc.sbuf_tensor(name, shape, dt))

        def sem(name):
            return own.enter_context(nc.semaphore(name))

        ids = tmp("ids4", [NL, NB], I32)
        idf = tmp("idf4", [NL, NB])
        lang = tmp("lang", [NL, 1])
        b1 = tmp("b1", [NL, 32])
        gamma = tmp("gamma4", [NL, C])
        beta = tmp("beta4", [NL, C])
        ps = own.enter_context(nc.psum_tensor("ps_s4", [P, 3, N], F32))
        loaded = sem("s4_loaded")
        chain_v = sem("s4_chain_v")
        hot = sem("s4_hot")
        picked = sem("s4_picked")
        loads = [
            (ids[:, :], D["itok_B_0_8"].to_broadcast([NL, NB])), (lang[:, :], D["c_lang"]),
            (W["ids_row"][:, :], D["itok_B_0_8"]),
            (b1[:, :], D["L1_cond2_b1"]), (W["b2"][:, :], D["L1_cond2_b2"]),
            (gamma[:, :], D["L1_cond2_gamma"]), (beta[:, :], D["L1_cond2_beta"]),
            (W["router"][:, :], D["L1_ffn_router_w"]), (W["router_b"][:, :], D["L1_ffn_router_b"].to_broadcast([P, NE])),
            (W["w1"][:, :, :], D["w1_all"]), (W["c1"][:, :, :], D["b1_all"]),
            (W["w2"][:, :, :, :], D["w2_all"]), (W["sb2"][:, :], D["L1_ffn_sb2"]), (W["rb2"][:, :], D["L1_ffn_rb2"]),
            (W["rank"][:, :], D["c_rank"].to_broadcast([P, NE])), (W["pick8"][:, :], D["c_pick"]),
        ]
        block = own.enter_context(nc.Block())

        @block.sync
        def _(sp):
            for dst, src in loads:
                sp.dma_start(dst, src).then_inc(loaded, 16)

        @block.gpsimd
        def _(pool):
            nc.gpsimd.memset(W["mw96"][:, :, :, :], 0.0)
            nc.gpsimd.memset(W["neg_half"][:, :], -0.5)

        @block.tensor
        def _(pe):
            pe.wait_ge(hot, 1)
            for k, rows in enumerate((gamma, beta)):
                nc.tensor.matmul(ps[:, k, 0:NB], rows[:, :], W["lang_hot"][:, :], start=True, stop=True)
            nc.tensor.matmul(ps[0:32, 2, 0:NB], b1[:, :], W["lang_hot"][:, :], start=True, stop=True).then_inc(picked, 1)

        @block.vector
        def _(dve):
            ch = Chain(dve, chain_v, 0, 1)
            dve.wait_ge(loaded, 16 * len(loads))
            ch.link(nc.vector.tensor_copy(idf[:, :], ids[:, :]))
            nc.vector.tensor_scalar(W["lang_hot"][:, :], idf[:, :], lang[:, 0:1], None, ALU.is_equal).then_inc(hot, 1)
            dve.wait_ge(picked, 1)
            nc.vector.tensor_copy(W["gamma_b"][:, :], ps[:, 0, 0:NB])
            nc.vector.tensor_copy(W["beta_b"][:, :], ps[:, 1, 0:NB])
            nc.vector.tensor_copy(W["b1_b"][:, :], ps[0:32, 2, 0:NB])
            ch.end()


def adapter_and_experts(nc, D, W, xt, out):
    with ExitStack() as own:
        def sb(name, shape, dt=F32):
            return own.enter_context(nc.sbuf_tensor(name, shape, dt))

        ps = own.enter_context(nc.psum_tensor("ps4", [P, 8, N], F32))
        x3 = sb("x3", [P, N])
        w1g = sb("w1g", [P, GB, 32])
        w2g = sb("w2g", [32, GB, C])
        hot_g = sb("hot_g", [NL, GB])
        had = sb("had", [32, GB, S])
        mean = sb("mean4", [P, GB])
        var = sb("var4", [P, GB])
        rstd = sb("rstd4", [P, GB])
        xc = sb("xc4", [P, GB, C])
        sq = sb("sq4", [P, GB, C])
        xn = sb("xn4", [P, GB, C])
        yt = sb("yt4", [P, N])
        lg = sb("lg4", [P, GB, NE])
        ex = sb("ex4", [P, GB, NE])
        hot = sb("hot4", [P, GB, NE])
        hot2 = sb("hot42", [P, GB, NE])
        top = sb("top42", [P, GB])
        den = sb("den42", [P, GB])
        m_parts = sb("m_parts4", [96, N], BF16)
        m_mid = sb("m_mid4", [96, N], BF16)
        m_rest = sb("m_rest4", [96, N])
        mw_t = sb("mw_t4", [NE, N])
        hh = sb("hh", [P, 4, N])
        hw = sb("hw", [P, 2, N])
        names = ("x3_copied adapters hot_copied ad1_mm ad1_done ad2_mm centred squared var_done rstd_done xn_done "
                 "xn_mm yt_done router_mm shifted exped mw_done mw_copied mw_mm m_split mask_mm hidden_mm hidden_done "
                 "weighted taken moe_mm x_done stored chain_v").split()
        Z = {n: own.enter_context(nc.semaphore("p4_" + n)) for n in names}
        block = own.enter_context(nc.Block())
        TILES = 2 * (NE + 1)

        @block.sync
        def _(sp):
            with sp.Fori(0, NG) as g:
                sp.wait_ge(Z["x_done"], g + 1)
                for b in range(GB):
                    lang = sp.value_load(W["ids_row"][0:1, bass.ds(g * GB + b, 1)], min_val=0, max_val=NL - 1)
                    sp.dma_start(w1g[:, b, :], D["L1_cond2_W1"][:, bass.ds(lang * 32, 32)]).then_inc(Z["adapters"], 16)
                    sp.dma_start(w2g[:, b, :], D["L1_cond2_W2"][:, bass.ds(lang * C, C)]).then_inc(Z["adapters"], 16)
                sp.wait_ge(Z["x_done"], g + 2)
                sp.dma_start(out[:, bass.ds(g * N, N)], xt[:, bass.ds(g * N, N)]).then_inc(Z["stored"], 16)
            sp.wait_ge(Z["stored"], 16 * NG)

        @block.gpsimd
        def _(pool):
            pool.sem_inc(Z["x_done"], 1)
            with pool.Fori(0, NG) as g:
                pool.wait_ge(Z["x_done"], g + 1)
                nc.gpsimd.tensor_copy(x3[:, :], xt[:, bass.ds(g * N, N)]).then_inc(Z["x3_copied"], 1)
                nc.gpsimd.tensor_copy(hot_g[:, :], W["lang_hot"][:, bass.ds(g * GB, GB)]).then_inc(Z["hot_copied"], 1)
                pool.wait_ge(Z["var_done"], g + 1)
                nc.gpsimd.tensor_tensor(rstd[:, :], var[:, :], W["neg_half"][:, :], ALU.pow).then_inc(Z["rstd_done"], 1)

        @block.tensor
        def _(pe):
            with pe.Fori(0, NG) as g:
                pe.wait_ge(Z["adapters"], 32 * GB * g + 32 * GB)
                pe.wait_ge(Z["x3_copied"], g + 1)
                for b in range(GB):
                    last = nc.tensor.matmul(ps[0:32, 0, b * S:(b + 1) * S], w1g[:, b, :], x3[:, b * S:(b + 1) * S],
                                            start=True, stop=True)
                last.then_inc(Z["ad1_mm"], 1)
                pe.wait_ge(Z["hot_copied"], g + 1)
                pe.wait_ge(Z["ad1_done"], g + 1)
                for b in range(GB):
                    to = ps[:, 1, b * C:(b + 1) * C]
                    nc.tensor.matmul(to, x3[:, b * S:(b + 1) * S], W["ident"][:, :], start=True, stop=False)
                    nc.tensor.matmul(to, had[:, b, :], w2g[:, b, :], start=False, stop=False)
                    last = nc.tensor.matmul(to, hot_g[:, b:b + 1].to_broadcast([NL, P]), W["b2"][:, :],
                                            start=False, stop=True)
                last.then_inc(Z["ad2_mm"], 1)
                pe.wait_ge(Z["xn_done"], g + 1)
                for b in range(GB):
                    last = nc.tensor.transpose(ps[:, 0, b * S:(b + 1) * S], xn[:, b, :], W["ident"][:, :])
                last.then_inc(Z["xn_mm"], 1)
                pe.wait_ge(Z["yt_done"], g + 1)
                for b in range(GB):
                    last = nc.tensor.matmul(ps[:, 1, b * NE:(b + 1) * NE], yt[:, b * S:(b + 1) * S], W["router"][:, :],
                                            start=True, stop=True)
                last.then_inc(Z["router_mm"], 1)

                def hidden(k):
                    if k >= 2:
                        pe.wait_ge(Z["hidden_done"], g * TILES + k - 1)
                    nc.tensor.matmul(ps[:, 2 + k % 2, :], W["w1"][:, k, :], yt[:, :],
                                     start=True, stop=True).then_inc(Z["hidden_mm"], 1)

                def mask(e):
                    if e >= 2:
                        pe.wait_ge(Z["weighted"], g * 2 * NE + 2 * (e - 1))
                    nc.tensor.matmul(ps[:, 4 + e % 2, :], W["pick8"][:, e:e + 1].to_broadcast([96, P]), m_parts[:, :],
                                     start=True, stop=True).then_inc(Z["mask_mm"], 1)

                def outwards(k):
                    if k < 2:
                        pe.wait_ge(Z["hidden_done"], g * TILES + k + 1)
                        src = hh[:, k, :]
                    else:
                        pe.wait_ge(Z["weighted"], g * 2 * NE + k - 1)
                        src = hw[:, k % 2, :]
                    ins = nc.tensor.matmul(ps[:, 6, :], W["w2"][:, k // 2, k % 2, :], src, start=(k == 0), stop=False)
                    if k >= 2:
                        ins.then_inc(Z["taken"], 1)

                hidden(0)
                hidden(1)
                outwards(0)
                hidden(2)
                outwards(1)
                hidden(3)
                pe.wait_ge(Z["mw_copied"], g + 1)
                for b in range(GB):
                    last = nc.tensor.matmul(ps[0:96, 7, b * S:(b + 1) * S],
                                            W["mw96"][:, b, :, :].rearrange("p k e -> p (k e)"), W["ident"][:, :],
                                            start=True, stop=True)
                last.then_inc(Z["mw_mm"], 1)
                pe.wait_ge(Z["m_split"], g + 1)
                mask(0)
                for k in range(2, TILES):
                    if k % 2 == 0 and k // 2 < NE:
                        mask(k // 2)
                    if k + 2 < TILES:
                        hidden(k + 2)
                    outwards(k)
                nc.tensor.matmul(ps[:, 6, :], W["rb2"][:, :], mw_t[:, :], start=False, stop=True).then_inc(Z["moe_mm"], 1)

        @block.scalar
        def _(act):
            with act.Fori(0, NG) as g:
                act.wait_ge(Z["centred"], g + 1)
                nc.scalar.activation(sq[:, :, :], xc[:, :, :], ACT.Square).then_inc(Z["squared"], 1)
                act.wait_ge(Z["shifted"], g + 1)
                nc.scalar.activation(ex[:, :, :], ex[:, :, :], ACT.Exp).then_inc(Z["exped"], 1)

                def gelu(k):
                    act.wait_ge(Z["hidden_mm"], g * TILES + k + 1)
                    if k >= 6:
                        act.wait_ge(Z["weighted"], g * 2 * NE + k - 5)
                    nc.scalar.activation(hh[:, k % 4, :], ps[:, 2 + k % 2, :], ACT.Gelu,
                                         bias=W["c1"][:, k // 2, k % 2:k % 2 + 1]).then_inc(Z["hidden_done"], 1)

                gelu(0)
                gelu(1)
                gelu(2)
                gelu(3)
                act.wait_ge(Z["mw_done"], g + 1)
                nc.scalar.copy(W["mw96"][:, :, :, 0:NE],
                               hot[:, :, :].unsqueeze(2).to_broadcast([P, GB, 3, NE])).then_inc(Z["mw_copied"], 1)
                for k in range(4, TILES):
                    gelu(k)

        @block.vector
        def _(dve):
            with dve.Fori(0, NG) as g:
                ch = Chain(dve, Z["chain_v"], g, 24)

                def vec(v):
                    return v[:, bass.ds(g * GB, GB)].unsqueeze(2)

                dve.wait_ge(Z["ad1_mm"], g + 1)
                ch.link(nc.vector.tensor_tensor(had[:, :, :], by_group(ps[0:32, 0, :]),
                                                vec(W["b1_b"]).to_broadcast([32, GB, S]), ALU.add))
                nc.vector.tensor_scalar(had[:, :, :], had[:, :, :], 0.0, None, ALU.max).then_inc(Z["ad1_done"], 1)
                dve.wait_ge(Z["ad2_mm"], g + 1)
                o = ps[:, 1, :].rearrange("p (b c) -> p b c", b=GB)
                ch.link(nc.vector.tensor_reduce(mean[:, :], o, X, ALU.add))
                ch.link(nc.vector.tensor_scalar(mean[:, :], mean[:, :], 1.0 / C, None, ALU.mult))
                nc.vector.tensor_tensor(xc[:, :, :], o, mean[:, :].unsqueeze(2).to_broadcast([P, GB, C]),
                                        ALU.subtract).then_inc(Z["centred"], 1)
                dve.wait_ge(Z["squared"], g + 1)
                ch.link(nc.vector.tensor_reduce(var[:, :], sq[:, :, :], X, ALU.add))
                nc.vector.tensor_scalar(var[:, :], var[:, :], 1.0 / C, LN_EPS, ALU.mult, ALU.add).then_inc(Z["var_done"], 1)
                dve.wait_ge(Z["rstd_done"], g + 1)
                nc.vector.tensor_tensor(xn[:, :, :], xc[:, :, :], rstd[:, :].unsqueeze(2).to_broadcast([P, GB, C]),
                                        ALU.mult).then_inc(Z["xn_done"], 1)
                dve.wait_ge(Z["xn_mm"], g + 1)
                y = by_group(yt[:, :])
                ch.link(nc.vector.tensor_tensor(y, by_group(ps[:, 0, :]), vec(W["gamma_b"]).to_broadcast([P, GB, S]), ALU.mult))
                nc.vector.tensor_tensor(y, y, vec(W["beta_b"]).to_broadcast([P, GB, S]), ALU.add).then_inc(Z["yt_done"], 1)
                dve.wait_ge(Z["router_mm"], g + 1)
                ch.link(nc.vector.tensor_tensor(lg[:, :, :], ps[:, 1, 0:GB * NE].rearrange("p (b e) -> p b e", b=GB),
                                                W["router_b"][:, :].unsqueeze(1).to_broadcast([P, GB, NE]), ALU.add))
                ch.link(nc.vector.tensor_reduce(top[:, :], lg[:, :, :], X, ALU.max))
                top_b = top[:, :].unsqueeze(2).to_broadcast([P, GB, NE])
                nc.vector.tensor_tensor(ex[:, :, :], lg[:, :, :], top_b, ALU.subtract).then_inc(Z["shifted"], 1)
                rank = W["rank"][:, :].unsqueeze(1).to_broadcast([P, GB, NE])

                def first_of_top(to):
                    ch.link(nc.vector.tensor_tensor(to[:, :, :], lg[:, :, :], top_b, ALU.is_equal))
                    ch.link(nc.vector.tensor_tensor(to[:, :, :], to[:, :, :], rank, ALU.mult))
                    ch.link(nc.vector.tensor_reduce(top[:, :], to[:, :, :], X, ALU.max))
                    ch.link(nc.vector.tensor_tensor(to[:, :, :], to[:, :, :], top_b, ALU.is_equal))

                first_of_top(hot)
                ch.link(nc.vector.scalar_tensor_tensor(out=lg[:, :, :], in0=hot[:, :, :], scalar=-1e30, in1=lg[:, :, :],
                                                       op0=ALU.mult, op1=ALU.add))
                ch.link(nc.vector.tensor_reduce(top[:, :], lg[:, :, :], X, ALU.max))
                first_of_top(hot2)
                ch.link(nc.vector.tensor_tensor(hot[:, :, :], hot[:, :, :], hot2[:, :, :], ALU.add))
                dve.wait_ge(Z["exped"], g + 1)
                nc.vector.tensor_tensor(hot[:, :, :], hot[:, :, :], ex[:, :, :], ALU.mult)
                ch.link(nc.vector.tensor_reduce(den[:, :], ex[:, :, :], X, ALU.add))
                ch.link(nc.vector.reciprocal(den[:, :], den[:, :]))
                nc.vector.tensor_tensor(hot[:, :, :], hot[:, :, :], den[:, :].unsqueeze(2).to_broadcast([P, GB, NE]),
                                        ALU.mult).then_inc(Z["mw_done"], 1)
                dve.wait_ge(Z["mw_mm"], g + 1)
                nc.vector.tensor_copy(mw_t[:, :], ps[0:NE, 7, :])
                split3(nc, ch, m_parts, m_mid, m_rest, ps[0:96, 7, :]).then_inc(Z["m_split"], 1)
                for k in range(2, TILES):
                    if k % 2 == 0:
                        dve.wait_ge(Z["mask_mm"], g * NE + k // 2)
                    dve.wait_ge(Z["hidden_done"], g * TILES + k + 1)
                    if k >= 4:
                        dve.wait_ge(Z["taken"], g * 2 * NE + k - 3)
                    nc.vector.tensor_tensor(hw[:, k % 2, :], hh[:, k % 4, :], ps[:, 4 + (k // 2 - 1) % 2, :],
                                            ALU.mult).then_inc(Z["weighted"], 1)
                dve.wait_ge(Z["moe_mm"], g + 1)
                nc.vector.scalar_tensor_tensor(out=xt[:, bass.ds(g * N, N)], in0=ps[:, 6, :], scalar=W["sb2"][:, 0:1],
                                               in1=x3[:, :], op0=ALU.add, op1=ALU.add).then_inc(Z["x_done"], 1)
                ch.end()


def build(nc, D, out):
    with ExitStack() as ctx:
        def sb(name, shape, dt=F32):
            return ctx.enter_context(nc.sbuf_tensor(name, shape, dt))

        xt = sb("xt", [P, NB * S])
        ident = sb("ident", [P, P])
        with ExitStack() as first:
            def w(name, shape, dt=F32):
                return first.enter_context(nc.sbuf_tensor(name, shape, dt))

            W = {
                "ident": ident, "lora_a": w("lora_a", [P, P]), "w_ab": w("w_ab", [P, 2 * DI]),
                "w_bc": w("w_bc", [P, NT, 96]), "w_delta": w("w_delta", [P, NT, DI]),
                "conv_w": w("conv_w", [P, NT, 4]), "conv_b": w("conv_b", [P, NT]),
                "dt_b": w("dt_b", [P, NT]), "a": w("a", [P, NT, NS]), "d_skip": w("d_skip", [P, NT]),
                "out_w": w("out_w", [P, NT, C]), "pick": w("pick", [96, 32], BF16),
                "gates": w("gates", [P, NB, NE]), "decay": w("decay", [P, 2, 2, GB, S]),
            }
            setup_scan(nc, first, D, W, xt)
            selective_scan(nc, D, W, xt)
        with ExitStack() as second:
            def w(name, shape, dt=F32):
                return second.enter_context(nc.sbuf_tensor(name, shape, dt))

            W = {
                "ident": ident, "shift": w("shift", [P, LAGS, S]), "wg_x": w("wg_x", [P, C]),
                "wg_ctx": w("wg_ctx", [P, C]), "bg": w("bg", [1, C]), "wn1": w("wn1", [P, 32]),
                "bn1": w("bn1", [32, 1]), "wn2": w("wn2", [32, ND]), "bn2": w("bn2", [ND, 1]),
                "w_soma": w("w_soma", [P, C]), "b_soma": w("b_soma", [P, 1]), "w_temp": w("w_temp", [P, C]),
                "b_temp": w("b_temp", [P, 1]), "w_out": w("w_out", [P, C]), "gamma": w("gamma", [P, 1]),
                "beta": w("beta", [P, 1]), "router": w("router", [P, NE]), "router_b": w("router_b", [P, NE]),
                "expert_w": w("expert_w", [P, NE, C]), "expert_b": w("expert_b", [NE, C]),
                "rank": w("rank", [P, NE]), "pick8": w("pick8", [96, 32], BF16),
                "from_start": w("from_start", [P, 4, S]), "k_ctx": w("k_ctx", [P, S]),
                "upto_end": w("upto_end", [P, CHUNKS, ND]), "bw": w("bw", [P, C]),
                "bw_lag": w("bw_lag", [ND, LAGS, C]), "ones": w("ones", [1, P]),
                "mw96": w("mw96", [P, GB, 3, 32]), "neg_half": w("neg_half", [P, GB]),
            }
            setup_ffn0(nc, D, W)
            traces_and_experts(nc, W, xt)
        with ExitStack() as third:
            def w(name, shape, dt=F32):
                return third.enter_context(nc.sbuf_tensor(name, shape, dt))

            W = {
                "lap": w("lap", [P, C]), "z": w("z", [P, 3, NB]), "w_qkv": w("w_qkv", [P, 3 * C]),
                "b_qkv": w("b_qkv", [P, 3]), "scale": w("scale", [P, 1]), "head": w("head", [P, 1]),
                "v_bias": w("v_bias", [P, 1]), "w_o": w("w_o", [P, C]), "b_o": w("b_o", [P, 1]),
                "same_head": w("same_head", [P, C]), "head_of": w("head_of", [P, HQ]), "v_block": w("v_block", [P, C]),
            }
            du_p = w("du_p", [P, S, NB])
            q_p = w("q_p", [P, S, NB])
            k_p = w("k_p", [P, S, NB])
            setup_attention(nc, D, W)
            diffusion_and_qk(nc, W, xt, du_p, q_p, k_p)
            attention(nc, W, xt, du_p, q_p, k_p)
        with ExitStack() as fourth:
            def w(name, shape, dt=F32):
                return fourth.enter_context(nc.sbuf_tensor(name, shape, dt))

            W = {
                "ident": ident, "b2": w("b2", [NL, C]), "ids_row": w("ids_row", [1, NB], I32),
                "router": w("router4", [P, NE]), "router_b": w("router_b4", [P, NE]),
                "w1": w("w1", [P, 2 * (NE + 1), P]), "c1": w("c1", [P, NE + 1, 2]),
                "w2": w("w2", [P, NE + 1, 2, C]), "sb2": w("sb2", [P, 1]), "rb2": w("rb2", [NE, C]),
                "rank": w("rank4", [P, NE]), "pick8": w("pick84", [96, 32], BF16), "mw96": w("mw964", [P, GB, 3, 32]),
                "neg_half": w("neg_half4", [P, GB]), "lang_hot": w("lang_hot", [NL, NB]),
                "gamma_b": w("gamma_b", [P, NB]), "beta_b": w("beta_b", [P, NB]), "b1_b": w("b1_b", [32, NB]),
            }
            setup_ffn1(nc, D, W)
            adapter_and_experts(nc, D, W, xt, out)


def lay_out(a):
    def tiles(w, rows):
        return w.reshape(rows // P, P, -1).transpose(1, 0, 2)

    xp = a["L0_attn_x_proj_w"]
    bc = xp[DI:].T
    L = {
        "x": a["x"].transpose(2, 0, 1).reshape(C, NB * S),
        "L0_cond_lora_B": a["L0_cond_lora_B"].transpose(1, 0, 2).reshape(C, NE * R),
        "L0_cond_lora_A": a["L0_cond_lora_A"].transpose(2, 0, 1).reshape(C, NE * R),
        "L0_attn_in_proj_w": a["L0_attn_in_proj_w"].T,
        "x_proj_delta": tiles(xp[:DI], DI),
        "x_proj_bc": tiles(np.concatenate([bc, bc, bc], axis=1), DI),
        "L0_attn_dt_proj_w": tiles(a["L0_attn_dt_proj_w"].T, DI),
        "L0_cond_gate_W1": a["L0_cond_gate_W1"],
        "L0_cond_gate_b1": a["L0_cond_gate_b1"].reshape(-1, 1),
        "L0_cond_gate_W2": a["L0_cond_gate_W2"],
        "L0_cond_gate_b2": a["L0_cond_gate_b2"].reshape(1, -1),
        "itok_B_4_6": a["itok_B_4_6"].reshape(1, -1),
        "L0_attn_conv_w": tiles(a["L0_attn_conv_w"].reshape(DI, 4), DI),
        "L0_attn_conv_b": a["L0_attn_conv_b"].reshape(NT, P).T,
        "L0_attn_dt_proj_b": a["L0_attn_dt_proj_b"].reshape(NT, P).T,
        "L0_attn_D_param": a["L0_attn_D_param"].reshape(NT, P).T,
        "L0_attn_A_log": tiles(a["L0_attn_A_log"], DI),
        "L0_attn_out_proj_w": tiles(a["L0_attn_out_proj_w"].T, DI),
        "condB_tauraws": a["condB_tauraws"].reshape(1, ND),
        "tau_column": np.tile(a["condB_tauraws"], P // ND).reshape(P, 1),
        "L0_cond2_tau_ctx": a["L0_cond2_tau_ctx"].reshape(1, 1),
        "cond_1024": a["cond_1024"].T,
        "wg_x": a["L0_cond2_Wg"][:, :C].T, "wg_ctx": a["L0_cond2_Wg"][:, C:].T,
        "L0_cond2_bg": a["L0_cond2_bg"].reshape(1, C),
        "L0_cond2_Wn1": a["L0_cond2_Wn1"].T, "L0_cond2_bn1": a["L0_cond2_bn1"].reshape(-1, 1),
        "cond_256": a["cond_256"].T, "condB_bn2": a["condB_bn2"].reshape(ND, 1),
        "L0_cond2_Wsoma": a["L0_cond2_Wsoma"].T, "L0_cond2_bsoma": a["L0_cond2_bsoma"].reshape(C, 1),
        "L0_cond2_Wtemp": a["L0_cond2_Wtemp"].T, "L0_cond2_btemp": a["L0_cond2_btemp"].reshape(C, 1),
        "L0_cond2_Wout": a["L0_cond2_Wout"].T, "L0_cond2_gamma": a["L0_cond2_gamma"].reshape(C, 1),
        "L0_cond2_beta": a["L0_cond2_beta"].reshape(C, 1),
        "L0_ffn_router_w": a["L0_ffn_router_w"].T, "L0_ffn_router_b": a["L0_ffn_router_b"].reshape(1, NE),
        "L0_ffn_expert_w": a["L0_ffn_expert_w"].transpose(2, 0, 1), "L0_ffn_expert_b": a["L0_ffn_expert_b"],
        "condB_zX": a["condB_zX"].reshape(1, NB), "condB_zY": a["condB_zY"].reshape(1, NB),
        "condB_zR": a["condB_zR"].reshape(1, NB),
        "L1_attn_in_proj_weight": a["L1_attn_in_proj_weight"].T,
        "L1_attn_in_proj_bias": a["L1_attn_in_proj_bias"].reshape(3, C).T,
        "L1_attn_logit_scale": np.repeat(a["L1_attn_logit_scale"].reshape(-1), C // 16).reshape(C, 1),
        "L1_attn_head_scale": np.repeat(a["L1_attn_head_scale"].reshape(-1), C // 16).reshape(C, 1),
        "L1_attn_out_w": a["L1_attn_out_w"].T, "L1_attn_out_b": a["L1_attn_out_b"].reshape(C, 1),
        "itok_B_0_8": a["itok_B_0_8"].reshape(1, NB),
        "L1_cond2_W1": a["L1_cond2_W1"].transpose(1, 0, 2).reshape(C, -1),
        "L1_cond2_W2": a["L1_cond2_W2"].transpose(1, 0, 2).reshape(32, -1),
        "L1_cond2_b1": a["L1_cond2_b1"], "L1_cond2_b2": a["L1_cond2_b2"],
        "L1_cond2_gamma": a["L1_cond2_gamma"], "L1_cond2_beta": a["L1_cond2_beta"],
        "L1_ffn_router_w": a["L1_ffn_router_w"], "L1_ffn_router_b": a["L1_ffn_router_b"].reshape(1, NE),
        "w1_all": np.concatenate([a["L1_ffn_sw1"][None], a["L1_ffn_rw1"]]).reshape(NE + 1, C, 2, P)
        .transpose(1, 0, 2, 3).reshape(C, 2 * (NE + 1), P),
        "b1_all": np.concatenate([a["L1_ffn_sb1"][None], a["L1_ffn_rb1"]]).reshape(NE + 1, 2, P).transpose(2, 0, 1),
        "w2_all": np.concatenate([a["L1_ffn_sw2"][None], a["L1_ffn_rw2"]]).reshape(NE + 1, 2, P, C).transpose(2, 0, 1, 3),
        "L1_ffn_sb2": a["L1_ffn_sb2"].reshape(C, 1), "L1_ffn_rb2": a["L1_ffn_rb2"],
        "c_expert": np.arange(NE, dtype=np.float32).reshape(1, -1),
        "c_ident": np.eye(P, dtype=np.float32),
        "c_pick": np.tile(np.eye(32, dtype=np.float32), (3, 1)),
    }
    s, t, k = np.arange(S), np.arange(S), np.arange(CHUNKS)
    since = t[None, :] - s[:, None]
    before = LAGS * k[None, :] - s[:, None]
    chunk = (4 * np.arange(4)[None, :] + np.arange(P)[:, None] // ND)[:, :, None]
    lag = np.arange(LAGS)
    L.update({
        "c_lag": lag.reshape(1, -1), "c_rank": np.arange(NE, 0, -1).reshape(1, -1),
        "c_upto_at": np.maximum(before - 1, 0), "c_upto_on": before > 0,
        "c_from_at": np.clip(t[None, None, :] - LAGS * chunk + 1, 0, LAGS),
        "c_from_on": t[None, None, :] // LAGS == chunk,
        "c_ctx_at": np.maximum(since, 0), "c_ctx_on": since >= 0,
        "c_shift": (since[:, None, :] == lag[None, :, None]) & (t // LAGS == (s // LAGS)[:, None])[:, None, :],
    })
    c = np.arange(C)
    lap = -2.0 * np.eye(C)
    for to in range(C):
        lap[abs(to - 1), to] += 1
        lap[C - 1 - abs(C - 2 - to), to] += 1
    L.update({
        "c_lap": lap, "c_same_head": c[:, None] // 8 == c[None, :] // 8,
        "c_head_of": c[:, None] // 8 % HQ == np.arange(HQ)[None, :],
        "c_v_block": np.arange(P)[:, None] // NB == (c // 8 % HQ)[None, :],
        "c_lang": np.arange(NL).reshape(NL, 1),
    })
    for name in L:
        if name.startswith("c_"):
            L[name] = L[name].astype(np.float32)
    return L


_BF16_CONSTS = ("c_pick",)


def kernel(**inputs):
    import ml_dtypes
    import concourse.bacc as _bacc
    from concourse.bass_utils import run_bass_kernel_spmd as _run

    nc = _bacc.Bacc("TRN2", target_bir_lowering=False, num_devices=1)
    arrays, D = {}, {}
    for name, a in lay_out({k: np.asarray(v) for k, v in inputs.items()}).items():
        if name in _BF16_CONSTS:
            a = a.astype(ml_dtypes.bfloat16)
        a = np.ascontiguousarray(a)
        arrays[f"in_{name}"] = a
        D[name] = nc.dram_tensor(f"in_{name}", a.shape, mybir.dt.from_np(a.dtype), kind="ExternalInput").ap()
    out = nc.dram_tensor("out_0", (C, NB * S), F32, kind="ExternalOutput").ap()
    build(nc, D, out)
    r = _run(nc, [arrays], core_ids=[0])
    got = np.asarray(r.results[0]["out_0"])
    return np.ascontiguousarray(got.reshape(C, NB, S).transpose(1, 2, 0))
```

```python
from contextlib import ExitStack, contextmanager

import numpy as np

import concourse.bass as bass
from concourse import mybir

F32 = mybir.dt.float32
BF16 = mybir.dt.bfloat16
I32 = mybir.dt.int32
ALU = mybir.AluOpType
ACT = mybir.ActivationFunctionType
X = mybir.AxisListType.X

P = 128
NB = 32
S = 128
C = 128
GB = 4
NG = NB // GB
N = GB * S
NE = 8
R = 16
DI = 256
NT = DI // P
NS = 16
LORA_SCALE = 32 / R
RING = 4
LAG = 2
ND = 32
LAGS = 8
CHUNKS = S // LAGS
LN_EPS = 1e-5
LOGIT_SCALE_MAX = float(np.log(1.0 / 0.01))
L2_EPS = 1e-12
HQ = 4
TB = 8
NL = 10


class Chain:

    def __init__(self, eng, sem, turn, per_turn):
        self.eng, self.sem, self.base, self.per_turn, self.at = eng, sem, turn * per_turn, per_turn, 0

    def link(self, ins):
        ins.then_inc(self.sem, 1)
        self.at += 1
        self.eng.wait_ge(self.sem, self.base + self.at)

    def end(self):
        assert self.at == self.per_turn, (self.at, self.per_turn)


@contextmanager
def phase_semaphores(nc):
    taken = []

    def sem(name):
        taken.append(nc.alloc_semaphore(name))
        return taken[-1]

    yield sem
    nc.clear_and_free_semaphores(taken)
    nc.all_engine_barrier()


def in_pairs(eng, front, body):
    front(0, 0)
    with eng.Fori(0, NG // 2 - 1) as i:
        body(2 * i, 0, 2 * i + 1)
        body(2 * i + 1, 1, 2 * i + 2)
    body(NG - 2, 0, NG - 1)
    body(NG - 1, 1, None)


def by_group(ap):
    return ap.rearrange("p (b t) -> p b t", b=GB)


def setup_scan(nc, ctx, D, W, xt):
    def sb(name, shape, dt=F32):
        return ctx.enter_context(nc.sbuf_tensor(name, shape, dt))

    with ExitStack() as own:
        def tmp(name, shape, dt=F32):
            return own.enter_context(nc.sbuf_tensor(name, shape, dt))

        def psum(name, shape):
            return own.enter_context(nc.psum_tensor(name, shape, F32))

        sem = own.enter_context(phase_semaphores(nc))

        lora_b = tmp("lora_b", [P, P])
        in_proj = tmp("in_proj", [P, 2 * DI])
        xp_rows = tmp("xp_rows", [P, NT, DI])
        dt_w = tmp("dt_w", [P, NT, DI])
        gate_w1 = tmp("gate_w1", [P, 32])
        gate_b1 = tmp("gate_b1", [32, 1])
        gate_w2 = tmp("gate_w2", [32, NE])
        gate_b2 = tmp("gate_b2", [P, NE])
        ids = tmp("ids", [P, NB], I32)
        idf = tmp("idf", [P, NB])
        expert = tmp("expert", [P, NE])
        allowed = tmp("allowed", [P, NB, NE])
        hid = tmp("hid", [32, NG, N])
        top = tmp("top", [P, NB])
        ps_h = psum("ps_h", [32, 2, N])
        ps_l = psum("ps_l", [P, NB, NE])
        ps_ab = psum("ps_ab", [P, 2 * DI])
        ps_d = psum("ps_d", [P, NT, DI])

        loaded = sem("setup_loaded")
        x_loaded = sem("x_loaded")
        hid_done = sem("hid_done")
        h_mm = sem("h_mm")
        logits_done = sem("logits_done")
        ab_mm = sem("ab_mm")
        delta_mm = sem("delta_mm")
        chain_v = sem("setup_chain_v")
        act_ready = sem("setup_act_ready")
        shifted = sem("logits_shifted")
        exped = sem("gates_exped")

        loads = [
            (lora_b[:, :], D["L0_cond_lora_B"]), (in_proj[:, :], D["L0_attn_in_proj_w"]),
            (xp_rows[:, :, :], D["x_proj_delta"]), (dt_w[:, :, :], D["L0_attn_dt_proj_w"]),
            (gate_w1[:, :], D["L0_cond_gate_W1"]), (gate_b1[:, :], D["L0_cond_gate_b1"]),
            (gate_w2[:, :], D["L0_cond_gate_W2"]),
            (gate_b2[:, :], D["L0_cond_gate_b2"].to_broadcast([P, NE])),
            (ids[:, :], D["itok_B_4_6"].to_broadcast([P, NB])),
            (expert[:, :], D["c_expert"].to_broadcast([P, NE])),
            (W["ident"][:, :], D["c_ident"]), (W["lora_a"][:, :], D["L0_cond_lora_A"]),
            (W["w_bc"][:, :, :], D["x_proj_bc"]), (W["conv_w"][:, :, :], D["L0_attn_conv_w"]),
            (W["conv_b"][:, :], D["L0_attn_conv_b"]), (W["dt_b"][:, :], D["L0_attn_dt_proj_b"]),
            (W["a"][:, :, :], D["L0_attn_A_log"]), (W["d_skip"][:, :], D["L0_attn_D_param"]),
            (W["out_w"][:, :, :], D["L0_attn_out_proj_w"]), (W["pick"][:, :], D["c_pick"]),
        ]
        block = own.enter_context(nc.Block())

        @block.sync
        def _(sp):
            sp.dma_start(xt[:, :], D["x"]).then_inc(x_loaded, 16)
            for dst, src in loads:
                sp.dma_start(dst, src).then_inc(loaded, 16)

        @block.tensor
        def _(pe):
            pe.wait_ge(loaded, 16 * len(loads))
            pe.wait_ge(x_loaded, 16)
            for g in range(NG):
                if g >= 2:
                    pe.wait_ge(hid_done, g - 1)
                nc.tensor.matmul(ps_h[:, g % 2, :], gate_w1[:, :], xt[:, g * N:(g + 1) * N],
                                 start=True, stop=True).then_inc(h_mm, 1)
            nc.tensor.matmul(ps_ab[:, :], lora_b[:, :], in_proj[:, :], start=True, stop=True).then_inc(ab_mm, 1)
            for kt in range(NT):
                for mt in range(NT):
                    last = nc.tensor.matmul(ps_d[:, kt, :], xp_rows[:, mt, kt * P:(kt + 1) * P], dt_w[:, mt, :],
                                            start=(mt == 0), stop=(mt == NT - 1))
            last.then_inc(delta_mm, 1)
            pe.wait_ge(hid_done, NG)
            for b in range(NB):
                last = nc.tensor.matmul(ps_l[:, b, :], hid[:, b // GB, (b % GB) * S:(b % GB + 1) * S],
                                        gate_w2[:, :], start=True, stop=True)
            last.then_inc(logits_done, 1)

        @block.scalar
        def _(act):
            act.wait_ge(loaded, 16 * len(loads))
            for g in range(NG):
                act.wait_ge(h_mm, g + 1)
                nc.scalar.activation(hid[:, g, :], ps_h[:, g % 2, :], ACT.Relu,
                                     bias=gate_b1[:, 0:1]).then_inc(hid_done, 1)
            act.wait_ge(ab_mm, 1)
            nc.scalar.mul(W["w_ab"][:, :], ps_ab[:, :], LORA_SCALE)
            act.wait_ge(delta_mm, 1)
            nc.scalar.copy(W["w_delta"][:, :, :], ps_d[:, :, :])
            nc.scalar.activation(W["a"][:, :, :], W["a"][:, :, :], ACT.Exp).then_inc(act_ready, 1)
            act.wait_ge(act_ready, 1)
            nc.scalar.mul(W["a"][:, :, :], W["a"][:, :, :], -1.0)
            act.wait_ge(shifted, 1)
            nc.scalar.activation(W["gates"][:, :, :], W["gates"][:, :, :], ACT.Exp).then_inc(exped, 1)

        @block.vector
        def _(dve):
            ch = Chain(dve, chain_v, 0, 12)
            dve.wait_ge(loaded, 16 * len(loads))
            ch.link(nc.vector.tensor_copy(idf[:, :], ids[:, :]))
            ch.link(nc.vector.tensor_scalar(idf[:, :], idf[:, :], 1.0, None, ALU.add))
            ch.link(nc.vector.tensor_tensor(allowed[:, :, :], idf[:, :].unsqueeze(2).to_broadcast([P, NB, NE]),
                                            expert[:, :].unsqueeze(1).to_broadcast([P, NB, NE]), ALU.is_equal))
            ch.link(nc.vector.memset(allowed[:, :, 0:1], 1.0))
            ch.link(nc.vector.tensor_scalar(allowed[:, :, :], allowed[:, :, :], 1e9, -1e9, ALU.mult, ALU.add))
            dve.wait_ge(logits_done, 1)
            gates = W["gates"][:, :, :]
            ch.link(nc.vector.tensor_tensor(gates, ps_l[:, :, :],
                                            gate_b2[:, :].unsqueeze(1).to_broadcast([P, NB, NE]), ALU.add))
            ch.link(nc.vector.tensor_tensor(gates, gates, allowed[:, :, :], ALU.add))
            ch.link(nc.vector.tensor_reduce(top[:, :], gates, X, ALU.max))
            nc.vector.tensor_tensor(gates, gates, top[:, :].unsqueeze(2).to_broadcast([P, NB, NE]),
                                    ALU.subtract).then_inc(shifted, 1)
            dve.wait_ge(exped, 1)
            ch.link(nc.vector.tensor_reduce(top[:, :], gates, X, ALU.add))
            ch.link(nc.vector.reciprocal(top[:, :], top[:, :]))
            ch.link(nc.vector.tensor_tensor(gates, gates, top[:, :].unsqueeze(2).to_broadcast([P, NB, NE]), ALU.mult))
            ch.link(nc.vector.memset(W["decay"][:, :, :, :, :], 0.0))
            ch.end()


def selective_scan(nc, D, W, xt):
    with ExitStack() as own:
        def sb(name, shape, dt=F32):
            return own.enter_context(nc.sbuf_tensor(name, shape, dt))

        def psum(name, shape):
            return own.enter_context(nc.psum_tensor(name, shape, F32))

        sem = own.enter_context(phase_semaphores(nc))

        ps_y = psum("ps_y", [P, NT, N])
        ps_b = psum("ps_b", [P, 2, N])
        ps_c = psum("ps_c", [P, 2, N])
        ps_w = psum("ps_w", [P, 2, N])
        gates_g = sb("gates_g", [P, GB, NE, R])
        gexp = sb("gexp", [P, N])
        mixed = sb("mixed", [P, N])
        conv = sb("conv", [P, NT, N])
        spa = sb("spa", [P, NT, N])
        spr = sb("spr", [P, NT, N])
        xi = sb("xi", [P, 2, NT, N])
        zs = sb("zs", [P, 2, NT, N])
        delta = sb("delta", [P, 2, NT, N])
        u = sb("u", [P, 2, NT, N])
        bc_parts = sb("bc_parts", [96, 2, N], BF16)
        bc_mid = sb("bc_mid", [96, N], BF16)
        bc_rest = sb("bc_rest", [96, N])
        b_sb = sb("b_sb", [P, 2, 2, N])
        decay = W["decay"]
        dbx = sb("dbx", [P, RING, 2, N])
        h = sb("h", [P, 2, 2, N])
        ch_sb = sb("ch_sb", [P, RING, 2, N])
        pair_sum = sb("pair_sum", [P, 2, N])
        yd = sb("yd", [P, NT, N])
        attn = sb("attn", [P, N])

        copied = sem("gates_copied")
        a_mm = sem("lora_a_mm")
        gexp_mm = sem("gexp_mm")
        gexp_done = sem("gexp_done")
        mixed_done = sem("mixed_done")
        x_mm = sem("in_proj_x_mm")
        z_mm = sem("in_proj_z_mm")
        conv0 = sem("conv_first_tap")
        zs_done = sem("z_silu")
        conv_done = sem("conv_done")
        xi_done = sem("xi_done")
        bc_mm = sem("bc_mm")
        delta_mm = sem("delta_mm2")
        parts_done = sem("bc_parts_done")
        sp_act = sem("softplus_act")
        sp_max = sem("softplus_max")
        u_done = sem("u_done")
        b_cast = sem("b_broadcast")
        c_cast = sem("c_broadcast")
        b_copied = sem("b_copied")
        decays = sem("decays")
        dbx_done = sem("dbx_done")
        scans = sem("scans")
        weighted = sem("weighted")
        paired = sem("paired")
        reduced = sem("reduced")
        y_read = sem("y_read")
        gated = sem("y_gated")
        out_mm = sem("out_mm")
        attn_done = sem("attn_done")
        chain_f = sem("front_chain_v")

        NP2 = NS // 2
        UNITS = NP2 * NT
        PAIRED = UNITS // RING

        def in_pair_sum(unit):
            return unit % RING == RING - 1

        block = own.enter_context(nc.Block())

        @block.tensor
        def _(pe):
            def front_mix(g):
                pe.wait_ge(attn_done, g + 1)
                nc.tensor.matmul(ps_w[:, 0, :], W["lora_a"][:, :], xt[:, bass.ds(g * N, N)],
                                 start=True, stop=True).then_inc(a_mm, 1)
                pe.wait_ge(copied, g + 1)
                for b in range(GB):
                    last = nc.tensor.transpose(ps_w[:, 1, b * S:(b + 1) * S],
                                               gates_g[:, b, :, :].rearrange("p e r -> p (e r)"), W["ident"][:, :])
                last.then_inc(gexp_mm, 1)

            def front_x(g):
                pe.wait_ge(mixed_done, g + 1)
                for j in range(NT):
                    last = nc.tensor.matmul(ps_w[:, j, :], W["w_ab"][:, j * P:(j + 1) * P], mixed[:, :],
                                            start=True, stop=True)
                last.then_inc(x_mm, 1)

            def front_z(g):
                pe.wait_ge(conv_done, g + 1)
                for j in range(NT):
                    last = nc.tensor.matmul(ps_w[:, j, :], W["w_ab"][:, (NT + j) * P:(NT + j + 1) * P], mixed[:, :],
                                            start=True, stop=True)
                last.then_inc(z_mm, 1)

            def front_bc(g, at):
                pe.wait_ge(zs_done, g + 1)
                pe.wait_ge(xi_done, g + 1)
                for kt in range(NT):
                    last = nc.tensor.matmul(ps_w[0:96, 0, :], W["w_bc"][:, kt, :], xi[:, at, kt, :],
                                            start=(kt == 0), stop=(kt == NT - 1))
                last.then_inc(bc_mm, 1)

            def front_delta(g, at):
                for jt in (1, 0):
                    if jt == 0:
                        pe.wait_ge(parts_done, g + 1)
                    for kt in range(NT):
                        last = nc.tensor.matmul(ps_w[:, jt, :], W["w_delta"][:, kt, jt * P:(jt + 1) * P],
                                                xi[:, at, kt, :], start=(kt == 0), stop=(kt == NT - 1))
                last.then_inc(delta_mm, 1)

            def front(g, at):
                front_mix(g)
                front_x(g)
                front_z(g)
                front_bc(g, at)
                front_delta(g, at)

            def cast(sem_done, to, first, g, at):
                for n in range(2):
                    last = nc.tensor.matmul(to[:, n, :], W["pick"][:, first + n:first + n + 1].to_broadcast([96, P]),
                                            bc_parts[:, at, :], start=True, stop=True)
                last.then_inc(sem_done, 1)

            def reduce(g, unit):
                if in_pair_sum(unit):
                    pe.wait_ge(paired, g * PAIRED + unit // RING + 1)
                    terms = [pair_sum[:, unit // RING % 2, :]]
                else:
                    pe.wait_ge(weighted, g * UNITS + unit + 2)
                    terms = [ch_sb[:, unit % RING, n, :] for n in range(2)]
                for n, term in enumerate(terms):
                    last = nc.tensor.matmul(ps_y[:, unit % NT, :], W["ident"][:, :], term,
                                            start=(unit < NT and n == 0),
                                            stop=(unit >= UNITS - NT and n == len(terms) - 1))
                last.then_inc(reduced, 1)

            def project(g):
                pe.wait_ge(gated, g + 1)
                for kt in range(NT):
                    last = nc.tensor.matmul(ps_w[:, 0, :], W["out_w"][:, kt, :], yd[:, kt, :],
                                            start=(kt == 0), stop=(kt == NT - 1))
                last.then_inc(out_mm, 1)

            def scan(g, at, ahead):
                pe.wait_ge(b_copied, g * NP2 + 1)
                cast(b_cast, ps_b, 0, g, at)
                for pair in range(NP2):
                    pe.wait_ge(weighted, g * UNITS + NT * pair + 1)
                    cast(c_cast, ps_c, NS + 2 * pair, g, at)
                    if pair + 1 < NP2:
                        pe.wait_ge(b_copied, g * NP2 + pair + 2)
                        cast(b_cast, ps_b, 2 * pair + 2, g, at)
                    if pair >= 1:
                        for tile in range(NT):
                            reduce(g, (pair - 1) * NT + tile)
                    if ahead is None:
                        continue
                    if pair == 0:
                        front_mix(ahead)
                    if pair == 1:
                        front_x(ahead)
                    if pair == 3:
                        front_z(ahead)
                    if pair == 5:
                        front_bc(ahead, 1 - at)
                    if pair == 6:
                        front_delta(ahead, 1 - at)
                for tile in range(NT):
                    reduce(g, (NP2 - 1) * NT + tile)
                project(g)

            pe.sem_inc(attn_done, 2)
            pe.sem_inc(gexp_mm, 1)
            pe.sem_inc(b_copied, 1)
            pe.sem_inc(weighted, 1)
            pe.sem_inc(scans, RING)
            pe.sem_inc(reduced, RING)
            pe.sem_inc(dbx_done, NT + 1)
            in_pairs(pe, front, scan)

        @block.scalar
        def _(act):
            def front_gates(g):
                act.wait_ge(gexp_mm, g + 2)
                nc.scalar.copy(gexp[:, :], ps_w[:, 1, :]).then_inc(gexp_done, 1)

            def front_conv(g):
                act.wait_ge(x_mm, g + 1)
                for tile in range(NT):
                    last = nc.scalar.activation(conv[:, tile, :], ps_w[:, tile, :], ACT.Identity,
                                                bias=W["conv_b"][:, tile:tile + 1], scale=W["conv_w"][:, tile, 3:4])
                last.then_inc(conv0, 1)

            def front_silu(g, at):
                act.wait_ge(z_mm, g + 1)
                nc.scalar.activation(zs[:, at, :, :], ps_w[:, :, :], ACT.Silu).then_inc(zs_done, 1)
                act.wait_ge(conv_done, g + 1)
                nc.scalar.activation(xi[:, at, :, :], conv[:, :, :], ACT.Silu).then_inc(xi_done, 1)

            def front_softplus(g):
                act.wait_ge(delta_mm, g + 1)
                for tile in range(NT):
                    last = nc.scalar.activation(spa[:, tile, :], ps_w[:, tile, :], ACT.Abs,
                                                bias=W["dt_b"][:, tile:tile + 1])
                last.then_inc(sp_act, 1)
                for tile in range(NT):
                    last = nc.scalar.activation(spr[:, tile, :], ps_w[:, tile, :], ACT.Relu,
                                                bias=W["dt_b"][:, tile:tile + 1])
                last.then_inc(sp_max, 1)
                act.wait_ge(sp_act, 3 * g + 1)
                nc.scalar.activation(spa[:, :, :], spa[:, :, :], ACT.Exp, scale=-1.0).then_inc(sp_act, 1)
                act.wait_ge(sp_act, 3 * g + 2)
                nc.scalar.activation(spa[:, :, :], spa[:, :, :], ACT.Ln, bias=1.0).then_inc(sp_act, 1)

            def front(g, at):
                front_gates(g)
                front_conv(g)
                front_silu(g, at)
                front_softplus(g)

            def scan(g, at, ahead):
                act.wait_ge(u_done, g + 1)
                for pair in range(NP2):
                    act.wait_ge(b_cast, g * NP2 + pair + 1)
                    act.wait_ge(dbx_done, g * UNITS + NT * pair + 1)
                    nc.scalar.copy(b_sb[:, pair % 2, :, :], ps_b[:, :, :]).then_inc(b_copied, 1)
                    for tile in range(NT):
                        unit = pair * NT + tile
                        act.wait_ge(scans, g * UNITS + unit + 1)
                        for n in range(2):
                            last = nc.scalar.activation(
                                decay[:, unit % RING, n, :, 1:S], by_group(delta[:, at, tile, :])[:, :, 1:S], ACT.Exp,
                                scale=W["a"][:, tile, 2 * pair + n:2 * pair + n + 1])
                        last.then_inc(decays, 1)
                    if ahead is None:
                        continue
                    if pair == 0:
                        front_gates(ahead)
                    if pair == 2:
                        front_conv(ahead)
                    if pair == 4:
                        front_silu(ahead, 1 - at)
                if ahead is not None:
                    front_softplus(ahead)

            in_pairs(act, front, scan)

        @block.gpsimd
        def _(pool):
            def front(g, at):
                pool.wait_ge(gexp_mm, g + 1)
                nc.gpsimd.tensor_copy(
                    gates_g[:, :, :, :],
                    W["gates"][:, bass.ds(g * GB, GB), :].unsqueeze(3).to_broadcast([P, GB, NE, R])).then_inc(copied, 1)

            def add_pair(g, unit):
                pool.wait_ge(weighted, g * UNITS + unit + 2)
                pool.wait_ge(reduced, g * UNITS + unit + 1)
                nc.gpsimd.tensor_tensor(pair_sum[:, unit // RING % 2, :], ch_sb[:, unit % RING, 0, :],
                                        ch_sb[:, unit % RING, 1, :], ALU.add).then_inc(paired, 1)

            def scan(g, at, ahead):
                if ahead is not None:
                    front(ahead, 1 - at)
                for unit in range(UNITS):
                    pair, tile = divmod(unit, NT)
                    if tile == 0:
                        pool.wait_ge(b_copied, g * NP2 + pair + 2)
                    pool.wait_ge(scans, g * UNITS + unit + 1)
                    nc.gpsimd.tensor_tensor(dbx[:, unit % RING, :, :], b_sb[:, pair % 2, :, :],
                                            u[:, at, tile, :].unsqueeze(1).to_broadcast([P, 2, N]),
                                            ALU.mult).then_inc(dbx_done, 1)
                    if unit >= LAG and in_pair_sum(unit - LAG):
                        add_pair(g, unit - LAG)
                for unit in range(UNITS - LAG, UNITS):
                    if in_pair_sum(unit):
                        add_pair(g, unit)

            in_pairs(pool, front, scan)

        @block.vector
        def _(dve):
            FRONT_LINKS = 7

            def front_mix(g):
                dve.wait_ge(a_mm, g + 1)
                dve.wait_ge(gexp_done, g + 1)
                nc.vector.tensor_tensor(mixed[:, :], ps_w[:, 0, :], gexp[:, :], ALU.mult).then_inc(mixed_done, 1)

            def front_conv(g, ch):
                dve.wait_ge(conv0, g + 1)
                for k in (2, 1, 0):
                    lag = 3 - k
                    for tile in range(NT):
                        to = by_group(conv[:, tile, :])[:, :, lag:S]
                        ins = nc.vector.scalar_tensor_tensor(
                            out=to, in0=by_group(ps_w[:, tile, :])[:, :, 0:S - lag],
                            scalar=W["conv_w"][:, tile, k:k + 1], in1=to, op0=ALU.mult, op1=ALU.add)
                        if tile < NT - 1:
                            continue
                        if k:
                            ch.link(ins)
                        else:
                            ins.then_inc(conv_done, 1)

            def front_parts(g, at, ch):
                dve.wait_ge(bc_mm, g + 1)
                split3(nc, ch, bc_parts[:, at, :], bc_mid, bc_rest, ps_w[0:96, 0, :]).then_inc(parts_done, 1)

            def front_u(g, at, ch):
                dve.wait_ge(sp_max, g + 1)
                dve.wait_ge(sp_act, 3 * g + 3)
                ch.link(nc.vector.tensor_tensor(delta[:, at, :, :], spr[:, :, :], spa[:, :, :], ALU.add))
                dve.wait_ge(xi_done, g + 1)
                nc.vector.tensor_tensor(u[:, at, :, :], delta[:, at, :, :], xi[:, at, :, :], ALU.mult).then_inc(u_done, 1)
                ch.end()

            def front(g, at):
                ch = Chain(dve, chain_f, g, FRONT_LINKS)
                front_mix(g)
                front_conv(g, ch)
                front_parts(g, at, ch)
                front_u(g, at, ch)

            def scan(g, at, ahead):
                if ahead is not None:
                    ch = Chain(dve, chain_f, ahead, FRONT_LINKS)
                for unit in range(UNITS):
                    pair, tile = divmod(unit, NT)
                    dve.wait_ge(decays, g * UNITS + unit + 1)
                    dve.wait_ge(dbx_done, g * UNITS + unit + NT + 2)
                    nc.vector.tensor_tensor_scan(
                        h[:, unit % 2, :, :].rearrange("p n t -> p (n t)"),
                        decay[:, unit % RING, :, :, :].rearrange("p n b t -> p (n b t)"),
                        dbx[:, unit % RING, :, :].rearrange("p n t -> p (n t)"), 0.0, ALU.mult,
                        ALU.add).then_inc(scans, 1)
                    dve.wait_ge(scans, g * UNITS + unit + RING + 1)
                    if tile == 0:
                        dve.wait_ge(c_cast, g * NP2 + pair + 1)
                    dve.wait_ge(reduced, g * UNITS + unit + 1)
                    nc.vector.tensor_tensor(ch_sb[:, unit % RING, :, :], h[:, unit % 2, :, :], ps_c[:, :, :],
                                            ALU.mult).then_inc(weighted, 1)
                    if ahead is None:
                        continue
                    if unit == 3:
                        front_mix(ahead)
                    if unit == 6:
                        front_conv(ahead, ch)
                    if unit == 11:
                        front_parts(ahead, 1 - at, ch)
                if ahead is not None:
                    front_u(ahead, 1 - at, ch)
                dve.wait_ge(reduced, g * UNITS + UNITS + RING)
                for tile in range(NT):
                    last = nc.vector.scalar_tensor_tensor(out=yd[:, tile, :], in0=xi[:, at, tile, :],
                                                          scalar=W["d_skip"][:, tile:tile + 1], in1=ps_y[:, tile, :],
                                                          op0=ALU.mult, op1=ALU.add)
                last.then_inc(y_read, 1)
                dve.wait_ge(y_read, g + 1)
                nc.vector.tensor_tensor(yd[:, :, :], yd[:, :, :], zs[:, at, :, :], ALU.mult).then_inc(gated, 1)
                dve.wait_ge(out_mm, g + 1)
                nc.vector.tensor_copy(attn[:, :], ps_w[:, 0, :]).then_inc(attn_done, 1)
                dve.wait_ge(attn_done, g + 3)
                xg = xt[:, bass.ds(g * N, N)]
                nc.vector.tensor_tensor(xg, xg, attn[:, :], ALU.add)

            in_pairs(dve, front, scan)


def setup_ffn0(nc, D, W):
    with ExitStack() as own:
        def tmp(name, shape, dt=F32):
            return own.enter_context(nc.sbuf_tensor(name, shape, dt))

        def sem(name):
            return own.enter_context(nc.semaphore(name))

        taus = tmp("taus", [P, ND + 2])
        tau_abs = tmp("tau_abs", [P, ND + 2])
        tau_max = tmp("tau_max", [P, ND + 2])
        soft = tmp("soft", [P, ND + 2])
        rate = tmp("rate", [P, ND + 2])
        blend_t = tmp("blend_t", [P, ND])
        blend4 = tmp("blend4", [P, 4, ND])
        top = tmp("blend_top", [P, 1])
        pow_at = tmp("pow_at", [P, LAGS])
        lag_pow = tmp("lag_pow", [P, LAGS])
        upto_at = tmp("upto_at", [P, CHUNKS])
        upto_on = tmp("upto_on", [P, CHUNKS])
        from_at = tmp("from_at", [P, 4, S])
        from_on = tmp("from_on", [P, 4, S])
        ctx_at = tmp("ctx_at", [P, S])
        ctx_on = tmp("ctx_on", [P, S])
        ps_bw = own.enter_context(nc.psum_tensor("ps_bw", [P, C], F32))

        loaded = sem("s2_loaded")
        a_abs = sem("s2_abs")
        a_exp = sem("s2_exp")
        a_ln = sem("s2_ln")
        rate_done = sem("s2_rate")
        shifted = sem("s2_blend_shifted")
        b_exp = sem("s2_blend_exp")
        b_done = sem("s2_blend_done")
        bw_mm = sem("s2_bw_mm")
        bw_copied = sem("s2_bw_copied")
        upto_arg = sem("s2_upto_arg")
        exps = sem("s2_exps")
        chain_v = sem("s2_chain_v")

        loads = [
            (taus[:, 0:ND], D["condB_tauraws"].to_broadcast([P, ND])),
            (taus[:, ND:ND + 1], D["tau_column"]),
            (taus[:, ND + 1:ND + 2], D["L0_cond2_tau_ctx"].to_broadcast([P, 1])),
            (blend_t[:, :], D["cond_1024"]), (pow_at[:, :], D["c_lag"].to_broadcast([P, LAGS])),
            (upto_at[:, :], D["c_upto_at"]), (upto_on[:, :], D["c_upto_on"]),
            (from_at[:, :, :], D["c_from_at"]), (from_on[:, :, :], D["c_from_on"]),
            (ctx_at[:, :], D["c_ctx_at"]), (ctx_on[:, :], D["c_ctx_on"]),
            (W["shift"][:, :, :], D["c_shift"]),
            (W["wg_x"][:, :], D["wg_x"]), (W["wg_ctx"][:, :], D["wg_ctx"]), (W["bg"][:, :], D["L0_cond2_bg"]),
            (W["wn1"][:, :], D["L0_cond2_Wn1"]), (W["bn1"][:, :], D["L0_cond2_bn1"]),
            (W["wn2"][:, :], D["cond_256"]), (W["bn2"][:, :], D["condB_bn2"]),
            (W["w_soma"][:, :], D["L0_cond2_Wsoma"]), (W["b_soma"][:, :], D["L0_cond2_bsoma"]),
            (W["w_temp"][:, :], D["L0_cond2_Wtemp"]), (W["b_temp"][:, :], D["L0_cond2_btemp"]),
            (W["w_out"][:, :], D["L0_cond2_Wout"]),
            (W["gamma"][:, :], D["L0_cond2_gamma"]), (W["beta"][:, :], D["L0_cond2_beta"]),
            (W["router"][:, :], D["L0_ffn_router_w"]),
            (W["router_b"][:, :], D["L0_ffn_router_b"].to_broadcast([P, NE])),
            (W["expert_w"][:, :, :], D["L0_ffn_expert_w"]), (W["expert_b"][:, :], D["L0_ffn_expert_b"]),
            (W["rank"][:, :], D["c_rank"].to_broadcast([P, NE])), (W["pick8"][:, :], D["c_pick"]),
        ]
        block = own.enter_context(nc.Block())

        @block.sync
        def _(sp):
            for dst, src in loads:
                sp.dma_start(dst, src).then_inc(loaded, 16)

        @block.scalar
        def _(act):
            act.wait_ge(loaded, 16 * len(loads))
            nc.scalar.activation(tau_abs[:, :], taus[:, :], ACT.Abs).then_inc(a_abs, 1)
            nc.scalar.activation(tau_max[:, :], taus[:, :], ACT.Relu).then_inc(a_abs, 1)
            act.wait_ge(a_abs, 1)
            nc.scalar.activation(soft[:, :], tau_abs[:, :], ACT.Exp, scale=-1.0).then_inc(a_exp, 1)
            act.wait_ge(a_exp, 1)
            nc.scalar.activation(soft[:, :], soft[:, :], ACT.Ln, bias=1.0).then_inc(a_ln, 1)
            act.wait_ge(shifted, 1)
            nc.scalar.activation(blend_t[:, :], blend_t[:, :], ACT.Exp).then_inc(b_exp, 1)
            act.wait_ge(rate_done, 1)
            nc.scalar.activation(lag_pow[:, :], pow_at[:, :], ACT.Exp, scale=rate[:, ND:ND + 1]).then_inc(exps, 1)
            nc.scalar.activation(W["from_start"][:, :, :], from_at[:, :, :], ACT.Exp,
                                 scale=rate[:, ND:ND + 1]).then_inc(exps, 1)
            nc.scalar.activation(W["k_ctx"][:, :], ctx_at[:, :], ACT.Exp,
                                 scale=rate[:, ND + 1:ND + 2]).then_inc(exps, 1)
            act.wait_ge(upto_arg, 1)
            nc.scalar.activation(W["upto_end"][:, :, :], W["upto_end"][:, :, :], ACT.Exp).then_inc(exps, 1)

        @block.tensor
        def _(pe):
            pe.wait_ge(b_done, 1)
            nc.tensor.matmul(ps_bw[:, :], blend4[:, :, :].rearrange("p k d -> p (k d)"), W["ident"][:, :],
                             start=True, stop=True).then_inc(bw_mm, 1)

        @block.gpsimd
        def _(pool):
            nc.gpsimd.memset(W["ones"][:, :], 1.0)
            nc.gpsimd.memset(W["mw96"][:, :, :, :], 0.0)
            nc.gpsimd.memset(W["neg_half"][:, :], -0.5)

        @block.vector
        def _(dve):
            ch = Chain(dve, chain_v, 0, 5)
            dve.wait_ge(loaded, 16 * len(loads))
            ch.link(nc.vector.tensor_reduce(top[:, :], blend_t[:, :], X, ALU.max))
            nc.vector.tensor_scalar(blend_t[:, :], blend_t[:, :], top[:, 0:1], None, ALU.subtract).then_inc(shifted, 1)
            dve.wait_ge(a_abs, 2)
            dve.wait_ge(a_ln, 1)
            nc.vector.scalar_tensor_tensor(out=rate[:, :], in0=tau_max[:, :], scalar=-1.0, in1=soft[:, :],
                                           op0=ALU.mult, op1=ALU.subtract).then_inc(rate_done, 1)
            dve.wait_ge(rate_done, 1)
            nc.vector.tensor_tensor(W["upto_end"][:, :, :], upto_at[:, :].unsqueeze(2).to_broadcast([P, CHUNKS, ND]),
                                    rate[:, 0:ND].unsqueeze(1).to_broadcast([P, CHUNKS, ND]),
                                    ALU.mult).then_inc(upto_arg, 1)
            dve.wait_ge(b_exp, 1)
            ch.link(nc.vector.tensor_reduce(top[:, :], blend_t[:, :], X, ALU.add))
            ch.link(nc.vector.reciprocal(top[:, :], top[:, :]))
            ch.link(nc.vector.tensor_scalar(blend_t[:, :], blend_t[:, :], top[:, 0:1], None, ALU.mult))
            nc.vector.tensor_copy(blend4[:, :, :], blend_t[:, :].unsqueeze(1).to_broadcast([P, 4, ND])).then_inc(b_done, 1)
            dve.wait_ge(bw_mm, 1)
            nc.vector.tensor_copy(W["bw"][:, :], ps_bw[:, :]).then_inc(bw_copied, 1)
            dve.wait_ge(exps, 4)
            dve.wait_ge(bw_copied, 1)
            ch.link(nc.vector.tensor_tensor(
                W["bw_lag"][:, :, :], W["bw"][0:ND, :].unsqueeze(1).to_broadcast([ND, LAGS, C]),
                lag_pow[0:ND, :].unsqueeze(2).to_broadcast([ND, LAGS, C]), ALU.mult))
            nc.vector.tensor_tensor(W["from_start"][:, :, :], W["from_start"][:, :, :], from_on[:, :, :], ALU.mult)
            nc.vector.tensor_tensor(W["k_ctx"][:, :], W["k_ctx"][:, :], ctx_on[:, :], ALU.mult)
            nc.vector.tensor_tensor(W["upto_end"][:, :, :], W["upto_end"][:, :, :],
                                    upto_on[:, :].unsqueeze(2).to_broadcast([P, CHUNKS, ND]), ALU.mult)
            ch.end()


def split3(nc, ch, parts, mid, rest, src):
    ch.link(nc.vector.tensor_copy(parts[:, :], src))
    ch.link(nc.vector.tensor_tensor(rest[:, :], src, parts[:, :], ALU.subtract))
    ch.link(nc.vector.tensor_copy(mid[:, :], rest[:, :]))
    ch.link(nc.vector.tensor_copy(parts[32:64, :], mid[32:64, :]))
    return nc.vector.tensor_tensor(parts[64:96, :], rest[64:96, :], mid[64:96, :], ALU.subtract)


def traces_and_experts(nc, W, xt):
    with ExitStack() as own:
        def sb(name, shape, dt=F32):
            return own.enter_context(nc.sbuf_tensor(name, shape, dt))

        def sem(name):
            return own.enter_context(nc.semaphore(name))

        ps = own.enter_context(nc.psum_tensor("ps2", [P, 8, N], F32))
        x1 = sb("x1", [P, N])
        xs = sb("xs", [P, GB, C])
        h1 = sb("h1", [32, N])
        soma = sb("soma", [P, N])
        ctx_t = sb("ctx_t", [P, N])
        mod_t = sb("mod_t", [ND, N])
        mod_s = sb("mod_s", [P, GB, ND])
        wg = sb("wg", [P, N])
        gated = sb("gated", [P, GB, C])
        upto = sb("upto", [P, 2, CHUNKS, ND])
        states = sb("states", [P, 2, 4, C])
        lagged = sb("lagged", [P, 2, LAGS, C])
        temp_t = sb("temp_t", [P, N])
        gate = sb("gate", [P, N])
        prod = sb("prod", [P, N])
        mean = sb("mean", [P, GB])
        var = sb("var", [P, GB])
        rstd = sb("rstd", [P, GB])
        xc = sb("xc", [P, GB, C])
        sq = sb("sq", [P, GB, C])
        xn = sb("xn", [P, GB, C])
        yt = sb("yt", [P, N])
        lg = sb("lg", [P, GB, NE])
        ex = sb("ex", [P, GB, NE])
        hot = sb("hot", [P, GB, NE])
        top = sb("top2", [P, GB])
        den = sb("den", [P, GB])
        first = sb("first", [P, GB])
        m_parts = sb("m_parts", [96, N], BF16)
        m_mid = sb("m_mid", [96, N], BF16)
        m_rest = sb("m_rest", [96, N])
        mw_t = sb("mw_t", [NE, N])
        ym = sb("ym", [P, 2, N])

        names = ("x1_copied xs_mm xs_copied h1_mm h1_done soma_mm soma_done ctx_mm ctx_copied mod_mm sig_done "
                 "mod_done wg_mm wg_done gated_done mods_mm mods_done upto_done states_mm lags_mm states_done "
                 "lagged_done temp_mm temp_copied gate_mm gate_done prod_done out_mm centred squared var_done "
                 "rstd_done xn_done xn_mm yt_done router_mm shifted_r exped_r mw_done mw_copied mw_mm m_split "
                 "mask_mm masked experts_mm x2_done chain_v2").split()
        Z = {n: sem("p2_" + n) for n in names}
        block = own.enter_context(nc.Block())

        @block.tensor
        def _(pe):
            with pe.Fori(0, NG) as g:
                pe.wait_ge(Z["x1_copied"], g + 1)
                for b in range(GB):
                    last = nc.tensor.transpose(ps[:, 0, b * S:(b + 1) * S], x1[:, b * S:(b + 1) * S], W["ident"][:, :])
                last.then_inc(Z["xs_mm"], 1)
                nc.tensor.matmul(ps[0:32, 1, :], W["wn1"][:, :], x1[:, :], start=True, stop=True).then_inc(Z["h1_mm"], 1)
                nc.tensor.matmul(ps[:, 2, :], W["w_soma"][:, :], x1[:, :], start=True, stop=True).then_inc(Z["soma_mm"], 1)
                pe.wait_ge(Z["xs_copied"], g + 1)
                pe.wait_ge(Z["h1_done"], g + 1)
                for b in range(GB):
                    last = nc.tensor.matmul(ps[:, 3, b * S:(b + 1) * S], xs[:, b, :], W["k_ctx"][:, :],
                                            start=True, stop=True)
                last.then_inc(Z["ctx_mm"], 1)
                nc.tensor.matmul(ps[0:ND, 1, :], W["wn2"][:, :], h1[:, :], start=True, stop=True).then_inc(Z["mod_mm"], 1)
                pe.wait_ge(Z["ctx_copied"], g + 1)
                for b in range(GB):
                    to, part = ps[:, 0, b * S:(b + 1) * S], slice(b * S, (b + 1) * S)
                    nc.tensor.matmul(to, x1[:, part], W["wg_x"][:, :], start=True, stop=False)
                    nc.tensor.matmul(to, ctx_t[:, part], W["wg_ctx"][:, :], start=False, stop=False)
                    last = nc.tensor.matmul(to, W["ones"][0:1, :], W["bg"][:, :], start=False, stop=True)
                last.then_inc(Z["wg_mm"], 1)
                pe.wait_ge(Z["mod_done"], g + 1)
                for b in range(GB):
                    last = nc.tensor.matmul(ps[:, 1, b * ND:(b + 1) * ND], mod_t[:, b * S:(b + 1) * S],
                                            W["ident"][0:ND, 0:ND], start=True, stop=True)
                last.then_inc(Z["mods_mm"], 1)
                pe.wait_ge(Z["gated_done"], g + 1)
                pe.wait_ge(Z["soma_done"], g + 1)

                def spread(b):
                    if b >= 1:
                        pe.wait_ge(Z["lagged_done"], g * GB + b)
                    for half in range(2):
                        last = nc.tensor.matmul(
                            ps[:, 2 + half, :], mod_t[:, b * S:(b + 1) * S],
                            W["bw_lag"][:, 4 * half:4 * half + 4, :].rearrange("d l c -> d (l c)"),
                            start=True, stop=True)
                    last.then_inc(Z["lags_mm"], 1)
                    pe.wait_ge(Z["upto_done"], g * GB + b + 1)
                    if b >= 2:
                        pe.wait_ge(Z["states_done"], g * GB + b - 1)
                    for j in range(4):
                        last = nc.tensor.matmul(
                            ps[:, 4 + b % 2, j * C:(j + 1) * C],
                            upto[:, b % 2, 4 * j:4 * j + 4, :].rearrange("s k d -> s (k d)"), gated[:, b, :],
                            start=True, stop=True)
                    last.then_inc(Z["states_mm"], 1)

                def gather(b):
                    to = ps[:, 6, b * S:(b + 1) * S]
                    pe.wait_ge(Z["states_done"], g * GB + b + 1)
                    for j in range(4):
                        nc.tensor.matmul(to, states[:, b % 2, j, :], W["from_start"][:, j, :],
                                         start=(j == 0), stop=False)
                    pe.wait_ge(Z["lagged_done"], g * GB + b + 1)
                    for lag in range(LAGS):
                        last = nc.tensor.matmul(to, lagged[:, b % 2, lag, :], W["shift"][:, lag, :],
                                                start=False, stop=(lag == LAGS - 1))
                    last.then_inc(Z["temp_mm"], 1)

                spread(0)
                for b in range(1, GB):
                    spread(b)
                    gather(b - 1)
                gather(GB - 1)
                pe.wait_ge(Z["temp_copied"], g + 1)
                nc.tensor.matmul(ps[:, 7, :], W["w_temp"][:, :], temp_t[:, :], start=True, stop=True).then_inc(Z["gate_mm"], 1)
                pe.wait_ge(Z["prod_done"], g + 1)
                for b in range(GB):
                    last = nc.tensor.matmul(ps[:, 0, b * C:(b + 1) * C], prod[:, b * S:(b + 1) * S], W["w_out"][:, :],
                                            start=True, stop=True)
                last.then_inc(Z["out_mm"], 1)
                pe.wait_ge(Z["xn_done"], g + 1)
                for b in range(GB):
                    last = nc.tensor.transpose(ps[:, 1, b * S:(b + 1) * S], xn[:, b, :], W["ident"][:, :])
                last.then_inc(Z["xn_mm"], 1)
                pe.wait_ge(Z["yt_done"], g + 1)
                for b in range(GB):
                    last = nc.tensor.matmul(ps[:, 2, b * NE:(b + 1) * NE], yt[:, b * S:(b + 1) * S], W["router"][:, :],
                                            start=True, stop=True)
                last.then_inc(Z["router_mm"], 1)
                pe.wait_ge(Z["mw_copied"], g + 1)
                for b in range(GB):
                    last = nc.tensor.matmul(ps[0:96, 3, b * S:(b + 1) * S],
                                            W["mw96"][:, b, :, :].rearrange("p k e -> p (k e)"), W["ident"][:, :],
                                            start=True, stop=True)
                last.then_inc(Z["mw_mm"], 1)
                pe.wait_ge(Z["m_split"], g + 1)

                def mask(e):
                    if e >= 2:
                        pe.wait_ge(Z["masked"], g * NE + e - 1)
                    nc.tensor.matmul(ps[:, 4 + e % 2, :], W["pick8"][:, e:e + 1].to_broadcast([96, P]), m_parts[:, :],
                                     start=True, stop=True).then_inc(Z["mask_mm"], 1)

                mask(0)
                nc.tensor.matmul(ps[:, 6, :], W["expert_b"][:, :], mw_t[:, :], start=True, stop=False)
                for e in range(NE):
                    if e + 1 < NE:
                        mask(e + 1)
                    pe.wait_ge(Z["masked"], g * NE + e + 1)
                    last = nc.tensor.matmul(ps[:, 6, :], W["expert_w"][:, e, :], ym[:, e % 2, :],
                                            start=False, stop=(e == NE - 1))
                last.then_inc(Z["experts_mm"], 1)

        @block.scalar
        def _(act):
            with act.Fori(0, NG) as g:
                act.wait_ge(Z["xs_mm"], g + 1)
                nc.scalar.copy(xs[:, :, :].rearrange("p b c -> p (b c)"), ps[:, 0, :]).then_inc(Z["xs_copied"], 1)
                act.wait_ge(Z["h1_mm"], g + 1)
                nc.scalar.activation(h1[:, :], ps[0:32, 1, :], ACT.Gelu, bias=W["bn1"][:, 0:1]).then_inc(Z["h1_done"], 1)
                act.wait_ge(Z["soma_mm"], g + 1)
                nc.scalar.activation(soma[:, :], ps[:, 2, :], ACT.Gelu, bias=W["b_soma"][:, 0:1]).then_inc(Z["soma_done"], 1)
                act.wait_ge(Z["mod_mm"], g + 1)
                nc.scalar.activation(mod_t[:, :], ps[0:ND, 1, :], ACT.Sigmoid, bias=W["bn2"][:, 0:1]).then_inc(Z["sig_done"], 1)
                act.wait_ge(Z["wg_mm"], g + 1)
                nc.scalar.activation(wg[:, :], ps[:, 0, :], ACT.Sigmoid).then_inc(Z["wg_done"], 1)
                act.wait_ge(Z["temp_mm"], GB * g + GB)
                nc.scalar.copy(temp_t[:, :], ps[:, 6, :]).then_inc(Z["temp_copied"], 1)
                act.wait_ge(Z["gate_mm"], g + 1)
                nc.scalar.activation(gate[:, :], ps[:, 7, :], ACT.Sigmoid, bias=W["b_temp"][:, 0:1]).then_inc(Z["gate_done"], 1)
                act.wait_ge(Z["centred"], g + 1)
                nc.scalar.activation(sq[:, :, :], xc[:, :, :], ACT.Square).then_inc(Z["squared"], 1)
                act.wait_ge(Z["xn_mm"], g + 1)
                nc.scalar.activation(yt[:, :], ps[:, 1, :], ACT.Identity, bias=W["beta"][:, 0:1],
                                     scale=W["gamma"][:, 0:1]).then_inc(Z["yt_done"], 1)
                act.wait_ge(Z["shifted_r"], g + 1)
                nc.scalar.activation(ex[:, :, :], ex[:, :, :], ACT.Exp).then_inc(Z["exped_r"], 1)
                act.wait_ge(Z["mw_done"], g + 1)
                nc.scalar.copy(W["mw96"][:, :, :, 0:NE],
                               hot[:, :, :].unsqueeze(2).to_broadcast([P, GB, 3, NE])).then_inc(Z["mw_copied"], 1)

        @block.gpsimd
        def _(pool):
            pool.sem_inc(Z["x2_done"], 1)
            with pool.Fori(0, NG) as g:
                pool.wait_ge(Z["x2_done"], g + 1)
                nc.gpsimd.tensor_copy(x1[:, :], xt[:, bass.ds(g * N, N)]).then_inc(Z["x1_copied"], 1)
                pool.wait_ge(Z["mods_done"], g + 1)
                for b in range(GB):
                    if b >= 2:
                        pool.wait_ge(Z["states_mm"], g * GB + b - 1)
                    nc.gpsimd.tensor_tensor(upto[:, b % 2, :, :], W["upto_end"][:, :, :],
                                            mod_s[:, b, :].unsqueeze(1).to_broadcast([P, CHUNKS, ND]),
                                            ALU.mult).then_inc(Z["upto_done"], 1)
                pool.wait_ge(Z["var_done"], g + 1)
                nc.gpsimd.tensor_tensor(rstd[:, :], var[:, :], W["neg_half"][:, :], ALU.pow).then_inc(Z["rstd_done"], 1)

        @block.vector
        def _(dve):
            with dve.Fori(0, NG) as g:
                ch = Chain(dve, Z["chain_v2"], g, 15)
                dve.wait_ge(Z["ctx_mm"], g + 1)
                nc.vector.tensor_copy(ctx_t[:, :], ps[:, 3, :]).then_inc(Z["ctx_copied"], 1)
                dve.wait_ge(Z["sig_done"], g + 1)
                nc.vector.tensor_scalar(mod_t[:, :], mod_t[:, :], 0.5, None, ALU.add).then_inc(Z["mod_done"], 1)
                dve.wait_ge(Z["wg_done"], g + 1)
                nc.vector.tensor_tensor(gated[:, :, :], xs[:, :, :], wg[:, :].rearrange("p (b c) -> p b c", b=GB),
                                        ALU.mult).then_inc(Z["gated_done"], 1)
                dve.wait_ge(Z["mods_mm"], g + 1)
                nc.vector.tensor_copy(mod_s[:, :, :], ps[:, 1, 0:GB * ND].rearrange("p (b d) -> p b d", b=GB)
                                      ).then_inc(Z["mods_done"], 1)
                dve.wait_ge(Z["gated_done"], g + 1)
                for b in range(GB):
                    dve.wait_ge(Z["lags_mm"], g * GB + b + 1)
                    if b >= 2:
                        dve.wait_ge(Z["temp_mm"], g * GB + b - 1)
                    nc.vector.tensor_tensor(
                        lagged[:, b % 2, :, :], ps[:, 2:4, :].rearrange("p h (l c) -> p (h l) c", c=C),
                        gated[:, b, :].unsqueeze(1).to_broadcast([P, LAGS, C]), ALU.mult).then_inc(Z["lagged_done"], 1)
                    dve.wait_ge(Z["states_mm"], g * GB + b + 1)
                    nc.vector.tensor_tensor(
                        states[:, b % 2, :, :], ps[:, 4 + b % 2, :].rearrange("p (j c) -> p j c", c=C),
                        W["bw"][:, :].unsqueeze(1).to_broadcast([P, 4, C]), ALU.mult).then_inc(Z["states_done"], 1)
                dve.wait_ge(Z["gate_done"], g + 1)
                nc.vector.tensor_tensor(prod[:, :], soma[:, :], gate[:, :], ALU.mult).then_inc(Z["prod_done"], 1)
                dve.wait_ge(Z["out_mm"], g + 1)
                o = ps[:, 0, :].rearrange("p (b c) -> p b c", b=GB)
                ch.link(nc.vector.tensor_reduce(mean[:, :], o, X, ALU.add))
                ch.link(nc.vector.tensor_scalar(mean[:, :], mean[:, :], 1.0 / C, None, ALU.mult))
                nc.vector.tensor_tensor(xc[:, :, :], o, mean[:, :].unsqueeze(2).to_broadcast([P, GB, C]),
                                        ALU.subtract).then_inc(Z["centred"], 1)
                dve.wait_ge(Z["squared"], g + 1)
                ch.link(nc.vector.tensor_reduce(var[:, :], sq[:, :, :], X, ALU.add))
                nc.vector.tensor_scalar(var[:, :], var[:, :], 1.0 / C, LN_EPS, ALU.mult, ALU.add).then_inc(Z["var_done"], 1)
                dve.wait_ge(Z["rstd_done"], g + 1)
                nc.vector.tensor_tensor(xn[:, :, :], xc[:, :, :], rstd[:, :].unsqueeze(2).to_broadcast([P, GB, C]),
                                        ALU.mult).then_inc(Z["xn_done"], 1)
                dve.wait_ge(Z["router_mm"], g + 1)
                ch.link(nc.vector.tensor_tensor(lg[:, :, :], ps[:, 2, 0:GB * NE].rearrange("p (b e) -> p b e", b=GB),
                                                W["router_b"][:, :].unsqueeze(1).to_broadcast([P, GB, NE]), ALU.add))
                ch.link(nc.vector.tensor_reduce(top[:, :], lg[:, :, :], X, ALU.max))
                top_b = top[:, :].unsqueeze(2).to_broadcast([P, GB, NE])
                nc.vector.tensor_tensor(ex[:, :, :], lg[:, :, :], top_b, ALU.subtract).then_inc(Z["shifted_r"], 1)
                ch.link(nc.vector.tensor_tensor(hot[:, :, :], lg[:, :, :], top_b, ALU.is_equal))
                ch.link(nc.vector.tensor_tensor(hot[:, :, :], hot[:, :, :],
                                                W["rank"][:, :].unsqueeze(1).to_broadcast([P, GB, NE]), ALU.mult))
                ch.link(nc.vector.tensor_reduce(first[:, :], hot[:, :, :], X, ALU.max))
                ch.link(nc.vector.tensor_tensor(hot[:, :, :], hot[:, :, :],
                                                first[:, :].unsqueeze(2).to_broadcast([P, GB, NE]), ALU.is_equal))
                dve.wait_ge(Z["exped_r"], g + 1)
                ch.link(nc.vector.tensor_reduce(den[:, :], ex[:, :, :], X, ALU.add))
                ch.link(nc.vector.reciprocal(den[:, :], den[:, :]))
                nc.vector.tensor_tensor(hot[:, :, :], hot[:, :, :], den[:, :].unsqueeze(2).to_broadcast([P, GB, NE]),
                                        ALU.mult).then_inc(Z["mw_done"], 1)
                dve.wait_ge(Z["mw_mm"], g + 1)
                nc.vector.tensor_copy(mw_t[:, :], ps[0:NE, 3, :])
                split3(nc, ch, m_parts, m_mid, m_rest, ps[0:96, 3, :]).then_inc(Z["m_split"], 1)
                for e in range(NE):
                    dve.wait_ge(Z["mask_mm"], g * NE + e + 1)
                    nc.vector.tensor_tensor(ym[:, e % 2, :], yt[:, :], ps[:, 4 + e % 2, :],
                                            ALU.mult).then_inc(Z["masked"], 1)
                dve.wait_ge(Z["experts_mm"], g + 1)
                nc.vector.tensor_tensor(xt[:, bass.ds(g * N, N)], x1[:, :], ps[:, 6, :], ALU.add).then_inc(Z["x2_done"], 1)
                ch.end()


def setup_attention(nc, D, W):
    with ExitStack() as own:
        def sem(name):
            return own.enter_context(nc.semaphore(name))

        loaded = sem("s3_loaded")
        capped = sem("s3_capped")
        scaled = sem("s3_scaled")
        loads = [
            (W["lap"][:, :], D["c_lap"]), (W["z"][:, 0, :], D["condB_zX"].to_broadcast([P, NB])),
            (W["z"][:, 1, :], D["condB_zY"].to_broadcast([P, NB])), (W["z"][:, 2, :], D["condB_zR"].to_broadcast([P, NB])),
            (W["w_qkv"][:, :], D["L1_attn_in_proj_weight"]), (W["b_qkv"][:, :], D["L1_attn_in_proj_bias"]),
            (W["scale"][:, :], D["L1_attn_logit_scale"]), (W["head"][:, :], D["L1_attn_head_scale"]),
            (W["w_o"][:, :], D["L1_attn_out_w"]), (W["b_o"][:, :], D["L1_attn_out_b"]),
            (W["same_head"][:, :], D["c_same_head"]), (W["head_of"][:, :], D["c_head_of"]),
            (W["quarter_of"][:, :], D["c_quarter_of"]),
            (W["v_block"][:, :], D["c_v_block"]),
        ]
        block = own.enter_context(nc.Block())

        @block.sync
        def _(sp):
            for dst, src in loads:
                sp.dma_start(dst, src).then_inc(loaded, 16)

        @block.vector
        def _(dve):
            dve.wait_ge(loaded, 16 * len(loads))
            nc.vector.tensor_scalar(W["scale"][:, :], W["scale"][:, :], LOGIT_SCALE_MAX, None, ALU.min).then_inc(capped, 1)
            nc.vector.tensor_tensor(W["v_bias"][:, :], W["b_qkv"][:, 2:3], W["head"][:, :], ALU.mult)

        @block.scalar
        def _(act):
            act.wait_ge(capped, 1)
            nc.scalar.activation(W["scale"][:, :], W["scale"][:, :], ACT.Exp).then_inc(scaled, 1)


def diffusion_and_qk(nc, W, xt, du_p, q_p, k_p):
    with ExitStack() as own:
        def sb(name, shape, dt=F32):
            return own.enter_context(nc.sbuf_tensor(name, shape, dt))

        ps = own.enter_context(nc.psum_tensor("ps3", [P, 5, N], F32))
        w = sb("stencil", [P, GB, S])
        du = sb("du", [P, GB, S])
        react = sb("react", [P, GB, S])
        qk = sb("qk", [P, 2, N])
        qk_sq = sb("qk_sq", [P, 2, N])
        norm = sb("norm", [P, 2, N])
        names = ("lap_mm summed edged chain_a du_done qk_mm qk_copied qk_squared norm_mm rooted turn_done "
                 "du_kept").split()
        Z = {n: own.enter_context(nc.semaphore("p3_" + n)) for n in names}
        block = own.enter_context(nc.Block())

        @block.tensor
        def _(pe):
            pe.sem_inc(Z["turn_done"], 1)
            with pe.Fori(0, NG) as g:
                pe.wait_ge(Z["turn_done"], g + 1)
                nc.tensor.matmul(ps[:, 0, :], W["lap"][:, :], xt[:, bass.ds(g * N, N)],
                                 start=True, stop=True).then_inc(Z["lap_mm"], 1)
                pe.wait_ge(Z["du_done"], g + 1)
                for j in range(2):
                    nc.tensor.matmul(ps[:, 1 + j, :], W["w_qkv"][:, j * C:(j + 1) * C],
                                     du[:, :, :].rearrange("p b t -> p (b t)"),
                                     start=True, stop=True).then_inc(Z["qk_mm"], 1)
                pe.wait_ge(Z["qk_squared"], 2 * g + 2)
                for j in range(2):
                    last = nc.tensor.matmul(ps[:, 3 + j, :], W["same_head"][:, :], qk_sq[:, j, :],
                                            start=True, stop=True)
                last.then_inc(Z["norm_mm"], 1)

        @block.scalar
        def _(act):
            with act.Fori(0, NG) as g:
                for j in range(2):
                    act.wait_ge(Z["qk_mm"], 2 * g + j + 1)
                    nc.scalar.activation(qk_sq[:, j, :], ps[:, 1 + j, :], ACT.Square,
                                         bias=W["b_qkv"][:, j:j + 1]).then_inc(Z["qk_squared"], 1)
                    nc.scalar.activation(qk[:, j, :], ps[:, 1 + j, :], ACT.Identity,
                                         bias=W["b_qkv"][:, j:j + 1]).then_inc(Z["qk_copied"], 1)
                act.wait_ge(Z["norm_mm"], g + 1)
                nc.scalar.activation(norm[:, :, :], ps[:, 3:5, :], ACT.Sqrt).then_inc(Z["rooted"], 1)

        @block.gpsimd
        def _(pool):
            with pool.Fori(0, NG) as g:
                pool.wait_ge(Z["turn_done"], g + 1)
                x = by_group(xt[:, bass.ds(g * N, N)])
                nc.gpsimd.tensor_tensor(w[:, :, 1:S - 1], x[:, :, 0:S - 2], x[:, :, 2:S], ALU.add).then_inc(Z["summed"], 1)

        @block.vector
        def _(dve):
            with dve.Fori(0, NG) as g:
                ch = Chain(dve, Z["chain_a"], g, 9)
                x = by_group(xt[:, bass.ds(g * N, N)])

                def z(k):
                    return W["z"][:, k, bass.ds(g * GB, GB)].unsqueeze(2).to_broadcast([P, GB, S])

                dve.wait_ge(Z["summed"], g + 1)
                nc.vector.tensor_scalar(w[:, :, 0:1], x[:, :, 1:2], 2.0, None, ALU.mult)
                ch.link(nc.vector.tensor_scalar(w[:, :, S - 1:S], x[:, :, S - 2:S - 1], 2.0, None, ALU.mult))
                nc.vector.scalar_tensor_tensor(out=react[:, :, :], in0=x, scalar=1.0, in1=x,
                                               op0=ALU.subtract, op1=ALU.mult)
                ch.link(nc.vector.scalar_tensor_tensor(out=w[:, :, :], in0=x, scalar=-2.0, in1=w[:, :, :],
                                                       op0=ALU.mult, op1=ALU.add))
                ch.link(nc.vector.tensor_tensor(w[:, :, :], w[:, :, :], z(1), ALU.mult))
                ch.link(nc.vector.tensor_tensor(react[:, :, :], react[:, :, :], z(2), ALU.mult))
                dve.wait_ge(Z["lap_mm"], g + 1)
                ch.link(nc.vector.tensor_tensor(du[:, :, :], by_group(ps[:, 0, :]), z(0), ALU.mult))
                ch.link(nc.vector.tensor_tensor(du[:, :, :], du[:, :, :], w[:, :, :], ALU.add))
                nc.vector.tensor_tensor(du[:, :, :], du[:, :, :], react[:, :, :], ALU.subtract).then_inc(Z["du_done"], 1)
                dve.wait_ge(Z["du_done"], g + 1)

                def by_position(kept):
                    return kept[:, :, bass.ds(g * GB, GB)].rearrange("p t b -> p b t")

                nc.vector.tensor_copy(by_position(du_p), du[:, :, :]).then_inc(Z["du_kept"], 1)
                dve.wait_ge(Z["rooted"], g + 1)
                ch.link(nc.vector.tensor_scalar(norm[:, :, :], norm[:, :, :], L2_EPS, None, ALU.max))
                ch.link(nc.vector.reciprocal(norm[:, :, :], norm[:, :, :]))
                dve.wait_ge(Z["qk_copied"], 2 * g + 2)
                ch.link(nc.vector.scalar_tensor_tensor(out=by_position(q_p), in0=by_group(qk[:, 0, :]),
                                                       scalar=W["scale"][:, 0:1], in1=by_group(norm[:, 0, :]),
                                                       op0=ALU.mult, op1=ALU.mult))
                nc.vector.tensor_tensor(by_position(k_p), by_group(qk[:, 1, :]), by_group(norm[:, 1, :]),
                                        ALU.mult).then_inc(Z["turn_done"], 1)
                ch.end()


def attention(nc, W, xt, du_p, q_p, k_p):
    with ExitStack() as own:
        def sb(name, shape, dt=F32):
            return own.enter_context(nc.sbuf_tensor(name, shape, dt))

        def psum(name, shape):
            return own.enter_context(nc.psum_tensor(name, shape, F32))

        ps_v = psum("ps_v", [P, TB, C])
        ps_s = psum("ps_s", [P, TB, HQ, NB])
        ps_o = psum("ps_o", [P, TB, NB])
        ps_f = psum("ps_f", [P, TB, NB])
        du4 = sb("du4", [P, TB, HQ, NB])
        kx = sb("kx", [P, TB, HQ, NB])
        qx = sb("qx", [P, TB, HQ, NB])
        vb = sb("vb", [P, TB, C])
        sc = sb("sc", [P, TB, HQ, NB])
        pt = sb("pt", [P, TB, HQ, NB])
        top = sb("top4", [P, TB, HQ])
        den = sb("den4", [P, TB, HQ])
        o_t = sb("o_t", [P, TB, NB])
        names = ("du_copied k_spread q_spread v_mm v_done s_mm chain_b chain_first chain_last shifted exped p_turned o_mm o_done f_mm "
                 "x_done").split()
        Z = {n: own.enter_context(nc.semaphore("p3b_" + n)) for n in names}
        block = own.enter_context(nc.Block())
        TURNS = S // TB

        @block.gpsimd
        def _(pool):
            def copy_du(t):
                nc.gpsimd.tensor_copy(du4[:, :, :, :], du_p[:, bass.ds(t * TB, TB), :].unsqueeze(2)
                                      .to_broadcast([P, TB, HQ, NB])).then_inc(Z["du_copied"], 1)

            def spread_k(t):
                nc.gpsimd.tensor_tensor(kx[:, :, :, :],
                                        k_p[:, bass.ds(t * TB, TB), :].unsqueeze(2).to_broadcast([P, TB, HQ, NB]),
                                        W["quarter_of"][:, :].unsqueeze(1).unsqueeze(3).to_broadcast([P, TB, HQ, NB]),
                                        ALU.mult).then_inc(Z["k_spread"], 1)

            spread_k(0)
            copy_du(0)
            with pool.Fori(0, TURNS - 1) as i:
                pool.wait_ge(Z["s_mm"], i + 1)
                spread_k(i + 1)
                pool.wait_ge(Z["v_mm"], i + 1)
                copy_du(i + 1)

        @block.tensor
        def _(pe):
            def scores():
                for t in range(TB):
                    last = nc.tensor.matmul(ps_s[:, t, :, :].rearrange("p q b -> p (q b)"),
                                            qx[:, t, :, :].rearrange("p h b -> p (h b)"),
                                            kx[:, t, :, :].rearrange("p q b -> p (q b)"), start=True, stop=True)
                last.then_inc(Z["s_mm"], 1)

            def values():
                for t in range(TB):
                    last = nc.tensor.matmul(ps_v[:, t, :], du4[:, t, :, :].rearrange("p h b -> p (h b)"),
                                            W["w_qkv"][:, 2 * C:3 * C], start=True, stop=True)
                last.then_inc(Z["v_mm"], 1)

            def mix():
                for t in range(TB):
                    for q in range(HQ):
                        last = nc.tensor.matmul(ps_o[32 * q:32 * q + 32, t, :], vb[:, t, 32 * q:32 * q + 32],
                                                pt[:, t, q, :], start=True, stop=True)
                last.then_inc(Z["o_mm"], 1)

            def project():
                nc.tensor.matmul(ps_f[:, :, :].rearrange("p t b -> p (t b)"), W["w_o"][:, :],
                                 o_t[:, :, :].rearrange("p t b -> p (t b)"), start=True, stop=True).then_inc(Z["f_mm"], 1)

            pe.wait_ge(Z["k_spread"], 1)
            pe.wait_ge(Z["q_spread"], 1)
            scores()
            pe.wait_ge(Z["du_copied"], 1)
            values()
            with pe.Fori(0, TURNS - 1) as i:
                pe.wait_ge(Z["k_spread"], i + 2)
                pe.wait_ge(Z["q_spread"], i + 2)
                scores()
                pe.wait_ge(Z["v_done"], i + 1)
                pe.wait_ge(Z["p_turned"], i + 1)
                mix()
                pe.wait_ge(Z["du_copied"], i + 2)
                values()
                pe.wait_ge(Z["o_done"], i + 1)
                project()
            pe.wait_ge(Z["v_done"], TURNS)
            pe.wait_ge(Z["p_turned"], TURNS)
            mix()
            pe.wait_ge(Z["o_done"], TURNS)
            project()

        @block.scalar
        def _(act):
            def exps():
                nc.scalar.activation(sc[:, :, :, :], sc[:, :, :, :], ACT.Exp).then_inc(Z["exped"], 1)

            def finish_o():
                nc.scalar.activation(o_t[:, :, :], ps_o[:, :, :], ACT.Identity, bias=W["v_bias"][:, 0:1],
                                     scale=W["head"][:, 0:1]).then_inc(Z["o_done"], 1)

            act.wait_ge(Z["shifted"], 1)
            exps()
            with act.Fori(0, TURNS - 1) as i:
                act.wait_ge(Z["o_mm"], i + 1)
                finish_o()
                act.wait_ge(Z["shifted"], i + 2)
                exps()
            act.wait_ge(Z["o_mm"], TURNS)
            finish_o()

        @block.vector
        def _(dve):
            def spread(t):
                nc.vector.tensor_tensor(qx[:, :, :, :],
                                        q_p[:, bass.ds(t * TB, TB), :].unsqueeze(2).to_broadcast([P, TB, HQ, NB]),
                                        W["head_of"][:, :].unsqueeze(1).unsqueeze(3).to_broadcast([P, TB, HQ, NB]),
                                        ALU.mult).then_inc(Z["q_spread"], 1)

            def shift(ch):
                s = ps_s[:, :, :, :].rearrange("p t q b -> p (t q) b")
                peak = top[:, :, :].rearrange("p t q -> p (t q)")
                ch.link(nc.vector.tensor_reduce(peak, s, X, ALU.max))
                nc.vector.tensor_tensor(sc[:, :, :, :].rearrange("p t q b -> p (t q) b"), s,
                                        peak.unsqueeze(2).to_broadcast([P, TB * HQ, NB]),
                                        ALU.subtract).then_inc(Z["shifted"], 1)

            def block_v():
                nc.vector.tensor_tensor(vb[:, :, :], ps_v[:, :, :], W["v_block"][:, :].unsqueeze(1)
                                        .to_broadcast([P, TB, C]), ALU.mult).then_inc(Z["v_done"], 1)

            def normalise(ch):
                flat = sc[:, :, :, :].rearrange("p t q b -> p (t q) b")
                ch.link(nc.vector.tensor_reduce(den[:, :, :].rearrange("p t q -> p (t q)"), flat, X, ALU.add))
                ch.link(nc.vector.reciprocal(den[:, :, :], den[:, :, :]))
                ch.link(nc.vector.tensor_tensor(flat, flat, den[:, :, :].rearrange("p t q -> p (t q)").unsqueeze(2)
                                                .to_broadcast([P, HQ * TB, NB]), ALU.mult))
                nc.vector.transpose(pt[:, :, :, :].rearrange("p t q b -> p (t q b)"),
                                    sc[:, :, :, :].rearrange("p t q b -> p (t q b)")).then_inc(Z["p_turned"], 1)

            def add(t):
                x = xt[:, :].rearrange("p (b t) -> p b t", b=NB)[:, :, bass.ds(t * TB, TB)]
                nc.vector.scalar_tensor_tensor(out=x, in0=ps_f[:, :, :].rearrange("p t b -> p b t"),
                                               scalar=W["b_o"][:, 0:1], in1=x, op0=ALU.add,
                                               op1=ALU.add).then_inc(Z["x_done"], 1)

            first = Chain(dve, Z["chain_first"], 0, 1)
            spread(0)
            dve.wait_ge(Z["s_mm"], 1)
            shift(first)
            dve.wait_ge(Z["v_mm"], 1)
            block_v()
            first.end()
            dve.wait_ge(Z["s_mm"], 1)
            spread(1)

            def turn(i, more):
                ch = Chain(dve, Z["chain_b"], i, 4)
                dve.wait_ge(Z["exped"], i + 1)
                normalise(ch)
                dve.wait_ge(Z["s_mm"], i + 2)
                shift(ch)
                if more:
                    spread(i + 2)
                dve.wait_ge(Z["v_mm"], i + 2)
                block_v()
                dve.wait_ge(Z["f_mm"], i + 1)
                add(i)
                ch.end()

            with dve.Fori(0, TURNS - 2) as i:
                turn(i, True)
            turn(TURNS - 2, False)
            last = Chain(dve, Z["chain_last"], 0, 3)
            dve.wait_ge(Z["exped"], TURNS)
            normalise(last)
            dve.wait_ge(Z["f_mm"], TURNS)
            add(TURNS - 1)
            last.end()


def setup_ffn1(nc, D, W):
    with ExitStack() as own:
        def tmp(name, shape, dt=F32):
            return own.enter_context(nc.sbuf_tensor(name, shape, dt))

        def sem(name):
            return own.enter_context(nc.semaphore(name))

        ids = tmp("ids4", [NL, NB], I32)
        idf = tmp("idf4", [NL, NB])
        lang = tmp("lang", [NL, 1])
        b1 = tmp("b1", [NL, 32])
        gamma = tmp("gamma4", [NL, C])
        beta = tmp("beta4", [NL, C])
        b2 = tmp("b2", [NL, C])
        ps = own.enter_context(nc.psum_tensor("ps_s4", [P, 4, N], F32))
        loaded = sem("s4_loaded")
        chain_v = sem("s4_chain_v")
        hot = sem("s4_hot")
        picked = sem("s4_picked")
        loads = [
            (ids[:, :], D["itok_B_0_8"].to_broadcast([NL, NB])), (lang[:, :], D["c_lang"]),
            (W["ids_row"][:, :], D["itok_B_0_8"]),
            (b1[:, :], D["L1_cond2_b1"]), (b2[:, :], D["L1_cond2_b2"]),
            (gamma[:, :], D["L1_cond2_gamma"]), (beta[:, :], D["L1_cond2_beta"]),
            (W["router"][:, :], D["L1_ffn_router_w"]), (W["router_b"][:, :], D["L1_ffn_router_b"].to_broadcast([P, NE])),
            (W["w1"][:, :, :], D["w1_all"]), (W["c1"][:, :, :], D["b1_all"]),
            (W["w2"][:, :, :, :], D["w2_all"]), (W["sb2"][:, :], D["L1_ffn_sb2"]), (W["rb2"][:, :], D["L1_ffn_rb2"]),
            (W["rank"][:, :], D["c_rank"].to_broadcast([P, NE])), (W["pick8"][:, :], D["c_pick"]),
        ]
        block = own.enter_context(nc.Block())

        @block.sync
        def _(sp):
            for dst, src in loads:
                sp.dma_start(dst, src).then_inc(loaded, 16)

        @block.gpsimd
        def _(pool):
            nc.gpsimd.memset(W["mw96"][:, :, :, :], 0.0)
            nc.gpsimd.memset(W["neg_half"][:, :], -0.5)

        @block.tensor
        def _(pe):
            pe.wait_ge(hot, 1)
            for k, rows in enumerate((gamma, beta, b2)):
                nc.tensor.matmul(ps[:, k, 0:NB], rows[:, :], W["lang_hot"][:, :], start=True, stop=True)
            nc.tensor.matmul(ps[0:32, 3, 0:NB], b1[:, :], W["lang_hot"][:, :], start=True, stop=True).then_inc(picked, 1)

        @block.vector
        def _(dve):
            ch = Chain(dve, chain_v, 0, 1)
            dve.wait_ge(loaded, 16 * len(loads))
            ch.link(nc.vector.tensor_copy(idf[:, :], ids[:, :]))
            nc.vector.tensor_scalar(W["lang_hot"][:, :], idf[:, :], lang[:, 0:1], None, ALU.is_equal).then_inc(hot, 1)
            dve.wait_ge(picked, 1)
            nc.vector.tensor_copy(W["gamma_b"][:, :], ps[:, 0, 0:NB])
            nc.vector.tensor_copy(W["beta_b"][:, :], ps[:, 1, 0:NB])
            nc.vector.tensor_copy(W["b2_b"][:, :], ps[:, 2, 0:NB])
            nc.vector.tensor_copy(W["b1_b"][:, :], ps[0:32, 3, 0:NB])
            ch.end()


def adapter_and_experts(nc, D, W, xt, out):
    with ExitStack() as own:
        def sb(name, shape, dt=F32):
            return own.enter_context(nc.sbuf_tensor(name, shape, dt))

        ps = own.enter_context(nc.psum_tensor("ps4", [P, 8, N], F32))
        w1g = sb("w1g", [P, GB, 32])
        w2g = sb("w2g", [32, GB, C])
        had = sb("had", [32, GB, S])
        xa = sb("xa", [P, GB, S])
        mean = sb("mean4", [P, GB])
        var = sb("var4", [P, GB])
        rstd = sb("rstd4", [P, GB])
        xc = sb("xc4", [P, GB, C])
        sq = sb("sq4", [P, GB, C])
        xn = sb("xn4", [P, GB, C])
        yt = sb("yt4", [P, 2, N])
        lg = sb("lg4", [P, GB, NE])
        ex = sb("ex4", [P, GB, NE])
        hot = sb("hot4", [P, GB, NE])
        hot2 = sb("hot42", [P, GB, NE])
        top = sb("top42", [P, GB])
        den = sb("den42", [P, GB])
        m_parts = sb("m_parts4", [96, N], BF16)
        m_mid = sb("m_mid4", [96, N], BF16)
        m_rest = sb("m_rest4", [96, N])
        mw_t = sb("mw_t4", [NE, N])
        hh = sb("hh", [P, 4, N])
        hw = sb("hw", [P, 4, N])
        names = ("adapters ad1_mm ad1_done ad2_mm xa_done xa_mm centred squared var_done rstd_done xn_done "
                 "xn_mm yt_done router_mm shifted exped mw_done mw_copied mw_mm m_split mask_mm hidden_mm hidden_done "
                 "weighted taken moe_mm x_done stored chain_f chain_m").split()
        Z = {n: own.enter_context(nc.semaphore("p4_" + n)) for n in names}
        block = own.enter_context(nc.Block())
        TILES = 2 * (NE + 1)
        LEAD = 3

        @block.sync
        def _(sp):
            def load(g):
                for b in range(GB):
                    lang = sp.value_load(W["ids_row"][0:1, bass.ds(g * GB + b, 1)], min_val=0, max_val=NL - 1)
                    sp.dma_start(w1g[:, b, :], D["L1_cond2_W1"][:, bass.ds(lang * 32, 32)]).then_inc(Z["adapters"], 16)
                    sp.dma_start(w2g[:, b, :], D["L1_cond2_W2"][:, bass.ds(lang * C, C)]).then_inc(Z["adapters"], 16)

            def store(g):
                sp.wait_ge(Z["x_done"], g + 1)
                sp.dma_start(out[:, bass.ds(g * N, N)], xt[:, bass.ds(g * N, N)]).then_inc(Z["stored"], 16)

            load(0)
            with sp.Fori(0, NG - 1) as g:
                sp.wait_ge(Z["ad2_mm"], g + 1)
                load(g + 1)
                store(g)
            store(NG - 1)
            sp.wait_ge(Z["stored"], 16 * NG)

        @block.gpsimd
        def _(pool):
            with pool.Fori(0, NG) as g:
                pool.wait_ge(Z["var_done"], g + 1)
                nc.gpsimd.tensor_tensor(rstd[:, :], var[:, :], W["neg_half"][:, :], ALU.pow).then_inc(Z["rstd_done"], 1)

        @block.tensor
        def _(pe):
            def adapter_in(g):
                pe.wait_ge(Z["adapters"], 32 * GB * g + 32 * GB)
                for b in range(GB):
                    last = nc.tensor.matmul(ps[0:32, 0, b * S:(b + 1) * S], w1g[:, b, :],
                                            xt[:, bass.ds(g * N + b * S, S)], start=True, stop=True)
                last.then_inc(Z["ad1_mm"], 1)

            def adapter_out(g):
                pe.wait_ge(Z["ad1_done"], g + 1)
                for b in range(GB):
                    last = nc.tensor.matmul(ps[:, 1, b * S:(b + 1) * S], w2g[:, b, :], had[:, b, :],
                                            start=True, stop=True)
                last.then_inc(Z["ad2_mm"], 1)

            def to_tokens(g):
                pe.wait_ge(Z["xa_done"], g + 1)
                for b in range(GB):
                    last = nc.tensor.transpose(ps[:, 0, b * C:(b + 1) * C], xa[:, b, :], W["ident"][:, :])
                last.then_inc(Z["xa_mm"], 1)

            def to_channels(g):
                pe.wait_ge(Z["xn_done"], g + 1)
                for b in range(GB):
                    last = nc.tensor.transpose(ps[:, 1, b * S:(b + 1) * S], xn[:, b, :], W["ident"][:, :])
                last.then_inc(Z["xn_mm"], 1)

            def router(g, at):
                pe.wait_ge(Z["yt_done"], g + 1)
                for b in range(GB):
                    last = nc.tensor.matmul(ps[:, 0, b * NE:(b + 1) * NE], yt[:, at, b * S:(b + 1) * S],
                                            W["router"][:, :], start=True, stop=True)
                last.then_inc(Z["router_mm"], 1)

            def front(g, at):
                adapter_in(g)
                adapter_out(g)
                to_tokens(g)
                to_channels(g)
                router(g, at)

            def body(g, at, ahead):
                def hidden(k):
                    if k >= 2:
                        pe.wait_ge(Z["hidden_done"], g * TILES + k - 1)
                    nc.tensor.matmul(ps[:, 2 + k % 2, :], W["w1"][:, k, :], yt[:, at, :],
                                     start=True, stop=True).then_inc(Z["hidden_mm"], 1)

                def mask(e):
                    if e >= 2:
                        pe.wait_ge(Z["weighted"], g * 2 * NE + 2 * (e - 1))
                    nc.tensor.matmul(ps[:, 4 + e % 2, :], W["pick8"][:, e:e + 1].to_broadcast([96, P]), m_parts[:, :],
                                     start=True, stop=True).then_inc(Z["mask_mm"], 1)

                def outwards(k):
                    if k < 2:
                        pe.wait_ge(Z["hidden_done"], g * TILES + k + 1)
                        src = hh[:, k, :]
                    else:
                        pe.wait_ge(Z["weighted"], g * 2 * NE + k - 1)
                        src = hw[:, k % 4, :]
                    ins = nc.tensor.matmul(ps[:, 6 + at, :], W["w2"][:, k // 2, k % 2, :], src,
                                           start=(k == 0), stop=False)
                    if k >= 2:
                        ins.then_inc(Z["taken"], 1)

                hidden(0)
                hidden(1)
                pe.wait_ge(Z["mw_copied"], g + 1)
                for b in range(GB):
                    last = nc.tensor.transpose(ps[0:96, 1, b * S:(b + 1) * S],
                                               W["mw96"][:, b, :, :].rearrange("p k e -> p (k e)"), W["ident"][:, :])
                last.then_inc(Z["mw_mm"], 1)
                hidden(2)
                outwards(0)
                hidden(3)
                outwards(1)
                hidden(4)
                pe.wait_ge(Z["m_split"], g + 1)
                mask(0)
                for k in range(2, TILES):
                    if k % 2 == 0 and k // 2 < NE:
                        mask(k // 2)
                    if k + LEAD < TILES:
                        hidden(k + LEAD)
                    outwards(k)
                    if ahead is not None:
                        if k == 2:
                            adapter_in(ahead)
                        if k == 4:
                            adapter_out(ahead)
                        if k == 6:
                            to_tokens(ahead)
                        if k == 10:
                            to_channels(ahead)
                        if k == 12:
                            router(ahead, 1 - at)
                nc.tensor.matmul(ps[:, 6 + at, :], W["rb2"][:, :], mw_t[:, :],
                                 start=False, stop=True).then_inc(Z["moe_mm"], 1)

            in_pairs(pe, front, body)

        @block.scalar
        def _(act):
            def square(g):
                act.wait_ge(Z["centred"], g + 1)
                nc.scalar.activation(sq[:, :, :], xc[:, :, :], ACT.Square).then_inc(Z["squared"], 1)

            def exps(g):
                act.wait_ge(Z["shifted"], g + 1)
                nc.scalar.activation(ex[:, :, :], ex[:, :, :], ACT.Exp).then_inc(Z["exped"], 1)

            def copy_masks(g):
                act.wait_ge(Z["mw_done"], g + 1)
                nc.scalar.copy(W["mw96"][:, :, :, 0:NE],
                               hot[:, :, :].unsqueeze(2).to_broadcast([P, GB, 3, NE])).then_inc(Z["mw_copied"], 1)

            def front(g, at):
                square(g)
                exps(g)
                copy_masks(g)

            def body(g, at, ahead):
                for k in range(TILES):
                    act.wait_ge(Z["hidden_mm"], g * TILES + k + 1)
                    if k >= 6:
                        act.wait_ge(Z["weighted"], g * 2 * NE + k - 5)
                    nc.scalar.activation(hh[:, k % 4, :], ps[:, 2 + k % 2, :], ACT.Gelu,
                                         bias=W["c1"][:, k // 2, k % 2:k % 2 + 1]).then_inc(Z["hidden_done"], 1)
                    if ahead is not None and k == 10:
                        square(ahead)
                if ahead is not None:
                    exps(ahead)
                    copy_masks(ahead)

            in_pairs(act, front, body)

        @block.vector
        def _(dve):
            LINKS = (1, 1, 2, 1, 1, 2, 4, 6, 3)
            OFF = [sum(LINKS[:i]) for i in range(len(LINKS))]

            def chain(g, step):
                c = Chain(dve, Z["chain_f"], g, sum(LINKS))
                c.at = OFF[step]
                return c

            def vec(v, g):
                return v[:, bass.ds(g * GB, GB)].unsqueeze(2)

            rank = W["rank"][:, :].unsqueeze(1).to_broadcast([P, GB, NE])
            top_b = top[:, :].unsqueeze(2).to_broadcast([P, GB, NE])

            def first_of_top(ch, to):
                ch.link(nc.vector.tensor_tensor(to[:, :, :], lg[:, :, :], top_b, ALU.is_equal))
                ch.link(nc.vector.tensor_tensor(to[:, :, :], to[:, :, :], rank, ALU.mult))
                ch.link(nc.vector.tensor_reduce(top[:, :], to[:, :, :], X, ALU.max))
                ch.link(nc.vector.tensor_tensor(to[:, :, :], to[:, :, :], top_b, ALU.is_equal))

            def adapter_hidden(g):
                ch = chain(g, 0)
                dve.wait_ge(Z["ad1_mm"], g + 1)
                ch.link(nc.vector.tensor_tensor(had[:, :, :], by_group(ps[0:32, 0, :]),
                                                vec(W["b1_b"], g).to_broadcast([32, GB, S]), ALU.add))
                nc.vector.tensor_scalar(had[:, :, :], had[:, :, :], 0.0, None, ALU.max).then_inc(Z["ad1_done"], 1)

            def adapted(g):
                ch = chain(g, 1)
                dve.wait_ge(Z["ad2_mm"], g + 1)
                ch.link(nc.vector.tensor_tensor(xa[:, :, :].rearrange("p b t -> p (b t)"), ps[:, 1, :],
                                                xt[:, bass.ds(g * N, N)], ALU.add))
                nc.vector.tensor_tensor(xa[:, :, :], xa[:, :, :], vec(W["b2_b"], g).to_broadcast([P, GB, S]),
                                        ALU.add).then_inc(Z["xa_done"], 1)

            def centre(g):
                ch = chain(g, 2)
                dve.wait_ge(Z["xa_mm"], g + 1)
                o = ps[:, 0, :].rearrange("p (b c) -> p b c", b=GB)
                ch.link(nc.vector.tensor_reduce(mean[:, :], o, X, ALU.add))
                ch.link(nc.vector.tensor_scalar(mean[:, :], mean[:, :], 1.0 / C, None, ALU.mult))
                nc.vector.tensor_tensor(xc[:, :, :], o, mean[:, :].unsqueeze(2).to_broadcast([P, GB, C]),
                                        ALU.subtract).then_inc(Z["centred"], 1)

            def variance(g):
                ch = chain(g, 3)
                dve.wait_ge(Z["squared"], g + 1)
                ch.link(nc.vector.tensor_reduce(var[:, :], sq[:, :, :], X, ALU.add))
                nc.vector.tensor_scalar(var[:, :], var[:, :], 1.0 / C, LN_EPS, ALU.mult, ALU.add).then_inc(Z["var_done"], 1)

            def normalise(g):
                dve.wait_ge(Z["rstd_done"], g + 1)
                nc.vector.tensor_tensor(xn[:, :, :], xc[:, :, :], rstd[:, :].unsqueeze(2).to_broadcast([P, GB, C]),
                                        ALU.mult).then_inc(Z["xn_done"], 1)

            def to_experts(g, at):
                ch = chain(g, 4)
                dve.wait_ge(Z["xn_mm"], g + 1)
                y = by_group(yt[:, at, :])
                ch.link(nc.vector.tensor_tensor(y, by_group(ps[:, 1, :]), vec(W["gamma_b"], g).to_broadcast([P, GB, S]),
                                                ALU.mult))
                nc.vector.tensor_tensor(y, y, vec(W["beta_b"], g).to_broadcast([P, GB, S]), ALU.add).then_inc(Z["yt_done"], 1)

            def logits(g):
                ch = chain(g, 5)
                dve.wait_ge(Z["router_mm"], g + 1)
                ch.link(nc.vector.tensor_tensor(lg[:, :, :], ps[:, 0, 0:GB * NE].rearrange("p (b e) -> p b e", b=GB),
                                                W["router_b"][:, :].unsqueeze(1).to_broadcast([P, GB, NE]), ALU.add))
                ch.link(nc.vector.tensor_reduce(top[:, :], lg[:, :, :], X, ALU.max))
                nc.vector.tensor_tensor(ex[:, :, :], lg[:, :, :], top_b, ALU.subtract).then_inc(Z["shifted"], 1)

            def best(g):
                first_of_top(chain(g, 6), hot)

            def second_best(g):
                ch = chain(g, 7)
                ch.link(nc.vector.scalar_tensor_tensor(out=lg[:, :, :], in0=hot[:, :, :], scalar=-1e30, in1=lg[:, :, :],
                                                       op0=ALU.mult, op1=ALU.add))
                ch.link(nc.vector.tensor_reduce(top[:, :], lg[:, :, :], X, ALU.max))
                first_of_top(ch, hot2)

            def weights(g):
                ch = chain(g, 8)
                ch.link(nc.vector.tensor_tensor(hot[:, :, :], hot[:, :, :], hot2[:, :, :], ALU.add))
                dve.wait_ge(Z["exped"], g + 1)
                nc.vector.tensor_tensor(hot[:, :, :], hot[:, :, :], ex[:, :, :], ALU.mult)
                ch.link(nc.vector.tensor_reduce(den[:, :], ex[:, :, :], X, ALU.add))
                ch.link(nc.vector.reciprocal(den[:, :], den[:, :]))
                nc.vector.tensor_tensor(hot[:, :, :], hot[:, :, :], den[:, :].unsqueeze(2).to_broadcast([P, GB, NE]),
                                        ALU.mult).then_inc(Z["mw_done"], 1)

            def front(g, at):
                adapter_hidden(g)
                adapted(g)
                centre(g)
                variance(g)
                normalise(g)
                to_experts(g, at)
                logits(g)
                best(g)
                second_best(g)
                weights(g)

            def body(g, at, ahead):
                ch = Chain(dve, Z["chain_m"], g, 4)
                dve.wait_ge(Z["mw_mm"], g + 1)
                split3(nc, ch, m_parts, m_mid, m_rest, ps[0:96, 1, :]).then_inc(Z["m_split"], 1)
                nc.vector.tensor_copy(mw_t[:, :], ps[0:NE, 1, :])
                for k in range(2, TILES):
                    if k % 2 == 0:
                        dve.wait_ge(Z["mask_mm"], g * NE + k // 2)
                    dve.wait_ge(Z["hidden_done"], g * TILES + k + 1)
                    if k >= 6:
                        dve.wait_ge(Z["taken"], g * 2 * NE + k - 5)
                    nc.vector.tensor_tensor(hw[:, k % 4, :], hh[:, k % 4, :], ps[:, 4 + (k // 2 - 1) % 2, :],
                                            ALU.mult).then_inc(Z["weighted"], 1)
                    if ahead is not None:
                        if k == 3:
                            adapter_hidden(ahead)
                        if k == 5:
                            adapted(ahead)
                        if k == 7:
                            centre(ahead)
                        if k == 8:
                            variance(ahead)
                        if k == 9:
                            normalise(ahead)
                        if k == 11:
                            to_experts(ahead, 1 - at)
                        if k == 13:
                            logits(ahead)
                        if k == 14:
                            best(ahead)
                        if k == 15:
                            second_best(ahead)
                if ahead is not None:
                    weights(ahead)
                dve.wait_ge(Z["moe_mm"], g + 1)
                x = xt[:, bass.ds(g * N, N)]
                nc.vector.scalar_tensor_tensor(out=x, in0=ps[:, 6 + at, :], scalar=W["sb2"][:, 0:1],
                                               in1=x, op0=ALU.add, op1=ALU.add).then_inc(Z["x_done"], 1)
                ch.end()

            in_pairs(dve, front, body)


def build(nc, D, out):
    with ExitStack() as ctx:
        def sb(name, shape, dt=F32):
            return ctx.enter_context(nc.sbuf_tensor(name, shape, dt))

        xt = sb("xt", [P, NB * S])
        ident = sb("ident", [P, P])
        with ExitStack() as first:
            def w(name, shape, dt=F32):
                return first.enter_context(nc.sbuf_tensor(name, shape, dt))

            W = {
                "ident": ident, "lora_a": w("lora_a", [P, P]), "w_ab": w("w_ab", [P, 2 * DI]),
                "w_bc": w("w_bc", [P, NT, 96]), "w_delta": w("w_delta", [P, NT, DI]),
                "conv_w": w("conv_w", [P, NT, 4]), "conv_b": w("conv_b", [P, NT]),
                "dt_b": w("dt_b", [P, NT]), "a": w("a", [P, NT, NS]), "d_skip": w("d_skip", [P, NT]),
                "out_w": w("out_w", [P, NT, C]), "pick": w("pick", [96, 32], BF16),
                "gates": w("gates", [P, NB, NE]), "decay": w("decay", [P, RING, 2, GB, S]),
            }
            setup_scan(nc, first, D, W, xt)
            selective_scan(nc, D, W, xt)
        with ExitStack() as second:
            def w(name, shape, dt=F32):
                return second.enter_context(nc.sbuf_tensor(name, shape, dt))

            W = {
                "ident": ident, "shift": w("shift", [P, LAGS, S]), "wg_x": w("wg_x", [P, C]),
                "wg_ctx": w("wg_ctx", [P, C]), "bg": w("bg", [1, C]), "wn1": w("wn1", [P, 32]),
                "bn1": w("bn1", [32, 1]), "wn2": w("wn2", [32, ND]), "bn2": w("bn2", [ND, 1]),
                "w_soma": w("w_soma", [P, C]), "b_soma": w("b_soma", [P, 1]), "w_temp": w("w_temp", [P, C]),
                "b_temp": w("b_temp", [P, 1]), "w_out": w("w_out", [P, C]), "gamma": w("gamma", [P, 1]),
                "beta": w("beta", [P, 1]), "router": w("router", [P, NE]), "router_b": w("router_b", [P, NE]),
                "expert_w": w("expert_w", [P, NE, C]), "expert_b": w("expert_b", [NE, C]),
                "rank": w("rank", [P, NE]), "pick8": w("pick8", [96, 32], BF16),
                "from_start": w("from_start", [P, 4, S]), "k_ctx": w("k_ctx", [P, S]),
                "upto_end": w("upto_end", [P, CHUNKS, ND]), "bw": w("bw", [P, C]),
                "bw_lag": w("bw_lag", [ND, LAGS, C]), "ones": w("ones", [1, P]),
                "mw96": w("mw96", [P, GB, 3, 32]), "neg_half": w("neg_half", [P, GB]),
            }
            setup_ffn0(nc, D, W)
            traces_and_experts(nc, W, xt)
        with ExitStack() as third:
            def w(name, shape, dt=F32):
                return third.enter_context(nc.sbuf_tensor(name, shape, dt))

            W = {
                "lap": w("lap", [P, C]), "z": w("z", [P, 3, NB]), "w_qkv": w("w_qkv", [P, 3 * C]),
                "b_qkv": w("b_qkv", [P, 3]), "scale": w("scale", [P, 1]), "head": w("head", [P, 1]),
                "v_bias": w("v_bias", [P, 1]), "w_o": w("w_o", [P, C]), "b_o": w("b_o", [P, 1]),
                "same_head": w("same_head", [P, C]), "head_of": w("head_of", [P, HQ]),
                "quarter_of": w("quarter_of", [P, HQ]), "v_block": w("v_block", [P, C]),
            }
            du_p = w("du_p", [P, S, NB])
            q_p = w("q_p", [P, S, NB])
            k_p = w("k_p", [P, S, NB])
            setup_attention(nc, D, W)
            diffusion_and_qk(nc, W, xt, du_p, q_p, k_p)
            attention(nc, W, xt, du_p, q_p, k_p)
        with ExitStack() as fourth:
            def w(name, shape, dt=F32):
                return fourth.enter_context(nc.sbuf_tensor(name, shape, dt))

            W = {
                "ident": ident, "b2_b": w("b2_b", [P, NB]), "ids_row": w("ids_row", [1, NB], I32),
                "router": w("router4", [P, NE]), "router_b": w("router_b4", [P, NE]),
                "w1": w("w1", [P, 2 * (NE + 1), P]), "c1": w("c1", [P, NE + 1, 2]),
                "w2": w("w2", [P, NE + 1, 2, C]), "sb2": w("sb2", [P, 1]), "rb2": w("rb2", [NE, C]),
                "rank": w("rank4", [P, NE]), "pick8": w("pick84", [96, 32], BF16), "mw96": w("mw964", [P, GB, 3, 32]),
                "neg_half": w("neg_half4", [P, GB]), "lang_hot": w("lang_hot", [NL, NB]),
                "gamma_b": w("gamma_b", [P, NB]), "beta_b": w("beta_b", [P, NB]), "b1_b": w("b1_b", [32, NB]),
            }
            setup_ffn1(nc, D, W)
            adapter_and_experts(nc, D, W, xt, out)


def lay_out(a):
    def tiles(w, rows):
        return w.reshape(rows // P, P, -1).transpose(1, 0, 2)

    xp = a["L0_attn_x_proj_w"]
    bc = xp[DI:].T
    L = {
        "x": a["x"].transpose(2, 0, 1).reshape(C, NB * S),
        "L0_cond_lora_B": a["L0_cond_lora_B"].transpose(1, 0, 2).reshape(C, NE * R),
        "L0_cond_lora_A": a["L0_cond_lora_A"].transpose(2, 0, 1).reshape(C, NE * R),
        "L0_attn_in_proj_w": a["L0_attn_in_proj_w"].T,
        "x_proj_delta": tiles(xp[:DI], DI),
        "x_proj_bc": tiles(np.concatenate([bc, bc, bc], axis=1), DI),
        "L0_attn_dt_proj_w": tiles(a["L0_attn_dt_proj_w"].T, DI),
        "L0_cond_gate_W1": a["L0_cond_gate_W1"],
        "L0_cond_gate_b1": a["L0_cond_gate_b1"].reshape(-1, 1),
        "L0_cond_gate_W2": a["L0_cond_gate_W2"],
        "L0_cond_gate_b2": a["L0_cond_gate_b2"].reshape(1, -1),
        "itok_B_4_6": a["itok_B_4_6"].reshape(1, -1),
        "L0_attn_conv_w": tiles(a["L0_attn_conv_w"].reshape(DI, 4), DI),
        "L0_attn_conv_b": a["L0_attn_conv_b"].reshape(NT, P).T,
        "L0_attn_dt_proj_b": a["L0_attn_dt_proj_b"].reshape(NT, P).T,
        "L0_attn_D_param": a["L0_attn_D_param"].reshape(NT, P).T,
        "L0_attn_A_log": tiles(a["L0_attn_A_log"], DI),
        "L0_attn_out_proj_w": tiles(a["L0_attn_out_proj_w"].T, DI),
        "condB_tauraws": a["condB_tauraws"].reshape(1, ND),
        "tau_column": np.tile(a["condB_tauraws"], P // ND).reshape(P, 1),
        "L0_cond2_tau_ctx": a["L0_cond2_tau_ctx"].reshape(1, 1),
        "cond_1024": a["cond_1024"].T,
        "wg_x": a["L0_cond2_Wg"][:, :C].T, "wg_ctx": a["L0_cond2_Wg"][:, C:].T,
        "L0_cond2_bg": a["L0_cond2_bg"].reshape(1, C),
        "L0_cond2_Wn1": a["L0_cond2_Wn1"].T, "L0_cond2_bn1": a["L0_cond2_bn1"].reshape(-1, 1),
        "cond_256": a["cond_256"].T, "condB_bn2": a["condB_bn2"].reshape(ND, 1),
        "L0_cond2_Wsoma": a["L0_cond2_Wsoma"].T, "L0_cond2_bsoma": a["L0_cond2_bsoma"].reshape(C, 1),
        "L0_cond2_Wtemp": a["L0_cond2_Wtemp"].T, "L0_cond2_btemp": a["L0_cond2_btemp"].reshape(C, 1),
        "L0_cond2_Wout": a["L0_cond2_Wout"].T, "L0_cond2_gamma": a["L0_cond2_gamma"].reshape(C, 1),
        "L0_cond2_beta": a["L0_cond2_beta"].reshape(C, 1),
        "L0_ffn_router_w": a["L0_ffn_router_w"].T, "L0_ffn_router_b": a["L0_ffn_router_b"].reshape(1, NE),
        "L0_ffn_expert_w": a["L0_ffn_expert_w"].transpose(2, 0, 1), "L0_ffn_expert_b": a["L0_ffn_expert_b"],
        "condB_zX": a["condB_zX"].reshape(1, NB), "condB_zY": a["condB_zY"].reshape(1, NB),
        "condB_zR": a["condB_zR"].reshape(1, NB),
        "L1_attn_in_proj_weight": a["L1_attn_in_proj_weight"].T,
        "L1_attn_in_proj_bias": a["L1_attn_in_proj_bias"].reshape(3, C).T,
        "L1_attn_logit_scale": np.repeat(a["L1_attn_logit_scale"].reshape(-1), C // 16).reshape(C, 1),
        "L1_attn_head_scale": np.repeat(a["L1_attn_head_scale"].reshape(-1), C // 16).reshape(C, 1),
        "L1_attn_out_w": a["L1_attn_out_w"].T, "L1_attn_out_b": a["L1_attn_out_b"].reshape(C, 1),
        "itok_B_0_8": a["itok_B_0_8"].reshape(1, NB),
        "L1_cond2_W1": a["L1_cond2_W1"].transpose(1, 0, 2).reshape(C, -1),
        "L1_cond2_W2": a["L1_cond2_W2"].transpose(1, 0, 2).reshape(32, -1),
        "L1_cond2_b1": a["L1_cond2_b1"], "L1_cond2_b2": a["L1_cond2_b2"],
        "L1_cond2_gamma": a["L1_cond2_gamma"], "L1_cond2_beta": a["L1_cond2_beta"],
        "L1_ffn_router_w": a["L1_ffn_router_w"], "L1_ffn_router_b": a["L1_ffn_router_b"].reshape(1, NE),
        "w1_all": np.concatenate([a["L1_ffn_sw1"][None], a["L1_ffn_rw1"]]).reshape(NE + 1, C, 2, P)
        .transpose(1, 0, 2, 3).reshape(C, 2 * (NE + 1), P),
        "b1_all": np.concatenate([a["L1_ffn_sb1"][None], a["L1_ffn_rb1"]]).reshape(NE + 1, 2, P).transpose(2, 0, 1),
        "w2_all": np.concatenate([a["L1_ffn_sw2"][None], a["L1_ffn_rw2"]]).reshape(NE + 1, 2, P, C).transpose(2, 0, 1, 3),
        "L1_ffn_sb2": a["L1_ffn_sb2"].reshape(C, 1), "L1_ffn_rb2": a["L1_ffn_rb2"],
        "c_expert": np.arange(NE, dtype=np.float32).reshape(1, -1),
        "c_ident": np.eye(P, dtype=np.float32),
        "c_pick": np.tile(np.eye(32, dtype=np.float32), (3, 1)),
    }
    s, t, k = np.arange(S), np.arange(S), np.arange(CHUNKS)
    since = t[None, :] - s[:, None]
    before = LAGS * k[None, :] - s[:, None]
    chunk = (4 * np.arange(4)[None, :] + np.arange(P)[:, None] // ND)[:, :, None]
    lag = np.arange(LAGS)
    L.update({
        "c_lag": lag.reshape(1, -1), "c_rank": np.arange(NE, 0, -1).reshape(1, -1),
        "c_upto_at": np.maximum(before - 1, 0), "c_upto_on": before > 0,
        "c_from_at": np.clip(t[None, None, :] - LAGS * chunk + 1, 0, LAGS),
        "c_from_on": t[None, None, :] // LAGS == chunk,
        "c_ctx_at": np.maximum(since, 0), "c_ctx_on": since >= 0,
        "c_shift": (since[:, None, :] == lag[None, :, None]) & (t // LAGS == (s // LAGS)[:, None])[:, None, :],
    })
    c = np.arange(C)
    lap = -2.0 * np.eye(C)
    for to in range(C):
        lap[abs(to - 1), to] += 1
        lap[C - 1 - abs(C - 2 - to), to] += 1
    L.update({
        "c_lap": lap, "c_same_head": c[:, None] // 8 == c[None, :] // 8,
        "c_head_of": c[:, None] // 8 % HQ == np.arange(HQ)[None, :],
        "c_quarter_of": c[:, None] // 32 == np.arange(HQ)[None, :],
        "c_v_block": np.arange(P)[:, None] // NB == (c // 8 % HQ)[None, :],
        "c_lang": np.arange(NL).reshape(NL, 1),
    })
    for name in L:
        if name.startswith("c_"):
            L[name] = L[name].astype(np.float32)
    return L


_BF16_CONSTS = ("c_pick",)


def kernel(**inputs):
    import ml_dtypes
    import concourse.bacc as _bacc
    from concourse.bass_utils import run_bass_kernel_spmd as _run

    nc = _bacc.Bacc("TRN2", target_bir_lowering=False, num_devices=1)
    arrays, D = {}, {}
    for name, a in lay_out({k: np.asarray(v) for k, v in inputs.items()}).items():
        if name in _BF16_CONSTS:
            a = a.astype(ml_dtypes.bfloat16)
        a = np.ascontiguousarray(a)
        arrays[f"in_{name}"] = a
        D[name] = nc.dram_tensor(f"in_{name}", a.shape, mybir.dt.from_np(a.dtype), kind="ExternalInput").ap()
    out = nc.dram_tensor("out_0", (C, NB * S), F32, kind="ExternalOutput").ap()
    build(nc, D, out)
    r = _run(nc, [arrays], core_ids=[0])
    got = np.asarray(r.results[0]["out_0"])
    return np.ascontiguousarray(got.reshape(C, NB, S).transpose(1, 2, 0))
```

```python
from contextlib import ExitStack, contextmanager

import numpy as np

import concourse.bass as bass
from concourse import mybir

F32 = mybir.dt.float32
BF16 = mybir.dt.bfloat16
I32 = mybir.dt.int32
ALU = mybir.AluOpType
ACT = mybir.ActivationFunctionType
X = mybir.AxisListType.X

P = 128
NB = 32
S = 128
C = 128
GB = 4
NG = NB // GB
N = GB * S
NE = 8
R = 16
DI = 256
NT = DI // P
NS = 16
LORA_SCALE = 32 / R
RING = 4
HRING = 3
BRING = 4
LAG = 3
ND = 32
LAGS = 8
CHUNKS = S // LAGS
LN_EPS = 1e-5
LOGIT_SCALE_MAX = float(np.log(1.0 / 0.01))
L2_EPS = 1e-12
HQ = 4
TB = 8
NL = 10


class Chain:

    def __init__(self, eng, sem, turn, per_turn):
        self.eng, self.sem, self.base, self.per_turn, self.at = eng, sem, turn * per_turn, per_turn, 0

    def link(self, ins):
        ins.then_inc(self.sem, 1)
        self.at += 1
        self.eng.wait_ge(self.sem, self.base + self.at)

    def end(self):
        assert self.at == self.per_turn, (self.at, self.per_turn)


@contextmanager
def phase_semaphores(nc):
    taken = []

    def sem(name):
        taken.append(nc.alloc_semaphore(name))
        return taken[-1]

    yield sem
    nc.clear_and_free_semaphores(taken)
    nc.all_engine_barrier()


def by_position(kept, g):
    return kept[:, :, bass.ds(g * GB, GB)].rearrange("p t b -> p b t")


def load_all(eng, sem, loads):
    for dst, src in loads:
        eng.dma_start(dst, src).then_inc(sem, 16)


def in_pairs(eng, front, body):
    front(0, 0)
    with eng.Fori(0, NG // 2 - 1) as i:
        body(2 * i, 0, 2 * i + 1, 2 * i + 2)
        body(2 * i + 1, 1, 2 * i + 2, 2 * i + 3)
    body(NG - 2, 0, NG - 1, None)
    body(NG - 1, 1, None, None)


def in_turns(eng, front, body):
    front(0)
    with eng.Fori(0, NG - 1) as g:
        body(g, g + 1)
    body(NG - 1, None)


def by_group(ap):
    return ap.rearrange("p (b t) -> p b t", b=GB)


def setup_scan(nc, ctx, D, W, xt):
    def sb(name, shape, dt=F32):
        return ctx.enter_context(nc.sbuf_tensor(name, shape, dt))

    with ExitStack() as own:
        def tmp(name, shape, dt=F32):
            return own.enter_context(nc.sbuf_tensor(name, shape, dt))

        def psum(name, shape):
            return own.enter_context(nc.psum_tensor(name, shape, F32))

        sem = own.enter_context(phase_semaphores(nc))

        lora_b = tmp("lora_b", [P, P])
        in_proj = tmp("in_proj", [P, 2 * DI])
        xp_rows = tmp("xp_rows", [P, NT, DI])
        dt_w = tmp("dt_w", [P, NT, DI])
        gate_w1 = tmp("gate_w1", [P, 32])
        gate_b1 = tmp("gate_b1", [P, 1])
        gate_w2 = tmp("gate_w2", [P, NE])
        quarter = tmp("quarter", [P, 4])
        w2_blocks = tmp("w2_blocks", [P, 4, NE])
        gate_b2 = tmp("gate_b2", [P, NE])
        ids = tmp("ids", [P, NB], I32)
        idf = tmp("idf", [P, NB])
        expert = tmp("expert", [P, NE])
        allowed = tmp("allowed", [P, NB, NE])
        hid = tmp("hid", [P, NG // 4, N])
        conv_w = tmp("conv_w", [P, 4, DI])
        w_x = tmp("w_x", [P, DI])
        top = tmp("top", [P, NB])
        ps_h = psum("ps_h", [P, NG // 4, N])
        ps_l = psum("ps_l", [P, NB, NE])
        ps_ab = psum("ps_ab", [P, 2 * DI])
        ps_d = psum("ps_d", [P, NT, DI])

        loaded = sem("setup_loaded")
        factors_loaded = sem("factors_loaded")
        QUARTERS = 4
        x_loaded = [sem("x_loaded%d" % q) for q in range(QUARTERS)]
        hid_done = sem("hid_done")
        w2_done = sem("w2_blocks_done")
        h_mm = sem("h_mm")
        logits_done = sem("logits_done")
        ab_mm = sem("ab_mm")
        delta_mm = sem("delta_mm")
        chain_v = sem("setup_chain_v")
        act_ready = sem("setup_act_ready")
        shifted = sem("logits_shifted")
        exped = sem("gates_exped")
        x_scaled = sem("w_x_scaled")

        factors = [
            (lora_b[:, :], D["L0_cond_lora_B"]), (in_proj[:, :], D["L0_attn_in_proj_w"]),
            (xp_rows[:, :, :], D["x_proj_delta"]), (dt_w[:, :, :], D["L0_attn_dt_proj_w"]),
        ]
        loads = [
            (gate_w1[:, :], D["L0_cond_gate_W1"]), (gate_b1[:, :], D["L0_cond_gate_b1"]),
            (gate_w2[:, :], D["L0_cond_gate_W2"]), (quarter[:, :], D["c_quarter"]),
            (gate_b2[:, :], D["L0_cond_gate_b2"].to_broadcast([P, NE])),
            (ids[:, :], D["itok_B_4_6"].to_broadcast([P, NB])),
            (expert[:, :], D["c_expert"].to_broadcast([P, NE])),
            (W["ident"][:, :], D["c_ident"]), (W["lora_a"][:, :], D["L0_cond_lora_A"]),
            (W["w_bc"][:, :, :], D["x_proj_bc"]), (conv_w[:, :, :], D["L0_attn_conv_w"].to_broadcast([P, 4 * DI])),
            (W["conv_b"][:, :], D["L0_attn_conv_b"]), (W["dt_b"][:, :], D["L0_attn_dt_proj_b"]),
            (W["a"][:, :, :], D["L0_attn_A_log"]), (W["d_skip"][:, :], D["L0_attn_D_param"]),
            (W["out_w"][:, :, :], D["L0_attn_out_proj_w"]), (W["pick"][:, :], D["c_pick"]),
        ]
        block = own.enter_context(nc.Block())

        @block.sync
        def _(sp):
            load_all(sp, factors_loaded, factors)
            for q in range(QUARTERS):
                at = slice(q * NB * S // QUARTERS, (q + 1) * NB * S // QUARTERS)
                sp.dma_start(xt[:, at], D["x"][:, at]).then_inc(x_loaded[q], 16)

        @block.tensor
        def _(pe):
            pe.wait_ge(factors_loaded, 16 * len(factors))
            nc.tensor.matmul(ps_ab[:, :], lora_b[:, :], in_proj[:, :], start=True, stop=True).then_inc(ab_mm, 1)
            for kt in range(NT):
                for mt in range(NT):
                    last = nc.tensor.matmul(ps_d[:, kt, :], xp_rows[:, mt, kt * P:(kt + 1) * P], dt_w[:, mt, :],
                                            start=(mt == 0), stop=(mt == NT - 1))
            last.then_inc(delta_mm, 1)
            pe.wait_ge(loaded, 16 * len(loads))
            for g in range(NG):
                if g % (NG // QUARTERS) == 0:
                    pe.wait_ge(x_loaded[g // (NG // QUARTERS)], 16)
                nc.tensor.matmul(ps_h[32 * (g % 4):32 * (g % 4) + 32, g // 4, :], gate_w1[:, :],
                                 xt[:, g * N:(g + 1) * N], start=True, stop=True).then_inc(h_mm, 1)
            pe.wait_ge(w2_done, 1)
            for half in range(NG // 4):
                pe.wait_ge(hid_done, half + 1)
                for b in range(GB):
                    last = nc.tensor.matmul(
                        ps_l[:, half * 4 * GB:(half + 1) * 4 * GB, :].rearrange("p (q b) e -> p q b e", b=GB)[:, :, b, :],
                        hid[:, half, b * S:(b + 1) * S], w2_blocks[:, :, :].rearrange("p q e -> p (q e)"),
                        start=True, stop=True)
            last.then_inc(logits_done, 1)

        @block.scalar
        def _(act):
            load_all(act, loaded, loads)
            act.wait_ge(ab_mm, 1)
            nc.scalar.mul(w_x[:, :], ps_ab[:, 0:DI], LORA_SCALE).then_inc(x_scaled, 1)
            nc.scalar.mul(W["w_z"][:, :], ps_ab[:, DI:2 * DI], LORA_SCALE)
            act.wait_ge(delta_mm, 1)
            nc.scalar.copy(W["w_delta"][:, :, :], ps_d[:, :, :])
            act.wait_ge(loaded, 16 * len(loads))
            for half in range(NG // 4):
                act.wait_ge(h_mm, 4 * half + 4)
                nc.scalar.activation(hid[:, half, :], ps_h[:, half, :], ACT.Relu,
                                     bias=gate_b1[:, 0:1]).then_inc(hid_done, 1)
            nc.scalar.activation(W["a"][:, :, :], W["a"][:, :, :], ACT.Exp).then_inc(act_ready, 1)
            act.wait_ge(act_ready, 1)
            nc.scalar.mul(W["a"][:, :, :], W["a"][:, :, :], -1.0)
            act.wait_ge(shifted, 1)
            nc.scalar.activation(W["gates"][:, :, :], W["gates"][:, :, :], ACT.Exp).then_inc(exped, 1)

        @block.vector
        def _(dve):
            ch = Chain(dve, chain_v, 0, 11)
            dve.wait_ge(loaded, 16 * len(loads))
            nc.vector.tensor_tensor(w2_blocks[:, :, :], gate_w2[:, :].unsqueeze(1).to_broadcast([P, 4, NE]),
                                    quarter[:, :].unsqueeze(2).to_broadcast([P, 4, NE]), ALU.mult).then_inc(w2_done, 1)
            ch.link(nc.vector.tensor_copy(idf[:, :], ids[:, :]))
            ch.link(nc.vector.tensor_scalar(idf[:, :], idf[:, :], 1.0, None, ALU.add))
            ch.link(nc.vector.tensor_tensor(allowed[:, :, :], idf[:, :].unsqueeze(2).to_broadcast([P, NB, NE]),
                                            expert[:, :].unsqueeze(1).to_broadcast([P, NB, NE]), ALU.is_equal))
            ch.link(nc.vector.memset(allowed[:, :, 0:1], 1.0))
            ch.link(nc.vector.tensor_scalar(allowed[:, :, :], allowed[:, :, :], 1e9, -1e9, ALU.mult, ALU.add))
            nc.vector.memset(W["decay"][:, :, :, :, 0:1], 0.0)
            dve.wait_ge(x_scaled, 1)
            nc.vector.tensor_tensor(W["w_conv"][:, :, :], w_x[:, :].unsqueeze(1).to_broadcast([P, 4, DI]),
                                    conv_w[:, :, :], ALU.mult)
            dve.wait_ge(logits_done, 1)
            gates = W["gates"][:, :, :]
            ch.link(nc.vector.tensor_tensor(gates, ps_l[:, :, :],
                                            gate_b2[:, :].unsqueeze(1).to_broadcast([P, NB, NE]), ALU.add))
            ch.link(nc.vector.tensor_tensor(gates, gates, allowed[:, :, :], ALU.add))
            ch.link(nc.vector.tensor_reduce(top[:, :], gates, X, ALU.max))
            nc.vector.tensor_tensor(gates, gates, top[:, :].unsqueeze(2).to_broadcast([P, NB, NE]),
                                    ALU.subtract).then_inc(shifted, 1)
            dve.wait_ge(exped, 1)
            ch.link(nc.vector.tensor_reduce(top[:, :], gates, X, ALU.add))
            ch.link(nc.vector.reciprocal(top[:, :], top[:, :]))
            ch.link(nc.vector.tensor_tensor(gates, gates, top[:, :].unsqueeze(2).to_broadcast([P, NB, NE]), ALU.mult))
            ch.end()


def selective_scan(nc, W, xt, later):
    with ExitStack() as own:
        def sb(name, shape, dt=F32):
            return own.enter_context(nc.sbuf_tensor(name, shape, dt))

        def psum(name, shape):
            return own.enter_context(nc.psum_tensor(name, shape, F32))

        sem = own.enter_context(phase_semaphores(nc))

        ps_y = psum("ps_y", [P, NT, N])
        ps_b = psum("ps_b", [P, 2, N])
        ps_c = psum("ps_c", [P, 2, N])
        ps_w = psum("ps_w", [P, 2, N])
        gates_g = sb("gates_g", [P, GB, NE, R])
        gexp = sb("gexp", [P, N])
        mixed = sb("mixed", [P, N])
        spa = sb("spa", [P, NT, N])
        spr = sb("spr", [P, NT, N])
        xi = sb("xi", [P, 2, NT, N])
        zs = sb("zs", [P, 2, NT, N])
        delta = sb("delta", [P, 2, NT, N])
        u = sb("u", [P, 2, NT, N])
        bc_parts = sb("bc_parts", [96, 2, N], BF16)
        bc_mid = sb("bc_mid", [96, N], BF16)
        bc_rest = sb("bc_rest", [96, N])
        b_sb = sb("b_sb", [P, BRING, 2, N])
        decay = W["decay"]
        dbx = sb("dbx", [P, RING, 2, N])
        h = sb("h", [P, HRING, 2, N])
        ch_sb = sb("ch_sb", [P, RING, 2, N])
        pair_sum = sb("pair_sum", [P, 2, N])
        yd = sb("yd", [P, NT, N])

        copied = sem("gates_copied")
        a_mm = sem("lora_a_mm")
        gexp_mm = sem("gexp_mm")
        gexp_done = sem("gexp_done")
        mixed_done = sem("mixed_done")
        x_mm = sem("in_proj_x_mm")
        z_mm = sem("in_proj_z_mm")
        z_copied = sem("z_copied")
        zs_done = sem("z_silu")
        xi_done = sem("xi_done")
        bc_mm = sem("bc_mm")
        delta_mm = sem("delta_mm2")
        parts_done = sem("bc_parts_done")
        sp_act = sem("softplus_act")
        sp_max = sem("softplus_max")
        u_done = sem("u_done")
        b_cast = sem("b_broadcast")
        c_cast = sem("c_broadcast")
        b_copied = sem("b_copied")
        decays = sem("decays")
        dbx_done = sem("dbx_done")
        scans = sem("scans")
        weighted = sem("weighted")
        paired = sem("paired")
        reduced = sem("reduced")
        y_read = sem("y_read")
        gated = sem("y_gated")
        out_mm = sem("out_mm")
        attn_done = sem("attn_done")
        chain_f = sem("front_chain_v")

        NP2 = NS // 2
        UNITS = NP2 * NT
        PAIRED = UNITS // RING

        def in_pair_sum(unit):
            return unit % RING == RING - 1

        block = own.enter_context(nc.Block())

        @block.sync
        def _(sp):
            load_all(sp, *later)

        @block.tensor
        def _(pe):
            def front_mix(g):
                if not isinstance(g, int) or g > 0:
                    pe.wait_ge(sp_max, g)
                nc.tensor.matmul(ps_w[:, 0, :], W["lora_a"][:, :], xt[:, bass.ds(g * N, N)],
                                 start=True, stop=True).then_inc(a_mm, 1)
                pe.wait_ge(copied, g + 1)
                for b in range(GB):
                    last = nc.tensor.transpose(ps_w[:, 1, b * S:(b + 1) * S],
                                               gates_g[:, b, :, :].rearrange("p e r -> p (e r)"), W["ident"][:, :])
                last.then_inc(gexp_mm, 1)

            def front_x(g, j, lags=range(4)):
                if j == 0 and lags[0] == 0:
                    pe.wait_ge(mixed_done, g + 1)
                for lag in lags:
                    last = nc.tensor.matmul(by_group(ps_w[:, j, :])[:, :, lag:S],
                                            W["w_conv"][:, 3 - lag, j * P:(j + 1) * P],
                                            by_group(mixed[:, :])[:, :, 0:S - lag],
                                            start=(lag == 0), stop=(lag == 3))
                if lags[-1] == 3:
                    last.then_inc(x_mm, 1)

            def front_z(g):
                pe.wait_ge(xi_done, g + 1)
                for j in range(NT):
                    last = nc.tensor.matmul(ps_w[:, j, :], W["w_z"][:, j * P:(j + 1) * P], mixed[:, :],
                                            start=True, stop=True)
                last.then_inc(z_mm, 1)

            def front_bc(g, at):
                pe.wait_ge(z_copied, g + 1)
                for kt in range(NT):
                    last = nc.tensor.matmul(ps_w[0:96, 0, :], W["w_bc"][:, kt, :], xi[:, at, kt, :],
                                            start=(kt == 0), stop=(kt == NT - 1))
                last.then_inc(bc_mm, 1)

            def front_delta(g, at, jt):
                if jt == 0:
                    pe.wait_ge(parts_done, g + 1)
                for kt in range(NT):
                    last = nc.tensor.matmul(ps_w[:, jt, :], W["w_delta"][:, kt, jt * P:(jt + 1) * P],
                                            xi[:, at, kt, :], start=(kt == 0), stop=(kt == NT - 1))
                last.then_inc(delta_mm, 1)

            def cast(to, first, g, at):
                for n in range(2):
                    last = nc.tensor.matmul(to[:, n, :], W["pick"][:, first + n:first + n + 1].to_broadcast([96, P]),
                                            bc_parts[:, at, :], start=True, stop=True)
                return last

            def cast_b(g, at, pair):
                pe.wait_ge(b_copied, g * NP2 + pair + 1)
                if pair == 0:
                    pe.wait_ge(parts_done, g + 1)
                cast(ps_b, 2 * pair, g, at).then_inc(b_cast, 1)

            def cast_c(g, at, pair):
                pe.wait_ge(weighted, g * UNITS + NT * pair + 1)
                cast(ps_c, NS + 2 * pair, g, at).then_inc(c_cast, 1)

            def front(g, at):
                front_mix(g)
                front_x(g, 0)
                front_x(g, 1)
                front_z(g)
                front_bc(g, at)
                front_delta(g, at, 1)
                front_delta(g, at, 0)
                cast_b(g, at, 0)
                cast_b(g, at, 1)
                cast_c(g, at, 0)
                front_mix(g + 1)
                cast_b(g, at, 2)

            def reduce(g, unit):
                if unit == 0:
                    pe.wait_ge(attn_done, g + 1)
                if in_pair_sum(unit):
                    pe.wait_ge(paired, g * PAIRED + unit // RING + 1)
                    terms = [pair_sum[:, unit // RING % 2, :]]
                else:
                    pe.wait_ge(weighted, g * UNITS + unit + 2)
                    terms = [ch_sb[:, unit % RING, n, :] for n in range(2)]
                for n, term in enumerate(terms):
                    last = nc.tensor.matmul(ps_y[:, unit % NT, :], W["ident"][:, :], term,
                                            start=(unit < NT and n == 0),
                                            stop=(unit >= UNITS - NT and n == len(terms) - 1))
                last.then_inc(reduced, 1)

            def project(g):
                pe.wait_ge(gated, g + 1)
                for kt in range(NT):
                    last = nc.tensor.matmul(ps_y[:, 0, :], W["out_w"][:, kt, :], yd[:, kt, :],
                                            start=(kt == 0), stop=(kt == NT - 1))
                last.then_inc(out_mm, 1)

            def scan(g, at, ahead, after):
                for pair in range(NP2):
                    if pair == 2:
                        cast_c(g, at, pair)
                    if pair >= 1 and pair + 2 < NP2:
                        cast_b(g, at, pair + 2)
                    if pair + 2 >= NP2 and ahead is not None:
                        cast_b(ahead, 1 - at, pair + 2 - NP2)
                    if ahead is not None and 1 <= pair <= NT:
                        front_x(ahead, pair - 1, range(2, 4))
                    if pair >= 2:
                        reduce(g, NT * pair - 3)
                    if pair >= 1 and pair != 2:
                        cast_c(g, at, pair)
                    if pair >= 1:
                        reduce(g, NT * pair - 2)
                    if ahead is None:
                        continue
                    if pair < NT:
                        front_x(ahead, pair, range(0, 2))
                    if pair == 3:
                        front_z(ahead)
                    if pair == 4:
                        front_bc(ahead, 1 - at)
                        front_delta(ahead, 1 - at, 1)
                    if pair == 5:
                        front_delta(ahead, 1 - at, 0)
                reduce(g, UNITS - 3)
                reduce(g, UNITS - 2)
                reduce(g, UNITS - 1)
                if after is not None:
                    front_mix(after)
                if ahead is not None:
                    cast_c(ahead, 1 - at, 0)
                    cast_b(ahead, 1 - at, 2)
                project(g)

            pe.sem_inc(attn_done, 1)
            pe.sem_inc(gexp_mm, 1)
            pe.sem_inc(b_copied, 1)
            pe.sem_inc(weighted, 1)
            pe.sem_inc(scans, RING)
            pe.sem_inc(reduced, RING)
            pe.sem_inc(dbx_done, BRING * NT - 1)
            in_pairs(pe, front, scan)

        @block.scalar
        def _(act):
            def front_gates(g):
                act.wait_ge(gexp_mm, g + 2)
                nc.scalar.copy(gexp[:, :], ps_w[:, 1, :]).then_inc(gexp_done, 1)

            def front_silu(g, at):
                act.wait_ge(x_mm, NT * g + NT)
                for tile in range(NT):
                    last = nc.scalar.activation(xi[:, at, tile, :], ps_w[:, tile, :], ACT.Silu,
                                                bias=W["conv_b"][:, tile:tile + 1])
                last.then_inc(xi_done, 1)

            def front_z(g, at):
                act.wait_ge(z_mm, g + 1)
                nc.scalar.copy(zs[:, at, :, :], ps_w[:, :, :]).then_inc(z_copied, 1)

            def silu_z(g, at):
                act.wait_ge(z_copied, g + 1)
                nc.scalar.activation(zs[:, at, :, :], zs[:, at, :, :], ACT.Silu).then_inc(zs_done, 1)

            def front_softplus(g):
                act.wait_ge(delta_mm, NT * g + NT)
                for tile in range(NT):
                    last = nc.scalar.activation(spa[:, tile, :], ps_w[:, tile, :], ACT.Abs,
                                                bias=W["dt_b"][:, tile:tile + 1])
                last.then_inc(sp_act, 1)
                for tile in range(NT):
                    last = nc.scalar.activation(spr[:, tile, :], ps_w[:, tile, :], ACT.Relu,
                                                bias=W["dt_b"][:, tile:tile + 1])
                last.then_inc(sp_max, 1)
                act.wait_ge(sp_act, 3 * g + 1)
                nc.scalar.activation(spa[:, :, :], spa[:, :, :], ACT.Exp, scale=-1.0).then_inc(sp_act, 1)
                act.wait_ge(sp_act, 3 * g + 2)
                nc.scalar.activation(spa[:, :, :], spa[:, :, :], ACT.Ln, bias=1.0).then_inc(sp_act, 1)

            def copy_b(g, pair):
                act.wait_ge(b_cast, g * NP2 + pair + 1)
                act.wait_ge(dbx_done, g * UNITS + NT * pair + 1)
                nc.scalar.copy(b_sb[:, pair % BRING, :, :], ps_b[:, :, :]).then_inc(b_copied, 1)

            def front(g, at):
                front_gates(g)
                front_silu(g, at)
                front_z(g, at)
                front_softplus(g)
                copy_b(g, 0)

            def scan(g, at, ahead, after):
                act.wait_ge(u_done, g + 1)
                for pair in range(NP2):
                    for tile in range(NT):
                        unit = pair * NT + tile
                        act.wait_ge(scans, g * UNITS + unit + 1)
                        for n in range(2):
                            last = nc.scalar.activation(
                                decay[:, unit % RING, n, :, 1:S], by_group(delta[:, at, tile, :])[:, :, 1:S], ACT.Exp,
                                scale=W["a"][:, tile, 2 * pair + n:2 * pair + n + 1])
                        last.then_inc(decays, 1)
                    if pair == 0 and ahead is not None:
                        front_gates(ahead)
                    if pair + 1 < NP2:
                        copy_b(g, pair + 1)
                    elif ahead is not None:
                        copy_b(ahead, 0)
                    if pair == 4 and ahead is not None:
                        front_z(ahead, 1 - at)
                    if pair == 3:
                        if ahead is not None:
                            front_silu(ahead, 1 - at)
                        silu_z(g, at)
                if ahead is not None:
                    front_softplus(ahead)

            in_pairs(act, front, scan)

        @block.gpsimd
        def _(pool):
            def spread_gates(g):
                pool.wait_ge(gexp_mm, g + 1)
                nc.gpsimd.tensor_copy(
                    gates_g[:, :, :, :],
                    W["gates"][:, bass.ds(g * GB, GB), :].unsqueeze(3).to_broadcast([P, GB, NE, R])).then_inc(copied, 1)

            def front(g, at):
                spread_gates(g)
                spread_gates(g + 1)

            def add_pair(g, unit):
                pool.wait_ge(weighted, g * UNITS + unit + 2)
                pool.wait_ge(reduced, g * UNITS + unit + 1)
                nc.gpsimd.tensor_tensor(pair_sum[:, unit // RING % 2, :], ch_sb[:, unit % RING, 0, :],
                                        ch_sb[:, unit % RING, 1, :], ALU.add).then_inc(paired, 1)

            def scan(g, at, ahead, after):
                for unit in range(UNITS):
                    pair, tile = divmod(unit, NT)
                    if unit == 0:
                        pool.wait_ge(u_done, g + 1)
                    if tile == 0:
                        pool.wait_ge(b_copied, g * NP2 + pair + 2)
                    pool.wait_ge(scans, g * UNITS + unit + 1)
                    nc.gpsimd.tensor_tensor(dbx[:, unit % RING, :, :], b_sb[:, pair % BRING, :, :],
                                            u[:, at, tile, :].unsqueeze(1).to_broadcast([P, 2, N]),
                                            ALU.mult).then_inc(dbx_done, 1)
                    if unit >= LAG and in_pair_sum(unit - LAG):
                        add_pair(g, unit - LAG)
                if after is not None:
                    spread_gates(after)
                for unit in range(UNITS - LAG, UNITS):
                    if in_pair_sum(unit):
                        add_pair(g, unit)

            in_pairs(pool, front, scan)

        @block.vector
        def _(dve):
            FRONT_LINKS = 5

            def front_mix(g):
                dve.wait_ge(a_mm, g + 1)
                dve.wait_ge(gexp_done, g + 1)
                nc.vector.tensor_tensor(mixed[:, :], ps_w[:, 0, :], gexp[:, :], ALU.mult).then_inc(mixed_done, 1)

            def front_parts(g, at, ch):
                dve.wait_ge(bc_mm, g + 1)
                split3(nc, ch, bc_parts[:, at, :], bc_mid, bc_rest, ps_w[0:96, 0, :]).then_inc(parts_done, 1)

            def front_u(g, at, ch):
                dve.wait_ge(sp_max, g + 1)
                dve.wait_ge(sp_act, 3 * g + 3)
                ch.link(nc.vector.tensor_tensor(delta[:, at, :, :], spr[:, :, :], spa[:, :, :], ALU.add))
                dve.wait_ge(xi_done, g + 1)
                nc.vector.tensor_tensor(u[:, at, :, :], delta[:, at, :, :], xi[:, at, :, :], ALU.mult).then_inc(u_done, 1)
                ch.end()

            def scan_unit(g, unit):
                dve.wait_ge(decays, g * UNITS + unit + 1)
                dve.wait_ge(dbx_done, g * UNITS + unit + BRING * NT)
                if unit >= HRING:
                    dve.wait_ge(weighted, g * UNITS + unit - HRING + 2)
                nc.vector.tensor_tensor_scan(
                    h[:, unit % HRING, :, :].rearrange("p n t -> p (n t)"),
                    decay[:, unit % RING, :, :, :].rearrange("p n b t -> p (n b t)"),
                    dbx[:, unit % RING, :, :].rearrange("p n t -> p (n t)"), 0.0, ALU.mult,
                    ALU.add).then_inc(scans, 1)

            def weigh_unit(g, unit):
                pair, tile = divmod(unit, NT)
                dve.wait_ge(scans, g * UNITS + unit + RING + 1)
                if tile == 0:
                    dve.wait_ge(c_cast, g * NP2 + pair + 1)
                dve.wait_ge(reduced, g * UNITS + unit + 1)
                nc.vector.tensor_tensor(ch_sb[:, unit % RING, :, :], h[:, unit % HRING, :, :], ps_c[:, :, :],
                                        ALU.mult).then_inc(weighted, 1)

            def first_units(g):
                scan_unit(g, 0)
                scan_unit(g, 1)
                weigh_unit(g, 0)

            def front(g, at):
                ch = Chain(dve, chain_f, g, FRONT_LINKS)
                front_mix(g)
                front_parts(g, at, ch)
                front_u(g, at, ch)
                front_mix(g + 1)
                first_units(g)

            def scan(g, at, ahead, after):
                if ahead is not None:
                    ch = Chain(dve, chain_f, ahead, FRONT_LINKS)
                for unit in range(1, UNITS):
                    if unit + 1 < UNITS:
                        scan_unit(g, unit + 1)
                    weigh_unit(g, unit)
                    if ahead is None:
                        continue
                    if unit == 9:
                        front_parts(ahead, 1 - at, ch)
                if ahead is not None:
                    front_u(ahead, 1 - at, ch)
                dve.wait_ge(reduced, g * UNITS + UNITS + RING)
                for tile in range(NT):
                    last = nc.vector.scalar_tensor_tensor(out=yd[:, tile, :], in0=xi[:, at, tile, :],
                                                          scalar=W["d_skip"][:, tile:tile + 1], in1=ps_y[:, tile, :],
                                                          op0=ALU.mult, op1=ALU.add)
                last.then_inc(y_read, 1)
                dve.wait_ge(y_read, g + 1)
                dve.wait_ge(zs_done, g + 1)
                nc.vector.tensor_tensor(yd[:, :, :], yd[:, :, :], zs[:, at, :, :], ALU.mult).then_inc(gated, 1)
                if after is not None:
                    front_mix(after)
                if ahead is not None:
                    first_units(ahead)
                dve.wait_ge(out_mm, g + 1)
                xg = xt[:, bass.ds(g * N, N)]
                nc.vector.tensor_tensor(xg, xg, ps_y[:, 0, :], ALU.add).then_inc(attn_done, 1)

            in_pairs(dve, front, scan)


def ffn0_loads(D, W):
    return [
        (W["taus"][:, 0:ND], D["condB_tauraws"].to_broadcast([P, ND])),
        (W["taus"][:, ND:ND + 1], D["tau_column"]),
        (W["taus"][:, ND + 1:ND + 2], D["L0_cond2_tau_ctx"].to_broadcast([P, 1])),
        (W["blend_t"][:, :], D["cond_1024"]), (W["pow_at"][:, :], D["c_lag"].to_broadcast([P, LAGS])),
        (W["upto_at"][:, :], D["c_upto_at"]), (W["upto_on"][:, :], D["c_upto_on"]),
        (W["from_at"][:, :], D["c_from_at"]), (W["from_on"][:, :], D["c_from_on"]),
        (W["ctx_on"][:, :], D["c_ctx_on"].to_broadcast([P, N])),
        (W["wg_x"][:, :], D["wg_x"]), (W["wg_ctx"][:, :], D["wg_ctx"]), (W["bg"][:, :], D["L0_cond2_bg"]),
        (W["wn1"][:, :], D["L0_cond2_Wn1"]), (W["bn1"][:, :], D["L0_cond2_bn1"]),
        (W["wn2"][:, :], D["cond_256"]), (W["bn2"][:, :], D["condB_bn2"]),
        (W["w_soma"][:, :], D["L0_cond2_Wsoma"]), (W["b_soma"][:, :], D["L0_cond2_bsoma"]),
        (W["w_temp"][:, :], D["L0_cond2_Wtemp"]), (W["b_temp"][:, :], D["L0_cond2_btemp"]),
        (W["w_out"][:, :], D["L0_cond2_Wout"]),
        (W["gamma"][:, :], D["L0_cond2_gamma"]), (W["beta"][:, :], D["L0_cond2_beta"]),
        (W["router"][:, :], D["L0_ffn_router_w"]),
        (W["router_b"][:, :], D["L0_ffn_router_b"].to_broadcast([P, NE])),
        (W["expert_w"][:, :, :], D["L0_ffn_expert_w"]), (W["expert_b"][:, :], D["L0_ffn_expert_b"]),
        (W["rank"][:, :], D["c_rank"].to_broadcast([P, NE])), (W["pick8"][:, :], D["c_pick"]),
    ]


def setup_ffn0(nc, W, loaded, loads):
    with ExitStack() as own:
        def tmp(name, shape, dt=F32):
            return own.enter_context(nc.sbuf_tensor(name, shape, dt))

        def sem(name):
            return own.enter_context(nc.semaphore(name))

        tau_abs = tmp("tau_abs", [P, ND + 2])
        tau_max = tmp("tau_max", [P, ND + 2])
        soft = tmp("soft", [P, ND + 2])
        rate = tmp("rate", [P, ND + 2])
        blend4 = tmp("blend4", [P, 4, ND])
        top = tmp("blend_top", [P, 1])
        lag_pow = tmp("lag_pow", [P, LAGS])
        ctx_alpha = tmp("ctx_alpha", [P, 1])
        ps_bw = own.enter_context(nc.psum_tensor("ps_bw", [P, C], F32))

        a_abs = sem("s2_abs")
        a_exp = sem("s2_exp")
        a_ln = sem("s2_ln")
        rate_done = sem("s2_rate")
        shifted = sem("s2_blend_shifted")
        b_exp = sem("s2_blend_exp")
        b_done = sem("s2_blend_done")
        bw_mm = sem("s2_bw_mm")
        bw_copied = sem("s2_bw_copied")
        upto_arg = sem("s2_upto_arg")
        exps = sem("s2_exps")
        chain_v = sem("s2_chain_v")

        block = own.enter_context(nc.Block())

        @block.scalar
        def _(act):
            act.wait_ge(loaded, 16 * len(loads))
            nc.scalar.activation(tau_abs[:, :], W["taus"][:, :], ACT.Abs).then_inc(a_abs, 1)
            nc.scalar.activation(tau_max[:, :], W["taus"][:, :], ACT.Relu).then_inc(a_abs, 1)
            act.wait_ge(a_abs, 1)
            nc.scalar.activation(soft[:, :], tau_abs[:, :], ACT.Exp, scale=-1.0).then_inc(a_exp, 1)
            act.wait_ge(a_exp, 1)
            nc.scalar.activation(soft[:, :], soft[:, :], ACT.Ln, bias=1.0).then_inc(a_ln, 1)
            act.wait_ge(shifted, 1)
            nc.scalar.activation(W["blend_t"][:, :], W["blend_t"][:, :], ACT.Exp).then_inc(b_exp, 1)
            act.wait_ge(rate_done, 1)
            nc.scalar.activation(lag_pow[:, :], W["pow_at"][:, :], ACT.Exp, scale=rate[:, ND:ND + 1]).then_inc(exps, 1)
            nc.scalar.activation(W["from_start"][:, :], W["from_at"][:, :], ACT.Exp,
                                 scale=rate[:, ND:ND + 1]).then_inc(exps, 1)
            nc.scalar.activation(ctx_alpha[:, :], rate[:, ND + 1:ND + 2], ACT.Exp).then_inc(exps, 1)
            act.wait_ge(upto_arg, 1)
            nc.scalar.activation(W["upto_end"][:, :, :], W["upto_end"][:, :, :], ACT.Exp).then_inc(exps, 1)

        @block.tensor
        def _(pe):
            pe.wait_ge(b_done, 1)
            nc.tensor.matmul(ps_bw[:, :], blend4[:, :, :].rearrange("p k d -> p (k d)"), W["ident"][:, :],
                             start=True, stop=True).then_inc(bw_mm, 1)

        @block.gpsimd
        def _(pool):
            nc.gpsimd.memset(W["mw96"][:, :, :, :], 0.0)
            nc.gpsimd.memset(W["neg_half"][:, :], -0.5)

        @block.vector
        def _(dve):
            ch = Chain(dve, chain_v, 0, 5)
            dve.wait_ge(loaded, 16 * len(loads))
            ch.link(nc.vector.tensor_reduce(top[:, :], W["blend_t"][:, :], X, ALU.max))
            nc.vector.tensor_scalar(W["blend_t"][:, :], W["blend_t"][:, :], top[:, 0:1], None, ALU.subtract).then_inc(shifted, 1)
            dve.wait_ge(a_abs, 2)
            dve.wait_ge(a_ln, 1)
            nc.vector.scalar_tensor_tensor(out=rate[:, :], in0=tau_max[:, :], scalar=-1.0, in1=soft[:, :],
                                           op0=ALU.mult, op1=ALU.subtract).then_inc(rate_done, 1)
            dve.wait_ge(rate_done, 1)
            nc.vector.tensor_tensor(W["upto_end"][:, :, :], W["upto_at"][:, :].unsqueeze(2).to_broadcast([P, CHUNKS, ND]),
                                    rate[:, 0:ND].unsqueeze(1).to_broadcast([P, CHUNKS, ND]),
                                    ALU.mult).then_inc(upto_arg, 1)
            dve.wait_ge(b_exp, 1)
            ch.link(nc.vector.tensor_reduce(top[:, :], W["blend_t"][:, :], X, ALU.add))
            ch.link(nc.vector.reciprocal(top[:, :], top[:, :]))
            ch.link(nc.vector.tensor_scalar(W["blend_t"][:, :], W["blend_t"][:, :], top[:, 0:1], None, ALU.mult))
            nc.vector.tensor_copy(blend4[:, :, :], W["blend_t"][:, :].unsqueeze(1).to_broadcast([P, 4, ND])).then_inc(b_done, 1)
            dve.wait_ge(bw_mm, 1)
            nc.vector.tensor_copy(W["bw"][:, :], ps_bw[:, :]).then_inc(bw_copied, 1)
            dve.wait_ge(exps, 4)
            dve.wait_ge(bw_copied, 1)
            ch.link(nc.vector.tensor_tensor(
                W["bw_lag"][:, :, :], W["bw"][0:ND, :].unsqueeze(1).to_broadcast([ND, LAGS, C]),
                lag_pow[0:ND, :].unsqueeze(2).to_broadcast([ND, LAGS, C]), ALU.mult))
            nc.vector.tensor_tensor(W["from_start"][:, :], W["from_start"][:, :], W["from_on"][:, :], ALU.mult)
            nc.vector.tensor_scalar(W["ctx_decay"][:, :], W["ctx_on"][:, :], ctx_alpha[:, 0:1], None, ALU.mult)
            nc.vector.tensor_tensor(W["upto_end"][:, :, :], W["upto_end"][:, :, :],
                                    W["upto_on"][:, :].unsqueeze(2).to_broadcast([P, CHUNKS, ND]), ALU.mult)
            ch.end()


def split3(nc, ch, parts, mid, rest, src):
    ch.link(nc.vector.tensor_copy(parts[:, :], src))
    ch.link(nc.vector.tensor_tensor(rest[:, :], src, parts[:, :], ALU.subtract))
    ch.link(nc.vector.tensor_copy(mid[:, :], rest[:, :]))
    ch.link(nc.vector.tensor_copy(parts[32:64, :], mid[32:64, :]))
    return nc.vector.tensor_tensor(parts[64:96, :], rest[64:96, :], mid[64:96, :], ALU.subtract)


def traces_and_experts(nc, W, xt, later):
    with ExitStack() as own:
        def sb(name, shape, dt=F32):
            return own.enter_context(nc.sbuf_tensor(name, shape, dt))

        def sem(name):
            return own.enter_context(nc.semaphore(name))

        ps = own.enter_context(nc.psum_tensor("ps2", [P, 8, N], F32))
        h1 = sb("h1", [32, N])
        soma = sb("soma", [P, N])
        ctx_t = sb("ctx_t", [P, N])
        mod_t = sb("mod_t", [ND, N])
        mod_s = sb("mod_s", [P, GB, ND])
        wg = sb("wg", [P, N])
        gated_t = sb("gated_t", [P, N])
        gated = sb("gated", [P, GB, C])
        upto = sb("upto", [P, 2, CHUNKS, ND])
        states = sb("states", [P, 2, 4, C])
        lagged = sb("lagged", [P, 2, N])
        lag_sum = sb("lag_sum", [P, N])
        temp_t = sb("temp_t", [P, N])
        gate = sb("gate", [P, N])
        prod = sb("prod", [P, N])
        mean = sb("mean", [P, GB])
        var = sb("var", [P, GB])
        rstd = sb("rstd", [P, GB])
        xc = sb("xc", [P, GB, C])
        sq = sb("sq", [P, GB, C])
        xn = sb("xn", [P, GB, C])
        yt = sb("yt", [P, N])
        lg = sb("lg", [P, GB, NE])
        ex = sb("ex", [P, GB, NE])
        hot = sb("hot", [P, GB, NE])
        top = sb("top2", [P, GB])
        den = sb("den", [P, GB])
        first = sb("first", [P, GB])
        m_parts = sb("m_parts", [96, N], BF16)
        m_mid = sb("m_mid", [96, N], BF16)
        m_rest = sb("m_rest", [96, N])
        mw_t = sb("mw_t", [NE, N])
        ym = sb("ym", [P, 2, N])

        names = ("ctx_done h1_mm h1_done wg_mm wg_done mod_mm sig_done mod_done gated_done tokens_mm tokens_done "
                 "mods_mm mods_done upto_done states_mm states_done lag_mm lag_done lag_added temp_mm temp_done "
                 "soma_mm soma_done gate_mm gate_done prod_done out_mm centred squared var_done "
                 "rstd_done xn_done xn_mm yt_done router_mm shifted_r exped_r mw_done mw_copied mw_mm m_split "
                 "mask_mm masked experts_mm x2_done chain_v2").split()
        Z = {n: sem("p2_" + n) for n in names}
        block = own.enter_context(nc.Block())

        def chunks(ap, start, stop):
            return ap.rearrange("p (k r) -> p k r", r=LAGS)[:, :, start:stop]

        def group_of(g):
            return xt[:, bass.ds(g * N, N)]

        def lag_bank(lag):
            return ps[:, lag % 2, 0:(N // LAGS) * (LAGS - lag)].rearrange("p (k r) -> p k r", r=LAGS - lag)

        @block.sync
        def _(sp):
            for sem_loads in later:
                load_all(sp, *sem_loads)

        @block.tensor
        def _(pe):
            def hidden_mod(g):
                if not isinstance(g, int):
                    pe.wait_ge(Z["soma_done"], g)
                nc.tensor.matmul(ps[0:32, 5, :], W["wn1"][:, :], group_of(g), start=True, stop=True).then_inc(Z["h1_mm"], 1)

            def context_gate(g):
                nc.tensor.matmul(ps[:, 2, :], W["wg_x"][:, :], group_of(g), start=True, stop=False)
                pe.wait_ge(Z["ctx_done"], g + 1)
                pe.wait_ge(Z["h1_done"], g + 1)
                nc.tensor.matmul(ps[:, 2, :], W["wg_ctx"][:, :], ctx_t[:, :], start=False, stop=True).then_inc(Z["wg_mm"], 1)

            def modulation():
                nc.tensor.matmul(ps[0:ND, 5, :], W["wn2"][:, :], h1[:, :], start=True, stop=True).then_inc(Z["mod_mm"], 1)

            def gated_tokens(g):
                pe.wait_ge(Z["gated_done"], g + 1)
                for b in range(GB):
                    last = nc.tensor.transpose(ps[:, 3, b * C:(b + 1) * C], gated_t[:, b * S:(b + 1) * S], W["ident"][:, :])
                last.then_inc(Z["tokens_mm"], 1)

            def mod_tokens(g):
                pe.wait_ge(Z["mod_done"], g + 1)
                for b in range(GB):
                    last = nc.tensor.matmul(ps[:, 5, b * ND:(b + 1) * ND], mod_t[:, b * S:(b + 1) * S],
                                            W["ident"][0:ND, 0:ND], start=True, stop=True)
                last.then_inc(Z["mods_mm"], 1)

            def lag_product(g, lag):
                if lag >= 2:
                    pe.wait_ge(Z["lag_done"], g * LAGS + lag - 1)
                nc.tensor.matmul(lag_bank(lag), W["bw_lag"][:, lag, :], chunks(mod_t[:, :], 0, LAGS - lag),
                                 start=True, stop=True).then_inc(Z["lag_mm"], 1)

            def states_in(g, b):
                if b == 0:
                    pe.wait_ge(Z["tokens_done"], g + 1)
                pe.wait_ge(Z["upto_done"], g * GB + b + 1)
                if b >= 2:
                    pe.wait_ge(Z["states_done"], g * GB + b - 1)
                for j in range(4):
                    last = nc.tensor.matmul(
                        ps[:, 2 + b % 2, j * C:(j + 1) * C],
                        upto[:, b % 2, 4 * j:4 * j + 4, :].rearrange("s k d -> s (k d)"), gated[:, b, :],
                        start=True, stop=True)
                last.then_inc(Z["states_mm"], 1)

            def gather(g, b):
                pe.wait_ge(Z["states_done"], g * GB + b + 1)
                for j in range(4):
                    at = b * S + j * 4 * LAGS
                    last = nc.tensor.matmul(ps[:, 4, at:at + 4 * LAGS], states[:, b % 2, j, :], W["from_start"][:, :],
                                            start=True, stop=True)
                last.then_inc(Z["temp_mm"], 1)

            def soma_in(g):
                nc.tensor.matmul(ps[:, 5, :], W["w_soma"][:, :], group_of(g), start=True, stop=True).then_inc(Z["soma_mm"], 1)

            def front(g):
                hidden_mod(g)
                context_gate(g)
                modulation()
                gated_tokens(g)
                mod_tokens(g)
                lag_product(g, 0)
                lag_product(g, 1)
                states_in(g, 0)
                lag_product(g, 2)
                states_in(g, 1)
                gather(g, 0)
                lag_product(g, 3)
                states_in(g, 2)
                lag_product(g, 4)
                gather(g, 1)
                lag_product(g, 5)
                states_in(g, 3)
                lag_product(g, 6)
                gather(g, 2)
                lag_product(g, 7)
                gather(g, 3)
                soma_in(g)

            def gate_in(g):
                pe.wait_ge(Z["temp_done"], g + 1)
                nc.tensor.matmul(ps[:, 6, :], W["w_temp"][:, :], temp_t[:, :], start=True, stop=True).then_inc(Z["gate_mm"], 1)

            def outwards(g):
                pe.wait_ge(Z["prod_done"], g + 1)
                for b in range(GB):
                    last = nc.tensor.matmul(ps[:, 6, b * C:(b + 1) * C], prod[:, b * S:(b + 1) * S], W["w_out"][:, :],
                                            start=True, stop=True)
                last.then_inc(Z["out_mm"], 1)

            def to_channels(g):
                pe.wait_ge(Z["xn_done"], g + 1)
                for b in range(GB):
                    last = nc.tensor.transpose(ps[:, 6, b * S:(b + 1) * S], xn[:, b, :], W["ident"][:, :])
                last.then_inc(Z["xn_mm"], 1)

            def router(g):
                pe.wait_ge(Z["yt_done"], g + 1)
                for b in range(GB):
                    last = nc.tensor.matmul(ps[:, 6, b * NE:(b + 1) * NE], yt[:, b * S:(b + 1) * S], W["router"][:, :],
                                            start=True, stop=True)
                last.then_inc(Z["router_mm"], 1)

            def masks_to_channels(g):
                pe.wait_ge(Z["mw_copied"], g + 1)
                for b in range(GB):
                    last = nc.tensor.transpose(ps[0:96, 6, b * S:(b + 1) * S],
                                               W["mw96"][:, b, :, :].rearrange("p k e -> p (k e)"), W["ident"][:, :])
                last.then_inc(Z["mw_mm"], 1)

            def experts(g, ahead):
                def mask(e):
                    if e >= 2:
                        pe.wait_ge(Z["masked"], g * NE + e - 1)
                    nc.tensor.matmul(ps[:, e % 2, :], W["pick8"][:, e:e + 1].to_broadcast([96, P]), m_parts[:, :],
                                     start=True, stop=True).then_inc(Z["mask_mm"], 1)

                pe.wait_ge(Z["m_split"], g + 1)
                if ahead is not None:
                    pe.wait_ge(Z["lag_done"], ahead * LAGS + LAGS)
                mask(0)
                nc.tensor.matmul(ps[:, 7, :], W["expert_b"][:, :], mw_t[:, :], start=True, stop=False)
                for e in range(NE):
                    if e + 1 < NE:
                        mask(e + 1)
                    pe.wait_ge(Z["masked"], g * NE + e + 1)
                    last = nc.tensor.matmul(ps[:, 7, :], W["expert_w"][:, e, :], ym[:, e % 2, :],
                                            start=False, stop=(e == NE - 1))
                last.then_inc(Z["experts_mm"], 1)

            def body(g, ahead):
                if ahead is None:
                    gate_in(g)
                    outwards(g)
                    to_channels(g)
                    router(g)
                    masks_to_channels(g)
                    experts(g, ahead)
                    return
                hidden_mod(ahead)
                gate_in(g)
                context_gate(ahead)
                modulation()
                outwards(g)
                gated_tokens(ahead)
                mod_tokens(ahead)
                lag_product(ahead, 0)
                lag_product(ahead, 1)
                states_in(ahead, 0)
                lag_product(ahead, 2)
                states_in(ahead, 1)
                lag_product(ahead, 3)
                gather(ahead, 0)
                to_channels(g)
                states_in(ahead, 2)
                router(g)
                lag_product(ahead, 4)
                gather(ahead, 1)
                lag_product(ahead, 5)
                states_in(ahead, 3)
                masks_to_channels(g)
                soma_in(ahead)
                lag_product(ahead, 6)
                gather(ahead, 2)
                lag_product(ahead, 7)
                gather(ahead, 3)
                experts(g, ahead)

            in_turns(pe, front, body)

        @block.scalar
        def _(act):
            def hidden_mod(g):
                act.wait_ge(Z["h1_mm"], g + 1)
                nc.scalar.activation(h1[:, :], ps[0:32, 5, :], ACT.Gelu, bias=W["bn1"][:, 0:1]).then_inc(Z["h1_done"], 1)

            def context_gate(g):
                act.wait_ge(Z["wg_mm"], g + 1)
                nc.scalar.activation(wg[:, :], ps[:, 2, :], ACT.Sigmoid, bias=W["bg"][:, 0:1]).then_inc(Z["wg_done"], 1)

            def modulation(g):
                act.wait_ge(Z["mod_mm"], g + 1)
                nc.scalar.activation(mod_t[:, :], ps[0:ND, 5, :], ACT.Sigmoid, bias=W["bn2"][:, 0:1]).then_inc(Z["sig_done"], 1)

            def gated_tokens(g):
                act.wait_ge(Z["tokens_mm"], g + 1)
                nc.scalar.copy(gated[:, :, :].rearrange("p b c -> p (b c)"), ps[:, 3, :]).then_inc(Z["tokens_done"], 1)

            def soma_in(g):
                act.wait_ge(Z["soma_mm"], g + 1)
                nc.scalar.activation(soma[:, :], ps[:, 5, :], ACT.Gelu, bias=W["b_soma"][:, 0:1]).then_inc(Z["soma_done"], 1)

            def front(g):
                hidden_mod(g)
                context_gate(g)
                modulation(g)
                gated_tokens(g)
                soma_in(g)

            def body(g, ahead):
                if ahead is not None:
                    hidden_mod(ahead)
                act.wait_ge(Z["gate_mm"], g + 1)
                nc.scalar.activation(gate[:, :], ps[:, 6, :], ACT.Sigmoid, bias=W["b_temp"][:, 0:1]).then_inc(Z["gate_done"], 1)
                if ahead is not None:
                    context_gate(ahead)
                    modulation(ahead)
                    gated_tokens(ahead)
                act.wait_ge(Z["centred"], g + 1)
                nc.scalar.activation(sq[:, :, :], xc[:, :, :], ACT.Square).then_inc(Z["squared"], 1)
                act.wait_ge(Z["xn_mm"], g + 1)
                nc.scalar.activation(yt[:, :], ps[:, 6, :], ACT.Identity, bias=W["beta"][:, 0:1],
                                     scale=W["gamma"][:, 0:1]).then_inc(Z["yt_done"], 1)
                act.wait_ge(Z["shifted_r"], g + 1)
                nc.scalar.activation(ex[:, :, :], ex[:, :, :], ACT.Exp).then_inc(Z["exped_r"], 1)
                act.wait_ge(Z["mw_done"], g + 1)
                nc.scalar.copy(W["mw96"][:, :, :, 0:NE],
                               hot[:, :, :].unsqueeze(2).to_broadcast([P, GB, 3, NE])).then_inc(Z["mw_copied"], 1)
                if ahead is not None:
                    soma_in(ahead)

            in_turns(act, front, body)

        @block.gpsimd
        def _(pool):
            def modulate(g, b):
                if b == 0:
                    pool.wait_ge(Z["mods_done"], g + 1)
                if b >= 2:
                    pool.wait_ge(Z["states_mm"], g * GB + b - 1)
                nc.gpsimd.tensor_tensor(upto[:, b % 2, :, :], W["upto_end"][:, :, :],
                                        mod_s[:, b, :].unsqueeze(1).to_broadcast([P, CHUNKS, ND]),
                                        ALU.mult).then_inc(Z["upto_done"], 1)

            def add_lag(g, lag):
                pool.wait_ge(Z["lag_done"], g * LAGS + lag + 1)
                if lag >= 2:
                    pool.wait_ge(Z["lag_added"], g * (LAGS - 1) + lag - 1)
                nc.gpsimd.tensor_tensor(chunks(lag_sum[:, :], lag, LAGS), chunks(lag_sum[:, :], lag, LAGS),
                                        chunks(lagged[:, lag % 2, :], 0, LAGS - lag), ALU.add).then_inc(Z["lag_added"], 1)

            def rstd_of(g):
                pool.wait_ge(Z["var_done"], g + 1)
                nc.gpsimd.tensor_tensor(rstd[:, :], var[:, :], W["neg_half"][:, :], ALU.pow).then_inc(Z["rstd_done"], 1)

            def averages(g, between):
                modulate(g, 0)
                modulate(g, 1)
                add_lag(g, 1)
                between()
                modulate(g, 2)
                for lag in (2, 3):
                    add_lag(g, lag)
                modulate(g, 3)
                for lag in range(4, LAGS):
                    add_lag(g, lag)

            def body(g, ahead):
                if ahead is None:
                    rstd_of(g)
                else:
                    averages(ahead, lambda: rstd_of(g))

            in_turns(pool, lambda g: averages(g, lambda: None), body)

        @block.vector
        def _(dve):
            def context(g):
                nc.vector.tensor_tensor_scan(ctx_t[:, :], W["ctx_decay"][:, :], group_of(g), 0.0, ALU.mult,
                                             ALU.add).then_inc(Z["ctx_done"], 1)

            def gated_in(g):
                dve.wait_ge(Z["wg_done"], g + 1)
                nc.vector.tensor_tensor(gated_t[:, :], group_of(g), wg[:, :], ALU.mult).then_inc(Z["gated_done"], 1)
                dve.wait_ge(Z["sig_done"], g + 1)
                nc.vector.tensor_scalar(mod_t[:, :], mod_t[:, :], 0.5, None, ALU.add).then_inc(Z["mod_done"], 1)
                dve.wait_ge(Z["mods_mm"], g + 1)
                nc.vector.tensor_copy(mod_s[:, :, :], ps[:, 5, 0:GB * ND].rearrange("p (b d) -> p b d", b=GB)
                                      ).then_inc(Z["mods_done"], 1)

            def weigh_lag(g, lag):
                dve.wait_ge(Z["lag_mm"], g * LAGS + lag + 1)
                if lag >= 3:
                    dve.wait_ge(Z["lag_added"], g * (LAGS - 1) + lag - 2)
                to = lag_sum[:, :] if lag == 0 else lagged[:, lag % 2, :]
                nc.vector.tensor_tensor(chunks(to, 0, LAGS - lag), lag_bank(lag), chunks(gated_t[:, :], 0, LAGS - lag),
                                        ALU.mult).then_inc(Z["lag_done"], 1)

            def blend_states(g, b):
                dve.wait_ge(Z["states_mm"], g * GB + b + 1)
                if b >= 2:
                    dve.wait_ge(Z["temp_mm"], g * GB + b - 1)
                nc.vector.tensor_tensor(
                    states[:, b % 2, :, :], ps[:, 2 + b % 2, :].rearrange("p (j c) -> p j c", c=C),
                    W["bw"][:, :].unsqueeze(1).to_broadcast([P, 4, C]), ALU.mult).then_inc(Z["states_done"], 1)

            def temporal(g):
                dve.wait_ge(Z["lag_added"], g * (LAGS - 1) + LAGS - 1)
                dve.wait_ge(Z["temp_mm"], g * GB + GB)
                nc.vector.tensor_tensor(temp_t[:, :], lag_sum[:, :], ps[:, 4, :], ALU.add).then_inc(Z["temp_done"], 1)

            def front(g):
                context(g)
                gated_in(g)
                weigh_lag(g, 0)
                weigh_lag(g, 1)
                blend_states(g, 0)
                weigh_lag(g, 2)
                blend_states(g, 1)
                weigh_lag(g, 3)
                blend_states(g, 2)
                weigh_lag(g, 4)
                weigh_lag(g, 5)
                blend_states(g, 3)
                weigh_lag(g, 6)
                weigh_lag(g, 7)
                temporal(g)

            top_b = top[:, :].unsqueeze(2).to_broadcast([P, GB, NE])

            def gate_soma(g):
                dve.wait_ge(Z["soma_done"], g + 1)
                dve.wait_ge(Z["gate_done"], g + 1)
                nc.vector.tensor_tensor(prod[:, :], soma[:, :], gate[:, :], ALU.mult).then_inc(Z["prod_done"], 1)

            def centre(g, ch):
                dve.wait_ge(Z["out_mm"], g + 1)
                o = ps[:, 6, :].rearrange("p (b c) -> p b c", b=GB)
                ch.link(nc.vector.tensor_reduce(mean[:, :], o, X, ALU.add))
                ch.link(nc.vector.tensor_scalar(mean[:, :], mean[:, :], 1.0 / C, None, ALU.mult))
                nc.vector.tensor_tensor(xc[:, :, :], o, mean[:, :].unsqueeze(2).to_broadcast([P, GB, C]),
                                        ALU.subtract).then_inc(Z["centred"], 1)

            def variance(g, ch):
                dve.wait_ge(Z["squared"], g + 1)
                ch.link(nc.vector.tensor_reduce(var[:, :], sq[:, :, :], X, ALU.add))
                nc.vector.tensor_scalar(var[:, :], var[:, :], 1.0 / C, LN_EPS, ALU.mult, ALU.add).then_inc(Z["var_done"], 1)

            def normalise(g):
                dve.wait_ge(Z["rstd_done"], g + 1)
                nc.vector.tensor_tensor(xn[:, :, :], xc[:, :, :], rstd[:, :].unsqueeze(2).to_broadcast([P, GB, C]),
                                        ALU.mult).then_inc(Z["xn_done"], 1)

            def logits(g, ch):
                dve.wait_ge(Z["router_mm"], g + 1)
                ch.link(nc.vector.tensor_tensor(lg[:, :, :], ps[:, 6, 0:GB * NE].rearrange("p (b e) -> p b e", b=GB),
                                                W["router_b"][:, :].unsqueeze(1).to_broadcast([P, GB, NE]), ALU.add))
                ch.link(nc.vector.tensor_reduce(top[:, :], lg[:, :, :], X, ALU.max))
                nc.vector.tensor_tensor(ex[:, :, :], lg[:, :, :], top_b, ALU.subtract).then_inc(Z["shifted_r"], 1)

            def best(ch):
                ch.link(nc.vector.tensor_tensor(hot[:, :, :], lg[:, :, :], top_b, ALU.is_equal))
                ch.link(nc.vector.tensor_tensor(hot[:, :, :], hot[:, :, :],
                                                W["rank"][:, :].unsqueeze(1).to_broadcast([P, GB, NE]), ALU.mult))
                ch.link(nc.vector.tensor_reduce(first[:, :], hot[:, :, :], X, ALU.max))
                ch.link(nc.vector.tensor_tensor(hot[:, :, :], hot[:, :, :],
                                                first[:, :].unsqueeze(2).to_broadcast([P, GB, NE]), ALU.is_equal))

            def weights(g, ch):
                dve.wait_ge(Z["exped_r"], g + 1)
                ch.link(nc.vector.tensor_reduce(den[:, :], ex[:, :, :], X, ALU.add))
                ch.link(nc.vector.reciprocal(den[:, :], den[:, :]))
                nc.vector.tensor_tensor(hot[:, :, :], hot[:, :, :], den[:, :].unsqueeze(2).to_broadcast([P, GB, NE]),
                                        ALU.mult).then_inc(Z["mw_done"], 1)

            def split_masks(g, ch):
                dve.wait_ge(Z["mw_mm"], g + 1)
                nc.vector.tensor_copy(mw_t[:, :], ps[0:NE, 6, :])
                split3(nc, ch, m_parts, m_mid, m_rest, ps[0:96, 6, :]).then_inc(Z["m_split"], 1)

            def experts(g, ahead):
                for e in range(NE):
                    if e == 2 and ahead is not None:
                        temporal(ahead)
                    dve.wait_ge(Z["mask_mm"], g * NE + e + 1)
                    nc.vector.tensor_tensor(ym[:, e % 2, :], yt[:, :], ps[:, e % 2, :],
                                            ALU.mult).then_inc(Z["masked"], 1)
                dve.wait_ge(Z["experts_mm"], g + 1)
                nc.vector.tensor_tensor(group_of(g), group_of(g), ps[:, 7, :], ALU.add).then_inc(Z["x2_done"], 1)

            def body(g, ahead):
                ch = Chain(dve, Z["chain_v2"], g, 15)
                if ahead is None:
                    gate_soma(g)
                    centre(g, ch)
                    variance(g, ch)
                    normalise(g)
                    logits(g, ch)
                    best(ch)
                    weights(g, ch)
                    split_masks(g, ch)
                    experts(g, ahead)
                    ch.end()
                    return
                context(ahead)
                gate_soma(g)
                gated_in(ahead)
                centre(g, ch)
                weigh_lag(ahead, 0)
                weigh_lag(ahead, 1)
                variance(g, ch)
                blend_states(ahead, 0)
                weigh_lag(ahead, 2)
                normalise(g)
                blend_states(ahead, 1)
                weigh_lag(ahead, 3)
                logits(g, ch)
                best(ch)
                blend_states(ahead, 2)
                weights(g, ch)
                weigh_lag(ahead, 4)
                weigh_lag(ahead, 5)
                blend_states(ahead, 3)
                split_masks(g, ch)
                weigh_lag(ahead, 6)
                weigh_lag(ahead, 7)
                experts(g, ahead)
                ch.end()

            in_turns(dve, front, body)


def attention_loads(D, W):
    return [
        (W["lap"][:, :], D["c_lap"]), (W["z"][:, 0, :], D["condB_zX"].to_broadcast([P, NB])),
        (W["z"][:, 1, :], D["condB_zY"].to_broadcast([P, NB])), (W["z"][:, 2, :], D["condB_zR"].to_broadcast([P, NB])),
        (W["w_qkv"][:, :], D["L1_attn_in_proj_weight"]), (W["b_qkv"][:, :], D["L1_attn_in_proj_bias"]),
        (W["scale"][:, :], D["L1_attn_logit_scale"]), (W["head"][:, :], D["L1_attn_head_scale"]),
        (W["w_o"][:, :], D["L1_attn_out_w"]), (W["b_o"][:, :], D["L1_attn_out_b"]),
        (W["to_heads"][:, :, :], D["c_to_heads"]), (W["from_heads"][:, :, :], D["c_from_heads"]), (W["head_of"][:, :], D["c_head_of"]),
        (W["quarter_of"][:, :], D["c_quarter_of"]),
        (W["v_block"][:, :], D["c_v_block"]),
    ]


def setup_attention(nc, W, loaded, loads):
    with ExitStack() as own:
        def sem(name):
            return own.enter_context(nc.semaphore(name))

        capped = sem("s3_capped")
        scaled = sem("s3_scaled")
        block = own.enter_context(nc.Block())

        @block.vector
        def _(dve):
            dve.wait_ge(loaded, 16 * len(loads))
            nc.vector.tensor_scalar(W["scale"][:, :], W["scale"][:, :], LOGIT_SCALE_MAX, None, ALU.min).then_inc(capped, 1)
            nc.vector.tensor_tensor(W["v_bias"][:, :], W["b_qkv"][:, 2:3], W["head"][:, :], ALU.mult)

        @block.scalar
        def _(act):
            act.wait_ge(capped, 1)
            nc.scalar.activation(W["scale"][:, :], W["scale"][:, :], ACT.Exp).then_inc(scaled, 1)


def diffusion_and_qk(nc, W, xt, du_p, q_p, k_p):
    with ExitStack() as own:
        def sb(name, shape, dt=F32):
            return own.enter_context(nc.sbuf_tensor(name, shape, dt))

        ps = own.enter_context(nc.psum_tensor("ps3", [P, 8, N], F32))
        w = sb("stencil", [P, GB, S])
        du = sb("du", [P, GB, S])
        react = sb("react", [P, GB, S])
        qk = sb("qk", [P, 2, N])
        qk_sq = sb("qk_sq", [P, 2, N])
        norm = sb("norm", [P, S])
        names = ("lap_mm chain_a chain_b du_done qk_mm qk_copied qk_squared norm_mm rooted inverted spread_mm "
                 "qk_kept du_kept").split()
        Z = {n: own.enter_context(nc.semaphore("p3_" + n)) for n in names}
        block = own.enter_context(nc.Block())

        @block.tensor
        def _(pe):
            def laplace(g):
                nc.tensor.matmul(ps[:, 0, :], W["lap"][:, :], xt[:, bass.ds(g * N, N)],
                                 start=True, stop=True).then_inc(Z["lap_mm"], 1)

            def project(g):
                pe.wait_ge(Z["du_done"], g + 1)
                for j in range(2):
                    nc.tensor.matmul(ps[:, 1 + j, :], W["w_qkv"][:, j * C:(j + 1) * C],
                                     du[:, :, :].rearrange("p b t -> p (b t)"),
                                     start=True, stop=True).then_inc(Z["qk_mm"], 1)

            def norms(g):
                pe.wait_ge(Z["qk_squared"], 2 * g + 2)
                for b in range(GB):
                    for j in range(2):
                        last = nc.tensor.matmul(ps[32 * b:32 * b + 32, 7, 0:S], W["to_heads"][:, j, :],
                                                qk_sq[:, j, b * S:(b + 1) * S], start=(j == 0), stop=(j == 1))
                last.then_inc(Z["norm_mm"], 1)

            def spread(g):
                pe.wait_ge(Z["inverted"], g + 1)
                for j in range(2):
                    for b in range(GB):
                        rows = slice(32 * b, 32 * b + 32)
                        last = nc.tensor.matmul(ps[:, 3 + b, j * S:(j + 1) * S], W["from_heads"][rows, j, :],
                                                norm[rows, :], start=True, stop=True)
                last.then_inc(Z["spread_mm"], 1)

            def front(g):
                laplace(g)
                project(g)

            def body(g, ahead):
                if ahead is not None:
                    laplace(ahead)
                norms(g)
                spread(g)
                if ahead is not None:
                    pe.wait_ge(Z["qk_copied"], 2 * g + 2)
                    project(ahead)

            in_turns(pe, front, body)

        @block.scalar
        def _(act):
            def squares(g):
                for j in range(2):
                    act.wait_ge(Z["qk_mm"], 2 * g + j + 1)
                    nc.scalar.activation(qk_sq[:, j, :], ps[:, 1 + j, :], ACT.Square,
                                         bias=W["b_qkv"][:, j:j + 1]).then_inc(Z["qk_squared"], 1)

            def copies(g):
                for j in range(2):
                    nc.scalar.activation(qk[:, j, :], ps[:, 1 + j, :], ACT.Identity,
                                         bias=W["b_qkv"][:, j:j + 1]).then_inc(Z["qk_copied"], 1)

            def front(g):
                squares(g)
                copies(g)

            def body(g, ahead):
                act.wait_ge(Z["norm_mm"], g + 1)
                nc.scalar.activation(norm[:, :], ps[:, 7, 0:S], ACT.Sqrt).then_inc(Z["rooted"], 1)
                if ahead is not None:
                    squares(ahead)
                    act.wait_ge(Z["qk_kept"], g + 1)
                    copies(ahead)

            in_turns(act, front, body)

        @block.gpsimd
        def _(pool):
            def keep_du(g):
                pool.wait_ge(Z["du_done"], g + 1)
                nc.gpsimd.tensor_copy(by_position(du_p, g), du[:, :, :]).then_inc(Z["du_kept"], 1)

            def body(g, ahead):
                if ahead is not None:
                    keep_du(ahead)

            in_turns(pool, keep_du, body)

        @block.vector
        def _(dve):
            def z(k, g):
                return W["z"][:, k, bass.ds(g * GB, GB)].unsqueeze(2).to_broadcast([P, GB, S])

            def stencil(g, ch):
                x = by_group(xt[:, bass.ds(g * N, N)])
                nc.vector.tensor_tensor(w[:, :, 1:S - 1], x[:, :, 0:S - 2], x[:, :, 2:S], ALU.add)
                nc.vector.tensor_scalar(w[:, :, 0:1], x[:, :, 1:2], 2.0, None, ALU.mult)
                ch.link(nc.vector.tensor_scalar(w[:, :, S - 1:S], x[:, :, S - 2:S - 1], 2.0, None, ALU.mult))
                nc.vector.scalar_tensor_tensor(out=react[:, :, :], in0=x, scalar=1.0, in1=x,
                                               op0=ALU.subtract, op1=ALU.mult)
                ch.link(nc.vector.scalar_tensor_tensor(out=w[:, :, :], in0=x, scalar=-2.0, in1=w[:, :, :],
                                                       op0=ALU.mult, op1=ALU.add))
                ch.link(nc.vector.tensor_tensor(w[:, :, :], w[:, :, :], z(1, g), ALU.mult))
                ch.link(nc.vector.tensor_tensor(react[:, :, :], react[:, :, :], z(2, g), ALU.mult))

            def step(g, ch):
                dve.wait_ge(Z["lap_mm"], g + 1)
                ch.link(nc.vector.tensor_tensor(du[:, :, :], by_group(ps[:, 0, :]), z(0, g), ALU.mult))
                ch.link(nc.vector.tensor_tensor(du[:, :, :], du[:, :, :], w[:, :, :], ALU.add))
                nc.vector.tensor_tensor(du[:, :, :], du[:, :, :], react[:, :, :], ALU.subtract).then_inc(Z["du_done"], 1)

            def front(g):
                ch = Chain(dve, Z["chain_a"], g, 6)
                stencil(g, ch)
                step(g, ch)
                ch.end()

            def body(g, ahead):
                if ahead is not None:
                    ch = Chain(dve, Z["chain_a"], ahead, 6)
                    dve.wait_ge(Z["du_done"], g + 1)
                    stencil(ahead, ch)
                part = Chain(dve, Z["chain_b"], g, 2)
                dve.wait_ge(Z["rooted"], g + 1)
                part.link(nc.vector.tensor_scalar(norm[:, :], norm[:, :], L2_EPS, None, ALU.max))
                nc.vector.reciprocal(norm[:, :], norm[:, :]).then_inc(Z["inverted"], 1)
                if ahead is not None:
                    dve.wait_ge(Z["qk_mm"], 2 * g + 2)
                    dve.wait_ge(Z["du_kept"], g + 1)
                    step(ahead, ch)
                    ch.end()
                dve.wait_ge(Z["spread_mm"], g + 1)
                dve.wait_ge(Z["qk_copied"], 2 * g + 2)
                part.link(nc.vector.scalar_tensor_tensor(out=by_position(q_p, g), in0=by_group(qk[:, 0, :]),
                                                         scalar=W["scale"][:, 0:1], in1=ps[:, 3:7, 0:S],
                                                         op0=ALU.mult, op1=ALU.mult))
                nc.vector.tensor_tensor(by_position(k_p, g), by_group(qk[:, 1, :]), ps[:, 3:7, S:2 * S],
                                        ALU.mult).then_inc(Z["qk_kept"], 1)
                part.end()

            in_turns(dve, front, body)


def attention(nc, W, xt, du_p, q_p, k_p, first_adapters):
    with ExitStack() as own:
        def sb(name, shape, dt=F32):
            return own.enter_context(nc.sbuf_tensor(name, shape, dt))

        def psum(name, shape):
            return own.enter_context(nc.psum_tensor(name, shape, F32))

        ps_v = psum("ps_v", [P, TB, C])
        ps_s = psum("ps_s", [P, TB, HQ, NB])
        ps_o = psum("ps_o", [P, TB, NB])
        ps_f = psum("ps_f", [P, TB, NB])
        du4 = sb("du4", [P, TB, HQ, NB])
        kx = sb("kx", [P, TB, HQ, NB])
        qx = sb("qx", [P, TB, HQ, NB])
        vb = sb("vb", [P, TB, C])
        sc = sb("sc", [P, TB, HQ, NB])
        pt = sb("pt", [P, TB, HQ, NB])
        top = sb("top4", [P, TB, HQ])
        den = sb("den4", [P, TB, HQ])
        o_t = sb("o_t", [P, TB, NB])
        names = ("du_copied k_spread q_spread v_mm v_done s_mm chain_b chain_first chain_last shifted exped p_turned o_mm o_done f_mm "
                 "x_done").split()
        Z = {n: own.enter_context(nc.semaphore("p3b_" + n)) for n in names}
        block = own.enter_context(nc.Block())
        TURNS = S // TB

        @block.sync
        def _(sp):
            first_adapters(sp)

        @block.gpsimd
        def _(pool):
            def copy_du(t):
                nc.gpsimd.tensor_copy(du4[:, :, :, :], du_p[:, bass.ds(t * TB, TB), :].unsqueeze(2)
                                      .to_broadcast([P, TB, HQ, NB])).then_inc(Z["du_copied"], 1)

            def spread_k(t):
                nc.gpsimd.tensor_tensor(kx[:, :, :, :],
                                        k_p[:, bass.ds(t * TB, TB), :].unsqueeze(2).to_broadcast([P, TB, HQ, NB]),
                                        W["quarter_of"][:, :].unsqueeze(1).unsqueeze(3).to_broadcast([P, TB, HQ, NB]),
                                        ALU.mult).then_inc(Z["k_spread"], 1)

            spread_k(0)
            copy_du(0)
            with pool.Fori(0, TURNS - 1) as i:
                pool.wait_ge(Z["s_mm"], i + 1)
                spread_k(i + 1)
                pool.wait_ge(Z["v_mm"], i + 1)
                copy_du(i + 1)

        @block.tensor
        def _(pe):
            def scores():
                for t in range(TB):
                    last = nc.tensor.matmul(ps_s[:, t, :, :].rearrange("p q b -> p (q b)"),
                                            qx[:, t, :, :].rearrange("p h b -> p (h b)"),
                                            kx[:, t, :, :].rearrange("p q b -> p (q b)"), start=True, stop=True)
                last.then_inc(Z["s_mm"], 1)

            def values():
                for t in range(TB):
                    last = nc.tensor.matmul(ps_v[:, t, :], du4[:, t, :, :].rearrange("p h b -> p (h b)"),
                                            W["w_qkv"][:, 2 * C:3 * C], start=True, stop=True)
                last.then_inc(Z["v_mm"], 1)

            def mix():
                for t in range(TB):
                    for q in range(HQ):
                        last = nc.tensor.matmul(ps_o[32 * q:32 * q + 32, t, :], vb[:, t, 32 * q:32 * q + 32],
                                                pt[:, t, q, :], start=True, stop=True)
                last.then_inc(Z["o_mm"], 1)

            def project():
                nc.tensor.matmul(ps_f[:, :, :].rearrange("p t b -> p (t b)"), W["w_o"][:, :],
                                 o_t[:, :, :].rearrange("p t b -> p (t b)"), start=True, stop=True).then_inc(Z["f_mm"], 1)

            pe.wait_ge(Z["k_spread"], 1)
            pe.wait_ge(Z["q_spread"], 1)
            scores()
            pe.wait_ge(Z["du_copied"], 1)
            values()
            with pe.Fori(0, TURNS - 1) as i:
                pe.wait_ge(Z["k_spread"], i + 2)
                pe.wait_ge(Z["q_spread"], i + 2)
                scores()
                pe.wait_ge(Z["v_done"], i + 1)
                pe.wait_ge(Z["p_turned"], i + 1)
                mix()
                pe.wait_ge(Z["du_copied"], i + 2)
                values()
                pe.wait_ge(Z["o_done"], i + 1)
                project()
            pe.wait_ge(Z["v_done"], TURNS)
            pe.wait_ge(Z["p_turned"], TURNS)
            mix()
            pe.wait_ge(Z["o_done"], TURNS)
            project()

        @block.scalar
        def _(act):
            def exps():
                nc.scalar.activation(sc[:, :, :, :], sc[:, :, :, :], ACT.Exp).then_inc(Z["exped"], 1)

            def finish_o():
                nc.scalar.activation(o_t[:, :, :], ps_o[:, :, :], ACT.Identity, bias=W["v_bias"][:, 0:1],
                                     scale=W["head"][:, 0:1]).then_inc(Z["o_done"], 1)

            act.wait_ge(Z["shifted"], 1)
            exps()
            with act.Fori(0, TURNS - 1) as i:
                act.wait_ge(Z["o_mm"], i + 1)
                finish_o()
                act.wait_ge(Z["shifted"], i + 2)
                exps()
            act.wait_ge(Z["o_mm"], TURNS)
            finish_o()

        @block.vector
        def _(dve):
            def spread(t):
                nc.vector.tensor_tensor(qx[:, :, :, :],
                                        q_p[:, bass.ds(t * TB, TB), :].unsqueeze(2).to_broadcast([P, TB, HQ, NB]),
                                        W["head_of"][:, :].unsqueeze(1).unsqueeze(3).to_broadcast([P, TB, HQ, NB]),
                                        ALU.mult).then_inc(Z["q_spread"], 1)

            def shift(ch):
                s = ps_s[:, :, :, :].rearrange("p t q b -> p (t q) b")
                peak = top[:, :, :].rearrange("p t q -> p (t q)")
                ch.link(nc.vector.tensor_reduce(peak, s, X, ALU.max))
                nc.vector.tensor_tensor(sc[:, :, :, :].rearrange("p t q b -> p (t q) b"), s,
                                        peak.unsqueeze(2).to_broadcast([P, TB * HQ, NB]),
                                        ALU.subtract).then_inc(Z["shifted"], 1)

            def block_v():
                nc.vector.tensor_tensor(vb[:, :, :], ps_v[:, :, :], W["v_block"][:, :].unsqueeze(1)
                                        .to_broadcast([P, TB, C]), ALU.mult).then_inc(Z["v_done"], 1)

            def normalise(ch):
                flat = sc[:, :, :, :].rearrange("p t q b -> p (t q) b")
                ch.link(nc.vector.tensor_reduce(den[:, :, :].rearrange("p t q -> p (t q)"), flat, X, ALU.add))
                ch.link(nc.vector.reciprocal(den[:, :, :], den[:, :, :]))
                ch.link(nc.vector.tensor_tensor(flat, flat, den[:, :, :].rearrange("p t q -> p (t q)").unsqueeze(2)
                                                .to_broadcast([P, HQ * TB, NB]), ALU.mult))
                nc.vector.transpose(pt[:, :, :, :].rearrange("p t q b -> p (t q b)"),
                                    sc[:, :, :, :].rearrange("p t q b -> p (t q b)")).then_inc(Z["p_turned"], 1)

            def add(t):
                x = xt[:, :].rearrange("p (b t) -> p b t", b=NB)[:, :, bass.ds(t * TB, TB)]
                nc.vector.scalar_tensor_tensor(out=x, in0=ps_f[:, :, :].rearrange("p t b -> p b t"),
                                               scalar=W["b_o"][:, 0:1], in1=x, op0=ALU.add,
                                               op1=ALU.add).then_inc(Z["x_done"], 1)

            first = Chain(dve, Z["chain_first"], 0, 1)
            spread(0)
            dve.wait_ge(Z["s_mm"], 1)
            shift(first)
            dve.wait_ge(Z["v_mm"], 1)
            block_v()
            first.end()
            dve.wait_ge(Z["s_mm"], 1)
            spread(1)

            def turn(i, more):
                ch = Chain(dve, Z["chain_b"], i, 4)
                dve.wait_ge(Z["exped"], i + 1)
                normalise(ch)
                dve.wait_ge(Z["s_mm"], i + 2)
                shift(ch)
                if more:
                    spread(i + 2)
                dve.wait_ge(Z["v_mm"], i + 2)
                block_v()
                dve.wait_ge(Z["f_mm"], i + 1)
                add(i)
                ch.end()

            with dve.Fori(0, TURNS - 2) as i:
                turn(i, True)
            turn(TURNS - 2, False)
            last = Chain(dve, Z["chain_last"], 0, 3)
            dve.wait_ge(Z["exped"], TURNS)
            normalise(last)
            dve.wait_ge(Z["f_mm"], TURNS)
            add(TURNS - 1)
            last.end()


def ffn1_loads(D, W):
    return [
        (W["ids"][:, :], D["itok_B_0_8"].to_broadcast([NL, NB])), (W["lang"][:, :], D["c_lang"]),
        (W["ids_row"][:, :], D["itok_B_0_8"]),
        (W["b1"][:, :], D["L1_cond2_b1"]), (W["b2"][:, :], D["L1_cond2_b2"]),
        (W["gamma"][:, :], D["L1_cond2_gamma"]), (W["beta"][:, :], D["L1_cond2_beta"]),
        (W["router"][:, :], D["L1_ffn_router_w"]), (W["router_b"][:, :], D["L1_ffn_router_b"].to_broadcast([P, NE])),
        (W["w1"][:, :, :], D["w1_all"]), (W["c1"][:, :, :], D["b1_all"]),
        (W["w2"][:, :, :, :], D["w2_all"]), (W["sb2"][:, :], D["L1_ffn_sb2"]), (W["rb2"][:, :], D["L1_ffn_rb2"]),
        (W["rank"][:, :], D["c_rank"].to_broadcast([P, NE])), (W["pick8"][:, :], D["c_pick"]),
    ]


def setup_ffn1(nc, W, loaded, loads):
    with ExitStack() as own:
        def tmp(name, shape, dt=F32):
            return own.enter_context(nc.sbuf_tensor(name, shape, dt))

        def sem(name):
            return own.enter_context(nc.semaphore(name))

        idf = tmp("idf4", [NL, NB])
        ps = own.enter_context(nc.psum_tensor("ps_s4", [P, 4, N], F32))
        chain_v = sem("s4_chain_v")
        hot = sem("s4_hot")
        picked = sem("s4_picked")
        block = own.enter_context(nc.Block())

        @block.gpsimd
        def _(pool):
            nc.gpsimd.memset(W["mw96"][:, :, :, :], 0.0)
            nc.gpsimd.memset(W["neg_half"][:, :], -0.5)

        @block.tensor
        def _(pe):
            pe.wait_ge(hot, 1)
            for k, rows in enumerate((W["gamma"], W["beta"], W["b2"])):
                nc.tensor.matmul(ps[:, k, 0:NB], rows[:, :], W["lang_hot"][:, :], start=True, stop=True)
            nc.tensor.matmul(ps[0:32, 3, 0:NB], W["b1"][:, :], W["lang_hot"][:, :], start=True, stop=True).then_inc(picked, 1)

        @block.vector
        def _(dve):
            ch = Chain(dve, chain_v, 0, 1)
            dve.wait_ge(loaded, 16 * len(loads))
            ch.link(nc.vector.tensor_copy(idf[:, :], W["ids"][:, :]))
            nc.vector.tensor_scalar(W["lang_hot"][:, :], idf[:, :], W["lang"][:, 0:1], None, ALU.is_equal).then_inc(hot, 1)
            dve.wait_ge(picked, 1)
            nc.vector.tensor_copy(W["gamma_b"][:, :], ps[:, 0, 0:NB])
            nc.vector.tensor_copy(W["beta_b"][:, :], ps[:, 1, 0:NB])
            nc.vector.tensor_copy(W["b2_b"][:, :], ps[:, 2, 0:NB])
            nc.vector.tensor_copy(W["b1_b"][:, :], ps[0:32, 3, 0:NB])
            ch.end()


def load_adapters(sp, D, W, adapters, g):
    for b in range(GB):
        lang = sp.value_load(W["ids_row"][0:1, bass.ds(g * GB + b, 1)], min_val=0, max_val=NL - 1)
        sp.dma_start(W["w1g"][:, b, :], D["L1_cond2_W1"][:, bass.ds(lang * 32, 32)]).then_inc(adapters, 16)
        sp.dma_start(W["w2g"][:, b, :], D["L1_cond2_W2"][:, bass.ds(lang * C, C)]).then_inc(adapters, 16)


def adapter_and_experts(nc, D, W, adapters, xt, out):
    with ExitStack() as own:
        def sb(name, shape, dt=F32):
            return own.enter_context(nc.sbuf_tensor(name, shape, dt))

        ps = own.enter_context(nc.psum_tensor("ps4", [P, 8, N], F32))
        had = sb("had", [32, GB, S])
        xa = sb("xa", [P, GB, S])
        mean = sb("mean4", [P, GB])
        var = sb("var4", [P, GB])
        rstd = sb("rstd4", [P, GB])
        xc = sb("xc4", [P, GB, C])
        sq = sb("sq4", [P, GB, C])
        xn = sb("xn4", [P, GB, C])
        yt = sb("yt4", [P, 2, N])
        lg = sb("lg4", [P, GB, NE])
        ex = sb("ex4", [P, GB, NE])
        hot = sb("hot4", [P, GB, NE])
        hot2 = sb("hot42", [P, GB, NE])
        top = sb("top42", [P, GB])
        den = sb("den42", [P, GB])
        m_parts = sb("m_parts4", [96, N], BF16)
        m_mid = sb("m_mid4", [96, N], BF16)
        m_rest = sb("m_rest4", [96, N])
        mw_t = sb("mw_t4", [NE, N])
        hh = sb("hh", [P, 4, N])
        hw = sb("hw", [P, 4, N])
        names = ("ad1_mm ad1_done ad2_mm xa_done xa_mm centred squared var_done rstd_done xn_done "
                 "xn_mm yt_done router_mm shifted exped mw_done mw_copied mw_mm m_split mask_mm hidden_mm hidden_done "
                 "weighted taken bias_mm x_done stored chain_f").split()
        Z = {n: own.enter_context(nc.semaphore("p4_" + n)) for n in names}
        block = own.enter_context(nc.Block())
        TILES = 2 * (NE + 1)
        LEAD = 3

        @block.sync
        def _(sp):
            def store(g):
                sp.wait_ge(Z["x_done"], g + 1)
                sp.dma_start(out[:, bass.ds(g * N, N)], xt[:, bass.ds(g * N, N)]).then_inc(Z["stored"], 16)

            sp.wait_ge(Z["ad2_mm"], 1)
            load_adapters(sp, D, W, adapters, 1)
            with sp.Fori(0, NG - 2) as g:
                sp.wait_ge(Z["ad2_mm"], g + 2)
                load_adapters(sp, D, W, adapters, g + 2)
                store(g)
            store(NG - 2)
            store(NG - 1)
            sp.wait_ge(Z["stored"], 16 * NG)

        @block.gpsimd
        def _(pool):
            with pool.Fori(0, NG) as g:
                pool.wait_ge(Z["var_done"], g + 1)
                nc.gpsimd.tensor_tensor(rstd[:, :], var[:, :], W["neg_half"][:, :], ALU.pow).then_inc(Z["rstd_done"], 1)

        @block.tensor
        def _(pe):
            def adapter_in(g):
                pe.wait_ge(adapters, 32 * GB * g + 32 * GB)
                for b in range(GB):
                    last = nc.tensor.matmul(ps[0:32, 0, b * S:(b + 1) * S], W["w1g"][:, b, :],
                                            xt[:, bass.ds(g * N + b * S, S)], start=True, stop=True)
                last.then_inc(Z["ad1_mm"], 1)

            def adapter_out(g):
                pe.wait_ge(Z["ad1_done"], g + 1)
                for b in range(GB):
                    last = nc.tensor.matmul(ps[:, 1, b * S:(b + 1) * S], W["w2g"][:, b, :], had[:, b, :],
                                            start=True, stop=True)
                last.then_inc(Z["ad2_mm"], 1)

            def to_tokens(g):
                pe.wait_ge(Z["xa_done"], g + 1)
                for b in range(GB):
                    last = nc.tensor.transpose(ps[:, 0, b * C:(b + 1) * C], xa[:, b, :], W["ident"][:, :])
                last.then_inc(Z["xa_mm"], 1)

            def to_channels(g):
                pe.wait_ge(Z["xn_done"], g + 1)
                for b in range(GB):
                    last = nc.tensor.transpose(ps[:, 1, b * S:(b + 1) * S], xn[:, b, :], W["ident"][:, :])
                last.then_inc(Z["xn_mm"], 1)

            def router(g, at):
                pe.wait_ge(Z["yt_done"], g + 1)
                for b in range(GB):
                    last = nc.tensor.matmul(ps[:, 0, b * NE:(b + 1) * NE], yt[:, at, b * S:(b + 1) * S],
                                            W["router"][:, :], start=True, stop=True)
                last.then_inc(Z["router_mm"], 1)

            def weights_in(g):
                pe.wait_ge(Z["mw_copied"], g + 1)
                for b in range(GB):
                    last = nc.tensor.transpose(ps[0:96, 1, b * S:(b + 1) * S],
                                               W["mw96"][:, b, :, :].rearrange("p k e -> p (k e)"), W["ident"][:, :])
                last.then_inc(Z["mw_mm"], 1)

            def front(g, at):
                adapter_in(g)
                adapter_out(g)
                to_tokens(g)
                to_channels(g)
                router(g, at)
                weights_in(g)

            def body(g, at, ahead, _):
                def hidden(k):
                    if k >= 2:
                        pe.wait_ge(Z["hidden_done"], g * TILES + k - 1)
                    nc.tensor.matmul(ps[:, 2 + k % 2, :], W["w1"][:, k, :], yt[:, at, :],
                                     start=True, stop=True).then_inc(Z["hidden_mm"], 1)

                def mask(e):
                    if e >= 2:
                        pe.wait_ge(Z["weighted"], g * 2 * NE + 2 * (e - 1))
                    nc.tensor.matmul(ps[:, 4 + e % 2, :], W["pick8"][:, e:e + 1].to_broadcast([96, P]), m_parts[:, :],
                                     start=True, stop=True).then_inc(Z["mask_mm"], 1)

                def outwards(k):
                    if k < 2:
                        pe.wait_ge(Z["hidden_done"], g * TILES + k + 1)
                        src = hh[:, k, :]
                    else:
                        pe.wait_ge(Z["weighted"], g * 2 * NE + k - 1)
                        src = hw[:, k % 4, :]
                    ins = nc.tensor.matmul(ps[:, 6 + at, :], W["w2"][:, k // 2, k % 2, :], src,
                                           start=(k == 0), stop=(k == TILES - 1))
                    if k >= 2:
                        ins.then_inc(Z["taken"], 1)

                hidden(0)
                hidden(1)
                hidden(2)
                outwards(0)
                hidden(3)
                outwards(1)
                hidden(4)
                pe.wait_ge(Z["m_split"], g + 1)
                mask(0)
                if ahead is not None:
                    adapter_in(ahead)
                for k in range(2, TILES):
                    if k % 2 == 0 and k // 2 < NE:
                        mask(k // 2)
                    if k + LEAD < TILES:
                        hidden(k + LEAD)
                    if k == TILES - 1:
                        nc.tensor.matmul(ps[:, 6 + at, :], W["rb2"][:, :], mw_t[:, :],
                                         start=False, stop=False).then_inc(Z["bias_mm"], 1)
                        if ahead is not None:
                            weights_in(ahead)
                    outwards(k)
                    if ahead is not None:
                        if k == 3:
                            adapter_out(ahead)
                        if k == 5:
                            to_tokens(ahead)
                        if k == 9:
                            to_channels(ahead)
                        if k == 11:
                            router(ahead, 1 - at)

            in_pairs(pe, front, body)

        @block.scalar
        def _(act):
            def square(g):
                act.wait_ge(Z["centred"], g + 1)
                nc.scalar.activation(sq[:, :, :], xc[:, :, :], ACT.Square).then_inc(Z["squared"], 1)

            def exps(g):
                act.wait_ge(Z["shifted"], g + 1)
                nc.scalar.activation(ex[:, :, :], ex[:, :, :], ACT.Exp).then_inc(Z["exped"], 1)

            def copy_masks(g):
                act.wait_ge(Z["mw_done"], g + 1)
                nc.scalar.copy(W["mw96"][:, :, :, 0:NE],
                               hot[:, :, :].unsqueeze(2).to_broadcast([P, GB, 3, NE])).then_inc(Z["mw_copied"], 1)

            def front(g, at):
                square(g)
                exps(g)
                copy_masks(g)

            def body(g, at, ahead, _):
                for k in range(TILES):
                    act.wait_ge(Z["hidden_mm"], g * TILES + k + 1)
                    if k >= 6:
                        act.wait_ge(Z["weighted"], g * 2 * NE + k - 5)
                    nc.scalar.activation(hh[:, k % 4, :], ps[:, 2 + k % 2, :], ACT.Gelu,
                                         bias=W["c1"][:, k // 2, k % 2:k % 2 + 1]).then_inc(Z["hidden_done"], 1)
                    if ahead is not None:
                        if k == 9:
                            square(ahead)
                        if k == 16:
                            exps(ahead)
                if ahead is not None:
                    copy_masks(ahead)

            in_pairs(act, front, body)

        @block.vector
        def _(dve):
            LINKS = (1, 1, 2, 1, 1, 2, 4, 6, 3, 4)
            OFF = [sum(LINKS[:i]) for i in range(len(LINKS))]

            def chain(g, step):
                c = Chain(dve, Z["chain_f"], g, sum(LINKS))
                c.at = OFF[step]
                return c

            def vec(v, g):
                return v[:, bass.ds(g * GB, GB)].unsqueeze(2)

            rank = W["rank"][:, :].unsqueeze(1).to_broadcast([P, GB, NE])
            top_b = top[:, :].unsqueeze(2).to_broadcast([P, GB, NE])

            def first_of_top(ch, to):
                ch.link(nc.vector.tensor_tensor(to[:, :, :], lg[:, :, :], top_b, ALU.is_equal))
                ch.link(nc.vector.tensor_tensor(to[:, :, :], to[:, :, :], rank, ALU.mult))
                ch.link(nc.vector.tensor_reduce(top[:, :], to[:, :, :], X, ALU.max))
                ch.link(nc.vector.tensor_tensor(to[:, :, :], to[:, :, :], top_b, ALU.is_equal))

            def adapter_hidden(g):
                ch = chain(g, 0)
                dve.wait_ge(Z["ad1_mm"], g + 1)
                ch.link(nc.vector.tensor_tensor(had[:, :, :], by_group(ps[0:32, 0, :]),
                                                vec(W["b1_b"], g).to_broadcast([32, GB, S]), ALU.add))
                nc.vector.tensor_scalar(had[:, :, :], had[:, :, :], 0.0, None, ALU.max).then_inc(Z["ad1_done"], 1)

            def adapted(g):
                ch = chain(g, 1)
                dve.wait_ge(Z["ad2_mm"], g + 1)
                ch.link(nc.vector.tensor_tensor(xa[:, :, :].rearrange("p b t -> p (b t)"), ps[:, 1, :],
                                                xt[:, bass.ds(g * N, N)], ALU.add))
                nc.vector.tensor_tensor(xa[:, :, :], xa[:, :, :], vec(W["b2_b"], g).to_broadcast([P, GB, S]),
                                        ALU.add).then_inc(Z["xa_done"], 1)

            def centre(g):
                ch = chain(g, 2)
                dve.wait_ge(Z["xa_mm"], g + 1)
                o = ps[:, 0, :].rearrange("p (b c) -> p b c", b=GB)
                ch.link(nc.vector.tensor_reduce(mean[:, :], o, X, ALU.add))
                ch.link(nc.vector.tensor_scalar(mean[:, :], mean[:, :], 1.0 / C, None, ALU.mult))
                nc.vector.tensor_tensor(xc[:, :, :], o, mean[:, :].unsqueeze(2).to_broadcast([P, GB, C]),
                                        ALU.subtract).then_inc(Z["centred"], 1)

            def variance(g):
                ch = chain(g, 3)
                dve.wait_ge(Z["squared"], g + 1)
                ch.link(nc.vector.tensor_reduce(var[:, :], sq[:, :, :], X, ALU.add))
                nc.vector.tensor_scalar(var[:, :], var[:, :], 1.0 / C, LN_EPS, ALU.mult, ALU.add).then_inc(Z["var_done"], 1)

            def normalise(g):
                dve.wait_ge(Z["rstd_done"], g + 1)
                nc.vector.tensor_tensor(xn[:, :, :], xc[:, :, :], rstd[:, :].unsqueeze(2).to_broadcast([P, GB, C]),
                                        ALU.mult).then_inc(Z["xn_done"], 1)

            def to_experts(g, at):
                ch = chain(g, 4)
                dve.wait_ge(Z["xn_mm"], g + 1)
                y = by_group(yt[:, at, :])
                ch.link(nc.vector.tensor_tensor(y, by_group(ps[:, 1, :]), vec(W["gamma_b"], g).to_broadcast([P, GB, S]),
                                                ALU.mult))
                nc.vector.tensor_tensor(y, y, vec(W["beta_b"], g).to_broadcast([P, GB, S]), ALU.add).then_inc(Z["yt_done"], 1)

            def logits(g):
                ch = chain(g, 5)
                dve.wait_ge(Z["router_mm"], g + 1)
                ch.link(nc.vector.tensor_tensor(lg[:, :, :], ps[:, 0, 0:GB * NE].rearrange("p (b e) -> p b e", b=GB),
                                                W["router_b"][:, :].unsqueeze(1).to_broadcast([P, GB, NE]), ALU.add))
                ch.link(nc.vector.tensor_reduce(top[:, :], lg[:, :, :], X, ALU.max))
                nc.vector.tensor_tensor(ex[:, :, :], lg[:, :, :], top_b, ALU.subtract).then_inc(Z["shifted"], 1)

            def best(g):
                first_of_top(chain(g, 6), hot)

            def second_best(g):
                ch = chain(g, 7)
                ch.link(nc.vector.scalar_tensor_tensor(out=lg[:, :, :], in0=hot[:, :, :], scalar=-1e30, in1=lg[:, :, :],
                                                       op0=ALU.mult, op1=ALU.add))
                ch.link(nc.vector.tensor_reduce(top[:, :], lg[:, :, :], X, ALU.max))
                first_of_top(ch, hot2)

            def weights(g):
                ch = chain(g, 8)
                ch.link(nc.vector.tensor_tensor(hot[:, :, :], hot[:, :, :], hot2[:, :, :], ALU.add))
                dve.wait_ge(Z["exped"], g + 1)
                nc.vector.tensor_tensor(hot[:, :, :], hot[:, :, :], ex[:, :, :], ALU.mult)
                ch.link(nc.vector.tensor_reduce(den[:, :], ex[:, :, :], X, ALU.add))
                ch.link(nc.vector.reciprocal(den[:, :], den[:, :]))
                nc.vector.tensor_tensor(hot[:, :, :], hot[:, :, :], den[:, :].unsqueeze(2).to_broadcast([P, GB, NE]),
                                        ALU.mult).then_inc(Z["mw_done"], 1)

            def split_weights(g):
                dve.wait_ge(Z["mw_mm"], g + 1)
                split3(nc, chain(g, 9), m_parts, m_mid, m_rest, ps[0:96, 1, :]).then_inc(Z["m_split"], 1)
                nc.vector.tensor_copy(mw_t[:, :], ps[0:NE, 1, :])

            def front(g, at):
                adapter_hidden(g)
                adapted(g)
                centre(g)
                variance(g)
                normalise(g)
                to_experts(g, at)
                logits(g)
                best(g)
                second_best(g)
                weights(g)
                split_weights(g)

            def body(g, at, ahead, _):
                for k in range(2, TILES):
                    if k % 2 == 0:
                        dve.wait_ge(Z["mask_mm"], g * NE + k // 2)
                    dve.wait_ge(Z["hidden_done"], g * TILES + k + 1)
                    if k >= 6:
                        dve.wait_ge(Z["taken"], g * 2 * NE + k - 5)
                    nc.vector.tensor_tensor(hw[:, k % 4, :], hh[:, k % 4, :], ps[:, 4 + (k // 2 - 1) % 2, :],
                                            ALU.mult).then_inc(Z["weighted"], 1)
                    if ahead is not None:
                        if k == 2:
                            adapter_hidden(ahead)
                        if k == 4:
                            adapted(ahead)
                        if k == 6:
                            centre(ahead)
                        if k == 7:
                            variance(ahead)
                        if k == 8:
                            normalise(ahead)
                        if k == 10:
                            to_experts(ahead, 1 - at)
                        if k == 12:
                            logits(ahead)
                        if k == 13:
                            best(ahead)
                        if k == 14:
                            second_best(ahead)
                        if k == TILES - 2:
                            weights(ahead)
                if ahead is not None:
                    dve.wait_ge(Z["bias_mm"], g + 1)
                    split_weights(ahead)
                dve.wait_ge(Z["taken"], g * 2 * NE + 2 * NE)
                x = xt[:, bass.ds(g * N, N)]
                nc.vector.scalar_tensor_tensor(out=x, in0=ps[:, 6 + at, :], scalar=W["sb2"][:, 0:1],
                                               in1=x, op0=ALU.add, op1=ALU.add).then_inc(Z["x_done"], 1)

            in_pairs(dve, front, body)


def build(nc, D, out):
    with ExitStack() as ctx:
        def w(name, shape, dt=F32):
            return ctx.enter_context(nc.sbuf_tensor(name, shape, dt))

        xt = w("xt", [P, NB * S])
        ident = w("ident", [P, P])
        loaded = [ctx.enter_context(nc.semaphore(name)) for name in ("ffn0_loaded", "attention_loaded", "ffn1_loaded")]
        W_ffn0 = {
            "ident": ident, "wg_x": w("wg_x", [P, C]),
            "wg_ctx": w("wg_ctx", [P, C]), "bg": w("bg", [P, 1]), "wn1": w("wn1", [P, 32]),
            "bn1": w("bn1", [32, 1]), "wn2": w("wn2", [32, ND]), "bn2": w("bn2", [ND, 1]),
            "w_soma": w("w_soma", [P, C]), "b_soma": w("b_soma", [P, 1]), "w_temp": w("w_temp", [P, C]),
            "b_temp": w("b_temp", [P, 1]), "w_out": w("w_out", [P, C]), "gamma": w("gamma", [P, 1]),
            "beta": w("beta", [P, 1]), "router": w("router", [P, NE]), "router_b": w("router_b", [P, NE]),
            "expert_w": w("expert_w", [P, NE, C]), "expert_b": w("expert_b", [NE, C]),
            "rank": w("rank", [P, NE]), "pick8": w("pick8", [96, 32], BF16),
            "from_start": w("from_start", [P, 4 * LAGS]), "ctx_decay": w("ctx_decay", [P, N]),
            "upto_end": w("upto_end", [P, CHUNKS, ND]), "bw": w("bw", [P, C]),
            "bw_lag": w("bw_lag", [ND, LAGS, C]),
            "mw96": w("mw96", [P, GB, 3, 32]), "neg_half": w("neg_half", [P, GB]),
            "taus": w("taus", [P, ND + 2]),
            "blend_t": w("blend_t", [P, ND]),
            "pow_at": w("pow_at", [P, LAGS]),
            "upto_at": w("upto_at", [P, CHUNKS]),
            "upto_on": w("upto_on", [P, CHUNKS]),
            "from_at": w("from_at", [P, 4 * LAGS]),
            "from_on": w("from_on", [P, 4 * LAGS]),
            "ctx_on": w("ctx_on", [P, N]),
        }
        ffn0 = (loaded[0], ffn0_loads(D, W_ffn0))
        with ExitStack() as first:
            def w(name, shape, dt=F32):
                return first.enter_context(nc.sbuf_tensor(name, shape, dt))

            W = {
                "ident": ident, "lora_a": w("lora_a", [P, P]), "w_z": w("w_z", [P, DI]), "w_conv": w("w_conv", [P, 4, DI]),
                "w_bc": w("w_bc", [P, NT, 96]), "w_delta": w("w_delta", [P, NT, DI]),
                "conv_b": w("conv_b", [P, NT]),
                "dt_b": w("dt_b", [P, NT]), "a": w("a", [P, NT, NS]), "d_skip": w("d_skip", [P, NT]),
                "out_w": w("out_w", [P, NT, C]), "pick": w("pick", [96, 32], BF16),
                "gates": w("gates", [P, NB, NE]), "decay": w("decay", [P, RING, 2, GB, S]),
            }
            setup_scan(nc, first, D, W, xt)
            selective_scan(nc, W, xt, ffn0)
        with ExitStack() as rest:
            def w(name, shape, dt=F32):
                return rest.enter_context(nc.sbuf_tensor(name, shape, dt))

            W_attention = {
                "lap": w("lap", [P, C]), "z": w("z", [P, 3, NB]), "w_qkv": w("w_qkv", [P, 3 * C]),
                "b_qkv": w("b_qkv", [P, 3]), "scale": w("scale", [P, 1]), "head": w("head", [P, 1]),
                "v_bias": w("v_bias", [P, 1]), "w_o": w("w_o", [P, C]), "b_o": w("b_o", [P, 1]),
                "to_heads": w("to_heads", [P, 2, 32]), "from_heads": w("from_heads", [P, 2, C]), "head_of": w("head_of", [P, HQ]),
                "quarter_of": w("quarter_of", [P, HQ]), "v_block": w("v_block", [P, C]),
            }
            W_ffn1 = {
                "ident": ident, "b2_b": w("b2_b", [P, NB]), "ids_row": w("ids_row", [1, NB], I32),
                "router": w("router4", [P, NE]), "router_b": w("router_b4", [P, NE]),
                "w1": w("w1", [P, 2 * (NE + 1), P]), "c1": w("c1", [P, NE + 1, 2]),
                "w2": w("w2", [P, NE + 1, 2, C]), "sb2": w("sb2", [P, 1]), "rb2": w("rb2", [NE, C]),
                "rank": w("rank4", [P, NE]), "pick8": w("pick84", [96, 32], BF16), "mw96": w("mw964", [P, GB, 3, 32]),
                "neg_half": w("neg_half4", [P, GB]), "lang_hot": w("lang_hot", [NL, NB]),
                "gamma_b": w("gamma_b", [P, NB]), "beta_b": w("beta_b", [P, NB]), "b1_b": w("b1_b", [32, NB]),
                "ids": w("ids4", [NL, NB], I32),
                "lang": w("lang", [NL, 1]),
                "b1": w("b1_rows", [NL, 32]),
                "gamma": w("gamma4", [NL, C]),
                "beta": w("beta4", [NL, C]),
                "b2": w("b2_rows", [NL, C]),
                "w1g": w("w1g", [P, GB, 32]), "w2g": w("w2g", [32, GB, C]),
            }
            adapters = rest.enter_context(nc.semaphore("adapters"))

            def first_adapters(sp):
                sp.wait_ge(loaded[2], 16 * len(ffn1[1]))
                load_adapters(sp, D, W_ffn1, adapters, 0)

            attn = (loaded[1], attention_loads(D, W_attention))
            ffn1 = (loaded[2], ffn1_loads(D, W_ffn1))
            setup_ffn0(nc, W_ffn0, *ffn0)
            traces_and_experts(nc, W_ffn0, xt, (attn, ffn1))
            with ExitStack() as kept:
                du_p, q_p, k_p = (kept.enter_context(nc.sbuf_tensor(name, [P, S, NB], F32))
                                  for name in ("du_p", "q_p", "k_p"))
                setup_attention(nc, W_attention, *attn)
                diffusion_and_qk(nc, W_attention, xt, du_p, q_p, k_p)
                attention(nc, W_attention, xt, du_p, q_p, k_p, first_adapters)
            setup_ffn1(nc, W_ffn1, *ffn1)
            adapter_and_experts(nc, D, W_ffn1, adapters, xt, out)


def lay_out(a):
    def tiles(w, rows):
        return w.reshape(rows // P, P, -1).transpose(1, 0, 2)

    xp = a["L0_attn_x_proj_w"]
    bc = xp[DI:].T
    L = {
        "x": a["x"].transpose(2, 0, 1).reshape(C, NB * S),
        "L0_cond_lora_B": a["L0_cond_lora_B"].transpose(1, 0, 2).reshape(C, NE * R),
        "L0_cond_lora_A": a["L0_cond_lora_A"].transpose(2, 0, 1).reshape(C, NE * R),
        "L0_attn_in_proj_w": a["L0_attn_in_proj_w"].T,
        "x_proj_delta": tiles(xp[:DI], DI),
        "x_proj_bc": tiles(np.concatenate([bc, bc, bc], axis=1), DI),
        "L0_attn_dt_proj_w": tiles(a["L0_attn_dt_proj_w"].T, DI),
        "L0_cond_gate_W1": a["L0_cond_gate_W1"],
        "L0_cond_gate_b1": np.tile(a["L0_cond_gate_b1"], 4).reshape(-1, 1),
        "L0_cond_gate_W2": np.tile(a["L0_cond_gate_W2"], (4, 1)),
        "L0_cond_gate_b2": a["L0_cond_gate_b2"].reshape(1, -1),
        "itok_B_4_6": a["itok_B_4_6"].reshape(1, -1),
        "L0_attn_conv_w": a["L0_attn_conv_w"].reshape(DI, 4).T.reshape(1, 4 * DI),
        "L0_attn_conv_b": a["L0_attn_conv_b"].reshape(NT, P).T,
        "L0_attn_dt_proj_b": a["L0_attn_dt_proj_b"].reshape(NT, P).T,
        "L0_attn_D_param": a["L0_attn_D_param"].reshape(NT, P).T,
        "L0_attn_A_log": tiles(a["L0_attn_A_log"], DI),
        "L0_attn_out_proj_w": tiles(a["L0_attn_out_proj_w"].T, DI),
        "condB_tauraws": a["condB_tauraws"].reshape(1, ND),
        "tau_column": np.tile(a["condB_tauraws"], P // ND).reshape(P, 1),
        "L0_cond2_tau_ctx": a["L0_cond2_tau_ctx"].reshape(1, 1),
        "cond_1024": a["cond_1024"].T,
        "wg_x": a["L0_cond2_Wg"][:, :C].T, "wg_ctx": a["L0_cond2_Wg"][:, C:].T,
        "L0_cond2_bg": a["L0_cond2_bg"].reshape(C, 1),
        "L0_cond2_Wn1": a["L0_cond2_Wn1"].T, "L0_cond2_bn1": a["L0_cond2_bn1"].reshape(-1, 1),
        "cond_256": a["cond_256"].T, "condB_bn2": a["condB_bn2"].reshape(ND, 1),
        "L0_cond2_Wsoma": a["L0_cond2_Wsoma"].T, "L0_cond2_bsoma": a["L0_cond2_bsoma"].reshape(C, 1),
        "L0_cond2_Wtemp": a["L0_cond2_Wtemp"].T, "L0_cond2_btemp": a["L0_cond2_btemp"].reshape(C, 1),
        "L0_cond2_Wout": a["L0_cond2_Wout"].T, "L0_cond2_gamma": a["L0_cond2_gamma"].reshape(C, 1),
        "L0_cond2_beta": a["L0_cond2_beta"].reshape(C, 1),
        "L0_ffn_router_w": a["L0_ffn_router_w"].T, "L0_ffn_router_b": a["L0_ffn_router_b"].reshape(1, NE),
        "L0_ffn_expert_w": a["L0_ffn_expert_w"].transpose(2, 0, 1), "L0_ffn_expert_b": a["L0_ffn_expert_b"],
        "condB_zX": a["condB_zX"].reshape(1, NB), "condB_zY": a["condB_zY"].reshape(1, NB),
        "condB_zR": a["condB_zR"].reshape(1, NB),
        "L1_attn_in_proj_weight": a["L1_attn_in_proj_weight"].T,
        "L1_attn_in_proj_bias": a["L1_attn_in_proj_bias"].reshape(3, C).T,
        "L1_attn_logit_scale": np.repeat(a["L1_attn_logit_scale"].reshape(-1), C // 16).reshape(C, 1),
        "L1_attn_head_scale": np.repeat(a["L1_attn_head_scale"].reshape(-1), C // 16).reshape(C, 1),
        "L1_attn_out_w": a["L1_attn_out_w"].T, "L1_attn_out_b": a["L1_attn_out_b"].reshape(C, 1),
        "itok_B_0_8": a["itok_B_0_8"].reshape(1, NB),
        "L1_cond2_W1": a["L1_cond2_W1"].transpose(1, 0, 2).reshape(C, -1),
        "L1_cond2_W2": a["L1_cond2_W2"].transpose(1, 0, 2).reshape(32, -1),
        "L1_cond2_b1": a["L1_cond2_b1"], "L1_cond2_b2": a["L1_cond2_b2"],
        "L1_cond2_gamma": a["L1_cond2_gamma"], "L1_cond2_beta": a["L1_cond2_beta"],
        "L1_ffn_router_w": a["L1_ffn_router_w"], "L1_ffn_router_b": a["L1_ffn_router_b"].reshape(1, NE),
        "w1_all": np.concatenate([a["L1_ffn_sw1"][None], a["L1_ffn_rw1"]]).reshape(NE + 1, C, 2, P)
        .transpose(1, 0, 2, 3).reshape(C, 2 * (NE + 1), P),
        "b1_all": np.concatenate([a["L1_ffn_sb1"][None], a["L1_ffn_rb1"]]).reshape(NE + 1, 2, P).transpose(2, 0, 1),
        "w2_all": np.concatenate([a["L1_ffn_sw2"][None], a["L1_ffn_rw2"]]).reshape(NE + 1, 2, P, C).transpose(2, 0, 1, 3),
        "L1_ffn_sb2": a["L1_ffn_sb2"].reshape(C, 1), "L1_ffn_rb2": a["L1_ffn_rb2"],
        "c_expert": np.arange(NE, dtype=np.float32).reshape(1, -1),
        "c_ident": np.eye(P, dtype=np.float32),
        "c_pick": np.tile(np.eye(32, dtype=np.float32), (3, 1)),
    }
    s, t, k = np.arange(S), np.arange(S), np.arange(CHUNKS)
    before = LAGS * k[None, :] - s[:, None]
    chunk = np.arange(P)[:, None] // ND
    lag = np.arange(LAGS)
    L.update({
        "c_lag": lag.reshape(1, -1), "c_rank": np.arange(NE, 0, -1).reshape(1, -1),
        "c_upto_at": np.maximum(before - 1, 0), "c_upto_on": before > 0,
        "c_from_at": np.clip(t[None, :4 * LAGS] - LAGS * chunk + 1, 0, LAGS),
        "c_from_on": t[None, :4 * LAGS] // LAGS == chunk,
        "c_ctx_on": (np.arange(N) % S != 0).reshape(1, -1),
    })
    c = np.arange(C)
    lap = -2.0 * np.eye(C)
    for to in range(C):
        lap[abs(to - 1), to] += 1
        lap[C - 1 - abs(C - 2 - to), to] += 1
    L.update({
        "c_lap": lap,
        "c_to_heads": c[:, None, None] // 8 + 16 * np.arange(2)[None, :, None] == np.arange(32)[None, None, :],
        "c_from_heads": c[None, None, :] // 8 + 16 * np.arange(2)[None, :, None] == (c % 32)[:, None, None],
        "c_head_of": c[:, None] // 8 % HQ == np.arange(HQ)[None, :],
        "c_quarter": c[:, None] // 32 == np.arange(4)[None, :],
        "c_quarter_of": c[:, None] // 32 == np.arange(HQ)[None, :],
        "c_v_block": np.arange(P)[:, None] // NB == (c // 8 % HQ)[None, :],
        "c_lang": np.arange(NL).reshape(NL, 1),
    })
    for name in L:
        if name.startswith("c_"):
            L[name] = L[name].astype(np.float32)
    return L


_BF16_CONSTS = ("c_pick",)


def kernel(**inputs):
    import ml_dtypes
    import concourse.bacc as _bacc
    from concourse.bass_utils import run_bass_kernel_spmd as _run

    nc = _bacc.Bacc("TRN2", target_bir_lowering=False, num_devices=1)
    arrays, D = {}, {}
    for name, a in lay_out({k: np.asarray(v) for k, v in inputs.items()}).items():
        if name in _BF16_CONSTS:
            a = a.astype(ml_dtypes.bfloat16)
        a = np.ascontiguousarray(a)
        arrays[f"in_{name}"] = a
        D[name] = nc.dram_tensor(f"in_{name}", a.shape, mybir.dt.from_np(a.dtype), kind="ExternalInput").ap()
    out = nc.dram_tensor("out_0", (C, NB * S), F32, kind="ExternalOutput").ap()
    build(nc, D, out)
    r = _run(nc, [arrays], core_ids=[0])
    got = np.asarray(r.results[0]["out_0"])
    return np.ascontiguousarray(got.reshape(C, NB, S).transpose(1, 2, 0))
```
